# Optimizing a Trainium2 kernel written in Bass

```python
import numpy as np
import jax
import jax.numpy as jnp

def _softmax(x, axis=-1):
    return jax.nn.softmax(x, axis=axis)

def _gelu(x):
    return jax.nn.gelu(x, approximate=True)

def _silu(x):
    return jax.nn.silu(x)

def _sigmoid(x):
    return jax.nn.sigmoid(x)

def _layernorm(x, axis=-1, eps=1e-05):
    m = jnp.mean(x, axis=axis, keepdims=True)
    v = jnp.var(x, axis=axis, keepdims=True)
    return (x - m) / jnp.sqrt(v + eps)

def _scatter_add(tgt, idx, src, axis=0):
    return tgt.at[idx].add(src)

def _segment_sum(src, seg, n):
    return jax.ops.segment_sum(src, seg, n)
kernel_name = 'mk_xattn_ffn_d4_seqx_r8_6072d8'

def setup_inputs(seed: int=0):
    np.random.seed(seed)
    _w = jnp.asarray

    def _rec_inputs():
        import jax
        import jax.numpy as jnp
        _rk = jax.random.key(seed)
        x = -0.000125 + 0.9999 * jax.random.normal(jax.random.fold_in(_rk, 1), (4, 512, 128), jnp.float32)
        _lenS = 512 - jax.random.randint(jax.random.fold_in(_rk, 7), (4,), 0, max(1, 512 // 4) + 1, jnp.int32)
        _lenS2 = 32 - jax.random.randint(jax.random.fold_in(_rk, 8), (4,), 0, max(1, 32 // 4) + 1, jnp.int32)
        _ctx_1024P = jax.random.normal(jax.random.fold_in(_rk, 11), (4, 16, 128), jnp.float32)
        _ctx_1024c = jax.random.dirichlet(jax.random.fold_in(_rk, 511), 0.3 * jnp.ones((16,), jnp.float32), (4, 32))
        _ctx_1024t = jnp.einsum('bsk,bkd->bsd', _ctx_1024c, _ctx_1024P)
        _ctx_1024t = _ctx_1024t * jax.lax.rsqrt(jnp.mean(jnp.square(_ctx_1024t)) + 1e-12) * 0.953939
        ctx_1024 = -0.000514642 + 1.00011 * (_ctx_1024t + 0.3 * jax.random.normal(jax.random.fold_in(_rk, 611), (4, 32, 128), jnp.float32))
        _validS = jnp.arange(512)[None, :] < _lenS[:, None]
        _validS2 = jnp.arange(32)[None, :] < _lenS2[:, None]
        _causal = jnp.tril(jnp.ones((512, 512), dtype=bool))
        mask_B_ik0 = jnp.where(jnp.ones((4,), dtype=bool), 68, 1563).astype(jnp.int32)
        mask_Bx1xSxS2_bk1 = jnp.broadcast_to(_validS2[:, None, None, :], (4, 1, 512, 32))
        return (x, ctx_1024, mask_B_ik0, mask_Bx1xSxS2_bk1)
    x, ctx_1024, mask_B_ik0, mask_Bx1xSxS2_bk1 = _rec_inputs()

    def _L0_xattn_setup():
        import jax, jax.numpy as jnp
        import numpy as np
        H, DH, WSIZE, PE_LEN = (8, 64, 4, 300)

        def sinusoidal_pe(T, d, n=10000.0):
            pos = jnp.arange(T, dtype=jnp.float32)[:, None]
            denom = jnp.power(n, 2.0 * jnp.arange(d // 2, dtype=jnp.float32) / d)
            ang = pos / denom
            pe = jnp.zeros((T, d), dtype=jnp.float32)
            pe = pe.at[:, 0::2].set(jnp.sin(ang))
            pe = pe.at[:, 1::2].set(jnp.cos(ang))
            return pe
        key = jax.random.key(seed)
        ks = jax.random.split(key, 6)
        B, NQ, NK, QD, VD = (8, 512, 32, 128, 128)
        inner = H * DH
        return {'x': jax.random.normal(ks[0], (B, NQ, QD), jnp.float32), 'hint_control': jax.random.normal(ks[1], (B, NK, VD), jnp.float32), 'Wq': jax.random.normal(ks[2], (QD, inner), jnp.float32) / np.sqrt(QD), 'Wk': jax.random.normal(ks[3], (VD, inner), jnp.float32) / np.sqrt(VD), 'Wv': jax.random.normal(ks[4], (VD, inner), jnp.float32) / np.sqrt(VD), 'Wo': jax.random.normal(ks[5], (inner, QD), jnp.float32) / np.sqrt(inner), 'bo': jnp.zeros((QD,), jnp.float32)}
    _L0_xattn_all = _L0_xattn_setup()
    _L0_xattn_in = {k: v for k, v in _L0_xattn_all.items() if k in ('Wq', 'Wk', 'Wv', 'Wo', 'bo')}
    del _L0_xattn_all

    def _L0_ffn_setup():
        import jax, jax.numpy as jnp
        import numpy as np
        D_MODEL = 128
        D_FF = 512
        NUM_EXPERTS = 8
        key = jax.random.key(seed)
        ks = jax.random.split(key, 8)
        scale_in = 1.0 / np.sqrt(D_MODEL)
        scale_ff = 1.0 / np.sqrt(D_FF)
        x = jax.random.normal(ks[0], (4, 256, D_MODEL), dtype=jnp.float32)
        gate_w = jax.random.uniform(ks[1], (NUM_EXPERTS, D_MODEL), jnp.float32, -scale_in, scale_in)
        gate_b = jax.random.uniform(ks[2], (NUM_EXPERTS,), jnp.float32, -scale_in, scale_in)
        expert_bias = jnp.zeros((NUM_EXPERTS,), dtype=jnp.float32)
        w1 = jax.random.uniform(ks[3], (NUM_EXPERTS, D_MODEL, D_FF), jnp.float32, -scale_in, scale_in)
        b1 = jax.random.uniform(ks[4], (NUM_EXPERTS, D_FF), jnp.float32, -scale_in, scale_in)
        w2 = jax.random.uniform(ks[5], (NUM_EXPERTS, D_FF, D_MODEL), jnp.float32, -scale_ff, scale_ff)
        b2 = jax.random.uniform(ks[6], (NUM_EXPERTS, D_MODEL), jnp.float32, -scale_ff, scale_ff)
        return {'x': x, 'gate_w': gate_w, 'gate_b': gate_b, 'expert_bias': expert_bias, 'w1': w1, 'b1': b1, 'w2': w2, 'b2': b2}
    _L0_ffn_all = _L0_ffn_setup()
    _L0_ffn_in = {k: v for k, v in _L0_ffn_all.items() if k in ('gate_w', 'gate_b', 'expert_bias', 'w1', 'b1', 'w2', 'b2')}
    del _L0_ffn_all

    def _L1_xattn_setup():
        import jax, jax.numpy as jnp
        import numpy as np
        B, S, D, H = (2, 256, 128, 16)
        DH = D // H

        def _split_heads(x):
            b, s, _ = x.shape
            return x.reshape(b, s, H, DH).transpose(0, 2, 1, 3)
        key = jax.random.key(seed)
        k = jax.random.split(key, 8)
        scale = 0.02
        return {'queries': jax.random.normal(k[0], (B, S, D), dtype=jnp.float32), 'keys': jax.random.normal(k[1], (B, S, D), dtype=jnp.float32), 'values': jax.random.normal(k[2], (B, S, D), dtype=jnp.float32), 'valid_length': jax.random.randint(k[3], (B,), 0, S, dtype=jnp.int64), 'Wq': jax.random.normal(k[4], (D, D), dtype=jnp.float32) * scale, 'Wk': jax.random.normal(k[5], (D, D), dtype=jnp.float32) * scale, 'Wv': jax.random.normal(k[6], (D, D), dtype=jnp.float32) * scale, 'Wo': jax.random.normal(k[7], (D, D), dtype=jnp.float32) * scale}
    _L1_xattn_all = _L1_xattn_setup()
    _L1_xattn_in = {k: v for k, v in _L1_xattn_all.items() if k in ('Wq', 'Wk', 'Wv', 'Wo')}
    del _L1_xattn_all

    def _L1_ffn_setup():
        import jax, jax.numpy as jnp
        import numpy as np
        N_EXPERTS = 16
        TOP_K = int(N_EXPERTS * 0.2)
        EPS = 1e-12
        key = jax.random.key(seed)
        ks = jax.random.split(key, 6)
        B, T, D, H, E = (4, 128, 128, 256, N_EXPERTS)
        x = jax.random.normal(ks[0], (B, T, D), dtype=jnp.float32)
        gate = jax.random.normal(ks[1], (D, E), dtype=jnp.float32)
        W1 = jax.random.normal(ks[2], (E, D, H), dtype=jnp.float32) * (1.0 / np.sqrt(D))
        b1 = jax.random.normal(ks[3], (E, H), dtype=jnp.float32) * 0.02
        W2 = jax.random.normal(ks[4], (E, H, D), dtype=jnp.float32) * (1.0 / np.sqrt(H))
        b2 = jax.random.normal(ks[5], (E, D), dtype=jnp.float32) * 0.02
        return {'x': x, 'gate': gate, 'W1': W1, 'b1': b1, 'W2': W2, 'b2': b2}
    _L1_ffn_all = _L1_ffn_setup()
    _L1_ffn_in = {k: v for k, v in _L1_ffn_all.items() if k in ('gate', 'W1', 'b1', 'W2', 'b2')}
    del _L1_ffn_all

    def _L2_xattn_setup():
        import jax, jax.numpy as jnp
        import numpy as np
        import math
        D_MODEL = 128
        N_HEADS = 16
        key = jax.random.key(seed)
        ks = jax.random.split(key, 11)
        N, L, S = (2, 256, 256)
        d = D_MODEL
        s = 1.0 / math.sqrt(d)
        return {'queries': jax.random.normal(ks[0], (N, L, d), dtype=jnp.float32), 'keys': jax.random.normal(ks[1], (N, S, d), dtype=jnp.float32), 'values': jax.random.normal(ks[2], (N, S, d), dtype=jnp.float32), 'Wq': jax.random.normal(ks[3], (d, d), dtype=jnp.float32) * s, 'bq': jax.random.normal(ks[4], (d,), dtype=jnp.float32) * s, 'Wk': jax.random.normal(ks[5], (d, d), dtype=jnp.float32) * s, 'bk': jax.random.normal(ks[6], (d,), dtype=jnp.float32) * s, 'Wv': jax.random.normal(ks[7], (d, d), dtype=jnp.float32) * s, 'bv': jax.random.normal(ks[8], (d,), dtype=jnp.float32) * s, 'Wo': jax.random.normal(ks[9], (d, d), dtype=jnp.float32) * s, 'bo': jax.random.normal(ks[10], (d,), dtype=jnp.float32) * s}
    _L2_xattn_all = _L2_xattn_setup()
    _L2_xattn_in = {k: v for k, v in _L2_xattn_all.items() if k in ('Wq', 'bq', 'Wk', 'bk', 'Wv', 'bv', 'Wo', 'bo')}
    del _L2_xattn_all

    def _L2_ffn_setup():
        import jax, jax.numpy as jnp
        import numpy as np

        def _bitlinear(x, w_latent):
            scale = jax.lax.stop_gradient(jnp.clip(jnp.mean(jnp.abs(w_latent), axis=1, keepdims=True), 1e-05, None))
            tern = jnp.clip(jnp.round(w_latent / scale), -1.0, 1.0)
            w = w_latent + jax.lax.stop_gradient(tern - w_latent)
            return x @ (w * scale).T
        key = jax.random.key(seed)
        ks = jax.random.split(key, 6)
        dim, hidden, rank = (128, 512, 16)
        B, S = (4, 512)
        x = jax.random.normal(ks[0], (B, S, dim), dtype=jnp.float32)
        w_fc = 0.02 * jax.random.normal(ks[1], (hidden, dim), dtype=jnp.float32)
        w_proj = 0.02 * jax.random.normal(ks[2], (dim, hidden), dtype=jnp.float32)
        u = 0.02 * jax.random.normal(ks[3], (hidden, rank), dtype=jnp.float32)
        v = 0.02 * jax.random.normal(ks[4], (rank, dim), dtype=jnp.float32)
        fast_b = jax.random.normal(ks[5], (rank, rank), dtype=jnp.float32)
        gate = jnp.float32(0.05)
        return {'x': x, 'fast_b': fast_b, 'w_fc': w_fc, 'w_proj': w_proj, 'u': u, 'v': v, 'gate': gate}
    _L2_ffn_all = _L2_ffn_setup()
    _L2_ffn_in = {k: v for k, v in _L2_ffn_all.items() if k in ('fast_b', 'w_fc', 'w_proj', 'u', 'v', 'gate')}
    del _L2_ffn_all

    def _L3_xattn_setup():
        import jax, jax.numpy as jnp
        import numpy as np
        HEADS = 16
        D_MODEL = 128
        D_K = D_MODEL // HEADS
        B, S = (2, 256)
        NEG = -1000000000.0
        key = jax.random.key(seed)
        ks = jax.random.split(key, 8)
        q = jax.random.normal(ks[0], (B, S, D_MODEL), dtype=jnp.float32)
        k = jax.random.normal(ks[1], (B, S, D_MODEL), dtype=jnp.float32)
        v = jax.random.normal(ks[2], (B, S, D_MODEL), dtype=jnp.float32)
        mask = jax.random.randint(ks[3], (B, 1, S, S), 0, 2) > 0
        scale = 1.0 / np.sqrt(D_MODEL)
        Wq = jax.random.normal(ks[4], (D_MODEL, D_MODEL), dtype=jnp.float32) * scale
        Wk = jax.random.normal(ks[5], (D_MODEL, D_MODEL), dtype=jnp.float32) * scale
        Wv = jax.random.normal(ks[6], (D_MODEL, D_MODEL), dtype=jnp.float32) * scale
        Wo = jax.random.normal(ks[7], (D_MODEL, D_MODEL), dtype=jnp.float32) * scale
        return {'q': q, 'k': k, 'v': v, 'mask': mask, 'Wq': Wq, 'Wk': Wk, 'Wv': Wv, 'Wo': Wo}
    _L3_xattn_all = _L3_xattn_setup()
    _L3_xattn_in = {k: v for k, v in _L3_xattn_all.items() if k in ('Wq', 'Wk', 'Wv', 'Wo')}
    del _L3_xattn_all

    def _L3_ffn_setup():
        import jax, jax.numpy as jnp
        import numpy as np
        D_MODEL = 128
        NUM_TILES = 64
        TPC = 8
        NUM_CLUSTERS = NUM_TILES // TPC
        GRID = 16
        COMP_H = 32
        NUM_KNOTS = 8
        EPS_LN = 1e-05

        def _calibrate(scores, knots, temperature):
            K = knots.shape[0]
            normalized = jax.nn.sigmoid(scores / (temperature[0] + 1e-06))
            idx_float = normalized * (K - 1)
            idx_low = jnp.clip(idx_float.astype(jnp.int32), 0, K - 2)
            idx_high = idx_low + 1
            t = idx_float - idx_low.astype(scores.dtype)
            val_low = knots[idx_low]
            val_high = knots[idx_high]
            return val_low + t * (val_high - val_low)

        def _forward(x, signatures_raw, knot_values, temperature, compress_w1, compress_b1, compress_w2, compress_b2, spline_w1, spline_b1, spline_w2, spline_b2, directions, norm_gamma, norm_beta, output_scale):
            B, T, D = x.shape
            xf = x.reshape(-1, D)
            q = jnp.where(signatures_raw > 0.3, 1.0, jnp.where(signatures_raw < -0.3, -1.0, 0.0)).astype(signatures_raw.dtype)
            sigs = signatures_raw + jax.lax.stop_gradient(q - signatures_raw)
            cluster_sigs = jnp.sign(sigs.reshape(NUM_CLUSTERS, TPC, D).mean(axis=1))
            cluster_scores = xf @ cluster_sigs.T
            cluster_gates = _calibrate(cluster_scores, knot_values, temperature)
            cluster_idx = jnp.argmax(cluster_gates, axis=-1)
            tile_scores = xf @ sigs.T
            tile_gates = _calibrate(tile_scores, knot_values, temperature)
            gates_by_cluster = tile_gates.reshape(-1, NUM_CLUSTERS, TPC)
            sel_gates = jnp.take_along_axis(gates_by_cluster, cluster_idx[:, None, None], axis=1)[:, 0, :]
            local_idx = jnp.argmax(sel_gates, axis=-1)
            tile_idx = cluster_idx * TPC + local_idx
            h = jax.nn.gelu(xf @ compress_w1 + compress_b1, approximate=False)
            comp = jnp.tanh(h @ compress_w2 + compress_b2)
            w1 = spline_w1[tile_idx]
            b1 = spline_b1[tile_idx]
            hh = jax.nn.relu(jnp.einsum('ni,nig->ng', comp, w1) + b1)
            w2 = spline_w2[tile_idx]
            b2 = spline_b2[tile_idx]
            mag = jnp.einsum('ng,ngo->no', hh, w2) + b2
            ffn_out = mag * directions[tile_idx] * output_scale[0]
            y = xf + ffn_out
            mu = y.mean(axis=-1, keepdims=True)
            var = ((y - mu) ** 2).mean(axis=-1, keepdims=True)
            y = (y - mu) / jnp.sqrt(var + EPS_LN) * norm_gamma + norm_beta
            return y.reshape(B, T, D)
        key = jax.random.key(seed)
        ks = jax.random.split(key, 12)
        B, T = (4, 512)
        x = jax.random.normal(ks[0], (B, T, D_MODEL), dtype=jnp.float32)
        signatures_raw = jax.random.normal(ks[1], (NUM_TILES, D_MODEL), dtype=jnp.float32) * 0.5
        knot_values = jax.nn.sigmoid(jnp.linspace(-3.0, 3.0, NUM_KNOTS).astype(jnp.float32))
        temperature = jnp.ones((1,), dtype=jnp.float32)
        compress_w1 = jax.random.normal(ks[2], (D_MODEL, COMP_H), dtype=jnp.float32) * (1.0 / np.sqrt(D_MODEL))
        compress_b1 = jnp.zeros((COMP_H,), dtype=jnp.float32)
        compress_w2 = jax.random.normal(ks[3], (COMP_H, 2), dtype=jnp.float32) * (1.0 / np.sqrt(COMP_H))
        compress_b2 = jnp.zeros((2,), dtype=jnp.float32)
        spline_w1 = jax.random.normal(ks[4], (NUM_TILES, 2, GRID), dtype=jnp.float32) * (1.0 / np.sqrt(2.0))
        spline_b1 = jnp.zeros((NUM_TILES, GRID), dtype=jnp.float32)
        spline_w2 = jax.random.normal(ks[5], (NUM_TILES, GRID, 1), dtype=jnp.float32) * (1.0 / np.sqrt(GRID))
        spline_b2 = jnp.zeros((NUM_TILES, 1), dtype=jnp.float32)
        directions = jax.random.normal(ks[6], (NUM_TILES, D_MODEL), dtype=jnp.float32) * 0.02
        norm_gamma = jnp.ones((D_MODEL,), dtype=jnp.float32)
        norm_beta = jnp.zeros((D_MODEL,), dtype=jnp.float32)
        output_scale = jnp.ones((1,), dtype=jnp.float32) * 0.1
        return dict(x=x, signatures_raw=signatures_raw, knot_values=knot_values, temperature=temperature, compress_w1=compress_w1, compress_b1=compress_b1, compress_w2=compress_w2, compress_b2=compress_b2, spline_w1=spline_w1, spline_b1=spline_b1, spline_w2=spline_w2, spline_b2=spline_b2, directions=directions, norm_gamma=norm_gamma, norm_beta=norm_beta, output_scale=output_scale)
    _L3_ffn_all = _L3_ffn_setup()
    _L3_ffn_in = {k: v for k, v in _L3_ffn_all.items() if k in ('signatures_raw', 'knot_values', 'temperature', 'compress_w1', 'compress_b1', 'compress_w2', 'compress_b2', 'spline_w1', 'spline_b1', 'spline_w2', 'spline_b2', 'directions', 'norm_gamma', 'norm_beta', 'output_scale')}
    del _L3_ffn_all
    return {'x': x, 'ctx_1024': ctx_1024, 'mask_B_ik0': mask_B_ik0, 'mask_Bx1xSxS2_bk1': mask_Bx1xSxS2_bk1, 'L0_xattn_Wq': _L0_xattn_in['Wq'], 'L0_xattn_Wk': _L0_xattn_in['Wk'], 'L0_xattn_Wv': _L0_xattn_in['Wv'], 'L0_xattn_Wo': _L0_xattn_in['Wo'], 'L0_xattn_bo': _L0_xattn_in['bo'], 'L0_ffn_gate_w': _L0_ffn_in['gate_w'], 'L0_ffn_gate_b': _L0_ffn_in['gate_b'], 'L0_ffn_expert_bias': _L0_ffn_in['expert_bias'], 'L0_ffn_w1': _L0_ffn_in['w1'], 'L0_ffn_b1': _L0_ffn_in['b1'], 'L0_ffn_w2': _L0_ffn_in['w2'], 'L0_ffn_b2': _L0_ffn_in['b2'], 'L1_xattn_Wq': _L1_xattn_in['Wq'], 'L1_xattn_Wk': _L1_xattn_in['Wk'], 'L1_xattn_Wv': _L1_xattn_in['Wv'], 'L1_xattn_Wo': _L1_xattn_in['Wo'], 'L1_ffn_gate': _L1_ffn_in['gate'], 'L1_ffn_W1': _L1_ffn_in['W1'], 'L1_ffn_b1': _L1_ffn_in['b1'], 'L1_ffn_W2': _L1_ffn_in['W2'], 'L1_ffn_b2': _L1_ffn_in['b2'], 'L2_xattn_Wq': _L2_xattn_in['Wq'], 'L2_xattn_bq': _L2_xattn_in['bq'], 'L2_xattn_Wk': _L2_xattn_in['Wk'], 'L2_xattn_bk': _L2_xattn_in['bk'], 'L2_xattn_Wv': _L2_xattn_in['Wv'], 'L2_xattn_bv': _L2_xattn_in['bv'], 'L2_xattn_Wo': _L2_xattn_in['Wo'], 'L2_xattn_bo': _L2_xattn_in['bo'], 'L2_ffn_fast_b': _L2_ffn_in['fast_b'], 'L2_ffn_w_fc': _L2_ffn_in['w_fc'], 'L2_ffn_w_proj': _L2_ffn_in['w_proj'], 'L2_ffn_u': _L2_ffn_in['u'], 'L2_ffn_v': _L2_ffn_in['v'], 'L2_ffn_gate': _L2_ffn_in['gate'], 'L3_xattn_Wq': _L3_xattn_in['Wq'], 'L3_xattn_Wk': _L3_xattn_in['Wk'], 'L3_xattn_Wv': _L3_xattn_in['Wv'], 'L3_xattn_Wo': _L3_xattn_in['Wo'], 'L3_ffn_signatures_raw': _L3_ffn_in['signatures_raw'], 'L3_ffn_knot_values': _L3_ffn_in['knot_values'], 'L3_ffn_temperature': _L3_ffn_in['temperature'], 'L3_ffn_compress_w1': _L3_ffn_in['compress_w1'], 'L3_ffn_compress_b1': _L3_ffn_in['compress_b1'], 'L3_ffn_compress_w2': _L3_ffn_in['compress_w2'], 'L3_ffn_compress_b2': _L3_ffn_in['compress_b2'], 'L3_ffn_spline_w1': _L3_ffn_in['spline_w1'], 'L3_ffn_spline_b1': _L3_ffn_in['spline_b1'], 'L3_ffn_spline_w2': _L3_ffn_in['spline_w2'], 'L3_ffn_spline_b2': _L3_ffn_in['spline_b2'], 'L3_ffn_directions': _L3_ffn_in['directions'], 'L3_ffn_norm_gamma': _L3_ffn_in['norm_gamma'], 'L3_ffn_norm_beta': _L3_ffn_in['norm_beta'], 'L3_ffn_output_scale': _L3_ffn_in['output_scale']}

def reference(x, ctx_1024, mask_B_ik0, mask_Bx1xSxS2_bk1, L0_xattn_Wq, L0_xattn_Wk, L0_xattn_Wv, L0_xattn_Wo, L0_xattn_bo, L0_ffn_gate_w, L0_ffn_gate_b, L0_ffn_expert_bias, L0_ffn_w1, L0_ffn_b1, L0_ffn_w2, L0_ffn_b2, L1_xattn_Wq, L1_xattn_Wk, L1_xattn_Wv, L1_xattn_Wo, L1_ffn_gate, L1_ffn_W1, L1_ffn_b1, L1_ffn_W2, L1_ffn_b2, L2_xattn_Wq, L2_xattn_bq, L2_xattn_Wk, L2_xattn_bk, L2_xattn_Wv, L2_xattn_bv, L2_xattn_Wo, L2_xattn_bo, L2_ffn_fast_b, L2_ffn_w_fc, L2_ffn_w_proj, L2_ffn_u, L2_ffn_v, L2_ffn_gate, L3_xattn_Wq, L3_xattn_Wk, L3_xattn_Wv, L3_xattn_Wo, L3_ffn_signatures_raw, L3_ffn_knot_values, L3_ffn_temperature, L3_ffn_compress_w1, L3_ffn_compress_b1, L3_ffn_compress_w2, L3_ffn_compress_b2, L3_ffn_spline_w1, L3_ffn_spline_b1, L3_ffn_spline_w2, L3_ffn_spline_b2, L3_ffn_directions, L3_ffn_norm_gamma, L3_ffn_norm_beta, L3_ffn_output_scale):
    import jax
    import jax.numpy as jnp

    def _L0_xattn_ref(x, hint_control, Wq, Wk, Wv, Wo, bo):
        import jax, jax.numpy as jnp
        import numpy as np
        H, DH, WSIZE, PE_LEN = (8, 64, 4, 300)

        def sinusoidal_pe(T, d, n=10000.0):
            pos = jnp.arange(T, dtype=jnp.float32)[:, None]
            denom = jnp.power(n, 2.0 * jnp.arange(d // 2, dtype=jnp.float32) / d)
            ang = pos / denom
            pe = jnp.zeros((T, d), dtype=jnp.float32)
            pe = pe.at[:, 0::2].set(jnp.sin(ang))
            pe = pe.at[:, 1::2].set(jnp.cos(ang))
            return pe
        B, NQ, _ = x.shape
        NK = hint_control.shape[1]
        scale = DH ** (-0.5)
        pe = sinusoidal_pe(PE_LEN, hint_control.shape[-1])[:NK]
        hc = hint_control + pe[None]
        q = (x @ Wq).reshape(B, NQ, H, DH).transpose(0, 2, 1, 3)
        k = (hc @ Wk).reshape(B, NK, H, DH).transpose(0, 2, 1, 3)
        v = (hc @ Wv).reshape(B, NK, H, DH).transpose(0, 2, 1, 3)
        qb = q.reshape(B, H, WSIZE, NQ // WSIZE, DH)
        kb = k.reshape(B, H, WSIZE, NK // WSIZE, DH)
        vb = v.reshape(B, H, WSIZE, NK // WSIZE, DH)
        sim = jnp.einsum('bhwid,bhwjd->bhwij', qb, kb) * scale
        attn = jax.nn.softmax(sim, axis=-1)
        out = jnp.einsum('bhwij,bhwjd->bhwid', attn, vb)
        out = out.reshape(B, H, NQ, DH).transpose(0, 2, 1, 3).reshape(B, NQ, H * DH)
        return out @ Wo + bo

    def _L0_ffn_ref(x, gate_w, gate_b, expert_bias, w1, b1, w2, b2):
        import jax, jax.numpy as jnp
        import numpy as np
        D_MODEL = 128
        D_FF = 512
        NUM_EXPERTS = 8
        gate_logits = jnp.einsum('bsd,ed->bse', x, gate_w) + gate_b + expert_bias
        top_idx = jnp.argmax(gate_logits, axis=-1)
        out = jnp.zeros_like(x)
        for e in range(NUM_EXPERTS):
            mask = (top_idx == e)[..., None].astype(x.dtype)
            h = jax.nn.relu(jnp.einsum('bsd,df->bsf', x, w1[e]) + b1[e])
            y = jnp.einsum('bsf,fd->bsd', h, w2[e]) + b2[e]
            out = out + mask * y
        return out

    def _L1_xattn_ref(queries, keys, values, valid_length, Wq, Wk, Wv, Wo):
        import jax, jax.numpy as jnp
        import numpy as np
        B, S, D, H = (2, 256, 128, 16)
        DH = D // H

        def _split_heads(x):
            b, s, _ = x.shape
            return x.reshape(b, s, H, DH).transpose(0, 2, 1, 3)
        q = _split_heads(queries @ Wq)
        k = _split_heads(keys @ Wk)
        v = _split_heads(values @ Wv)
        scores = jnp.einsum('bhqd,bhkd->bhqk', q, k)
        attn = jax.nn.softmax(scores, axis=-1)
        out = jnp.einsum('bhqk,bhkd->bhqd', attn, v)
        out = out.transpose(0, 2, 1, 3).reshape(queries.shape[0], queries.shape[1], D)
        return out @ Wo

    def _L1_ffn_ref(x, gate, W1, b1, W2, b2):
        import jax, jax.numpy as jnp
        import numpy as np
        N_EXPERTS = 16
        TOP_K = int(N_EXPERTS * 0.2)
        EPS = 1e-12
        raw_gate = jax.nn.softmax(jnp.einsum('btd,de->bte', x, gate), axis=-1)
        _, topk_idx = jax.lax.top_k(raw_gate, TOP_K)
        mask = jax.nn.one_hot(topk_idx, raw_gate.shape[-1], dtype=raw_gate.dtype).sum(axis=2)
        gate_topk = mask * raw_gate
        gate_topk = gate_topk / jnp.maximum(jnp.sum(jnp.abs(gate_topk), axis=-1, keepdims=True), EPS)
        hidden = jax.nn.relu(jnp.einsum('btd,edh->bteh', x, W1) + b1)
        expert_out = jnp.einsum('bteh,ehd->bted', hidden, W2) + b2
        return jnp.einsum('bte,bted->btd', gate_topk, expert_out)

    def _L2_xattn_ref(queries, keys, values, Wq, bq, Wk, bk, Wv, bv, Wo, bo):
        import jax, jax.numpy as jnp
        import numpy as np
        import math
        D_MODEL = 128
        N_HEADS = 16
        N, L, _ = queries.shape
        S = keys.shape[1]
        H = N_HEADS
        q = (queries @ Wq.T + bq).reshape(N, L, H, -1)
        k = (keys @ Wk.T + bk).reshape(N, S, H, -1)
        v = (values @ Wv.T + bv).reshape(N, S, H, -1)
        D = k.shape[-1]
        sm = jnp.einsum('nlhd,nshd->nlhs', q, k) / math.sqrt(D)
        causal_mask = jnp.triu(jnp.ones((L, S), dtype=bool), k=1)
        sm = jnp.where(causal_mask[None, :, None, :], -jnp.inf, sm)
        sm = jax.nn.softmax(sm, axis=-1)
        attn = jnp.einsum('nlhs,nshd->nlhd', sm, v)
        new_values = attn.reshape(N, L, H * D)
        return new_values @ Wo.T + bo

    def _L2_ffn_ref(x, fast_b, w_fc, w_proj, u, v, gate):
        import jax, jax.numpy as jnp
        import numpy as np

        def _bitlinear(x, w_latent):
            scale = jax.lax.stop_gradient(jnp.clip(jnp.mean(jnp.abs(w_latent), axis=1, keepdims=True), 1e-05, None))
            tern = jnp.clip(jnp.round(w_latent / scale), -1.0, 1.0)
            w = w_latent + jax.lax.stop_gradient(tern - w_latent)
            return x @ (w * scale).T
        h = _bitlinear(x, w_fc) + gate * (x @ v.T @ fast_b.T @ u.T)
        r = jnp.maximum(h, 0.0)
        return _bitlinear(r * r, w_proj)

    def _L3_xattn_ref(q, k, v, mask, Wq, Wk, Wv, Wo):
        import jax, jax.numpy as jnp
        import numpy as np
        HEADS = 16
        D_MODEL = 128
        D_K = D_MODEL // HEADS
        B, S = (2, 256)
        NEG = -1000000000.0
        b, s, _ = q.shape

        def proj(x, W):
            return (x @ W.T).reshape(b, -1, HEADS, D_K).transpose(0, 2, 1, 3)
        qh, kh, vh = (proj(q, Wq), proj(k, Wk), proj(v, Wv))
        att = jnp.einsum('bhqd,bhkd->bhqk', qh, kh) / jnp.sqrt(jnp.float32(D_K))
        att = jnp.where(mask, NEG, att)
        att = jax.nn.softmax(att, axis=-1)
        out = jnp.einsum('bhqk,bhkd->bhqd', att, vh)
        out = out.transpose(0, 2, 1, 3).reshape(b, -1, D_MODEL)
        return out @ Wo.T

    def _L3_ffn_ref(x, signatures_raw, knot_values, temperature, compress_w1, compress_b1, compress_w2, compress_b2, spline_w1, spline_b1, spline_w2, spline_b2, directions, norm_gamma, norm_beta, output_scale):
        import jax, jax.numpy as jnp
        import numpy as np
        D_MODEL = 128
        NUM_TILES = 64
        TPC = 8
        NUM_CLUSTERS = NUM_TILES // TPC
        GRID = 16
        COMP_H = 32
        NUM_KNOTS = 8
        EPS_LN = 1e-05

        def _calibrate(scores, knots, temperature):
            K = knots.shape[0]
            normalized = jax.nn.sigmoid(scores / (temperature[0] + 1e-06))
            idx_float = normalized * (K - 1)
            idx_low = jnp.clip(idx_float.astype(jnp.int32), 0, K - 2)
            idx_high = idx_low + 1
            t = idx_float - idx_low.astype(scores.dtype)
            val_low = knots[idx_low]
            val_high = knots[idx_high]
            return val_low + t * (val_high - val_low)

        def _forward(x, signatures_raw, knot_values, temperature, compress_w1, compress_b1, compress_w2, compress_b2, spline_w1, spline_b1, spline_w2, spline_b2, directions, norm_gamma, norm_beta, output_scale):
            B, T, D = x.shape
            xf = x.reshape(-1, D)
            q = jnp.where(signatures_raw > 0.3, 1.0, jnp.where(signatures_raw < -0.3, -1.0, 0.0)).astype(signatures_raw.dtype)
            sigs = signatures_raw + jax.lax.stop_gradient(q - signatures_raw)
            cluster_sigs = jnp.sign(sigs.reshape(NUM_CLUSTERS, TPC, D).mean(axis=1))
            cluster_scores = xf @ cluster_sigs.T
            cluster_gates = _calibrate(cluster_scores, knot_values, temperature)
            cluster_idx = jnp.argmax(cluster_gates, axis=-1)
            tile_scores = xf @ sigs.T
            tile_gates = _calibrate(tile_scores, knot_values, temperature)
            gates_by_cluster = tile_gates.reshape(-1, NUM_CLUSTERS, TPC)
            sel_gates = jnp.take_along_axis(gates_by_cluster, cluster_idx[:, None, None], axis=1)[:, 0, :]
            local_idx = jnp.argmax(sel_gates, axis=-1)
            tile_idx = cluster_idx * TPC + local_idx
            h = jax.nn.gelu(xf @ compress_w1 + compress_b1, approximate=False)
            comp = jnp.tanh(h @ compress_w2 + compress_b2)
            w1 = spline_w1[tile_idx]
            b1 = spline_b1[tile_idx]
            hh = jax.nn.relu(jnp.einsum('ni,nig->ng', comp, w1) + b1)
            w2 = spline_w2[tile_idx]
            b2 = spline_b2[tile_idx]
            mag = jnp.einsum('ng,ngo->no', hh, w2) + b2
            ffn_out = mag * directions[tile_idx] * output_scale[0]
            y = xf + ffn_out
            mu = y.mean(axis=-1, keepdims=True)
            var = ((y - mu) ** 2).mean(axis=-1, keepdims=True)
            y = (y - mu) / jnp.sqrt(var + EPS_LN) * norm_gamma + norm_beta
            return y.reshape(B, T, D)
        return _forward(x, signatures_raw, knot_values, temperature, compress_w1, compress_b1, compress_w2, compress_b2, spline_w1, spline_b1, spline_w2, spline_b2, directions, norm_gamma, norm_beta, output_scale)
    x = x + _L0_xattn_ref(_layernorm(x, axis=-1), ctx_1024, L0_xattn_Wq, L0_xattn_Wk, L0_xattn_Wv, L0_xattn_Wo, L0_xattn_bo)
    x = x + _L0_ffn_ref(_layernorm(x, axis=-1), L0_ffn_gate_w, L0_ffn_gate_b, L0_ffn_expert_bias, L0_ffn_w1, L0_ffn_b1, L0_ffn_w2, L0_ffn_b2)
    x = x + _L1_xattn_ref(_layernorm(x, axis=-1), ctx_1024, ctx_1024, mask_B_ik0, L1_xattn_Wq, L1_xattn_Wk, L1_xattn_Wv, L1_xattn_Wo)
    x = x + _L1_ffn_ref(_layernorm(x, axis=-1), L1_ffn_gate, L1_ffn_W1, L1_ffn_b1, L1_ffn_W2, L1_ffn_b2)
    x = x + _L2_xattn_ref(_layernorm(x, axis=-1), ctx_1024, ctx_1024, L2_xattn_Wq, L2_xattn_bq, L2_xattn_Wk, L2_xattn_bk, L2_xattn_Wv, L2_xattn_bv, L2_xattn_Wo, L2_xattn_bo)
    x = x + _L2_ffn_ref(_layernorm(x, axis=-1), L2_ffn_fast_b, L2_ffn_w_fc, L2_ffn_w_proj, L2_ffn_u, L2_ffn_v, L2_ffn_gate)
    x = x + _L3_xattn_ref(_layernorm(x, axis=-1), ctx_1024, ctx_1024, mask_Bx1xSxS2_bk1, L3_xattn_Wq, L3_xattn_Wk, L3_xattn_Wv, L3_xattn_Wo)
    x = x + _L3_ffn_ref(_layernorm(x, axis=-1), L3_ffn_signatures_raw, L3_ffn_knot_values, L3_ffn_temperature, L3_ffn_compress_w1, L3_ffn_compress_b1, L3_ffn_compress_w2, L3_ffn_compress_b2, L3_ffn_spline_w1, L3_ffn_spline_b1, L3_ffn_spline_w2, L3_ffn_spline_b2, L3_ffn_directions, L3_ffn_norm_gamma, L3_ffn_norm_beta, L3_ffn_output_scale)
    return x

_drawn_inputs = setup_inputs


def setup_inputs(seed=0):
    import zlib

    import numpy as np

    out = dict(_drawn_inputs(seed))
    spreads = {'L0_xattn_bo': (0.0, 0.1),
     'L0_ffn_expert_bias': (0.0, 0.1),
     'L3_ffn_compress_b1': (0.0, 2.0),
     'L3_ffn_compress_b2': (0.0, 2.0),
     'L3_ffn_spline_b1': (0.0, 2.0),
     'L3_ffn_spline_b2': (0.0, 2.0),
     'L3_ffn_norm_gamma': (1.0, 0.6),
     'L3_ffn_norm_beta': (0.0, 0.8)}
    factors = {'L1_xattn_Wq': 8.0,
     'L1_xattn_Wk': 8.0,
     'L1_ffn_b1': 7.296,
     'L1_ffn_b2': 5.02,
     'L2_xattn_bq': 4.137,
     'L2_xattn_bk': 64.0,
     'L2_ffn_fast_b': 8.0,
     'L2_ffn_w_fc': 8.0,
     'L2_ffn_w_proj': 8.0,
     'L2_ffn_u': 8.0,
     'L2_ffn_v': 8.0,
     'L3_ffn_signatures_raw': 8.0,
     'L3_ffn_knot_values': 8.0,
     'L3_ffn_compress_w1': 8.0,
     'L3_ffn_compress_w2': 8.0,
     'L3_ffn_spline_w1': 8.0,
     'L3_ffn_spline_w2': 8.0,
     'L3_ffn_directions': 8.0}
    for name, (base, spread) in spreads.items():
        noise = np.random.default_rng([zlib.crc32(name.encode()), seed]).standard_normal(out[name].shape)
        drawn = base * np.exp(spread * noise) if base else spread * noise
        out[name] = jnp.asarray(drawn.astype(out[name].dtype))
    for name, factor in factors.items():
        out[name] = (out[name] * factor).astype(out[name].dtype)
    return out
```

```python
from contextlib import ExitStack

import concourse.bass as bass
from concourse import mybir

F32 = mybir.dt.float32
U8 = mybir.dt.uint8
ALU = mybir.AluOpType
ACT = mybir.ActivationFunctionType
AX_X = mybir.AxisListType.X

P = 128
B, S, D = 4, 512, 128
W = S // P
SK = 32
H0, DH0, KW = 8, 64, 8
H, DH = 16, 8
HC = 4
VC = HC * DH + HC
EPS = 1e-5
BIG = 3.0e38
MOE = {1: (8, 4), 3: (16, 2)}
NEG3 = -1.0e9 * DH ** 0.5
KNOTS = 8
CL, TPC = 8, 8
NT = CL * TPC
GRID = 16
TAB = 4 * GRID + 1 + D
COMP = 32


def build(nc, A, out):
    ctx = ExitStack()
    with ctx:
        def sb(name, cols, parts=P, dt=F32):
            return ctx.enter_context(nc.sbuf_tensor(name, [parts, cols], dt))

        def sem(name):
            return ctx.enter_context(nc.semaphore(name))

        x = sb("x", B * S)
        bank = [ctx.enter_context(nc.psum_tensor(f"bank{i}", [P, 512], F32)) for i in range(8)]
        xT_ps, q_ps, s_ps, e_ps, y_ps = bank[0], bank[1], bank[2:4], bank[4:6], bank[7]
        o_ps = [bank[6], bank[1]]
        ident = sb("ident", P)
        ones = sb("ones", P)
        onerow = sb("onerow", P, parts=1)
        mask16 = sb("mask16", H)
        mask4 = sb("mask4", HC)
        desc = sb("desc", 16)
        mhalf = sb("mhalf", W)
        stats = sb("stats", W * 6)
        mv = sb("mv", W * 2)
        veps = sb("veps", W)
        rstd = sb("rstd", W)
        xn = sb("xn", S)
        xnT = sb("xnT", S)
        ctxT = sb("ctxT", B * SK)
        peT = sb("peT", SK)
        hcT = sb("hcT", B * SK)
        ctxR = sb("ctxR", B * P)
        wk0, wv0 = sb("wk0", 512), sb("wv0", 512)
        wq0T, wo0 = sb("wq0T", 512), sb("wo0", 512)
        kT0 = sb("kT0", 512)
        vZ = sb("vZ", 4 * 16 * 64)
        A0 = sb("A0", B * 256)
        VW0 = sb("VW0", B * W * P, parts=64)
        bo_row = {0: sb("bo0", 512, parts=1), 4: sb("bo4", 512, parts=1)}
        m0 = sb("m0", 32)
        r0 = sb("r0", 32)
        p0 = sb("p0", 256)
        pT0 = sb("pT0", 512, parts=64)
        AL = (2, 4, 6)
        wq = {l: sb(f"wq{l}", P) for l in AL}
        wk = {l: sb(f"wk{l}", P) for l in AL}
        wv = {l: sb(f"wv{l}", P) for l in AL}
        wo = {l: sb(f"wo{l}", P) for l in AL}
        bq, bk = sb("bq", 1), sb("bk", 1)
        bv_row = sb("bv_row", P, parts=1)
        kT = sb("kT", B * SK)
        kB = {l: sb(f"kB{l}", B * 512) for l in AL}
        vB = {l: sb(f"vB{l}", B * 4 * VC) for l in AL}
        cap4 = sb("cap4", SK)
        cap6 = sb("cap6", B * W * SK)
        mask_u8 = sb("mask_u8", B * W * SK, dt=U8)
        neg3 = sb("neg3", B * W * SK)
        qT = sb("qT", S)
        mx = sb("mx", 2 * H)
        e_sb = sb("e_sb", 2 * 512)
        eT = sb("eT", 2 * 512)
        rs = sb("rs", 2 * H)
        on = sb("on", S)
        oT = sb("oT", S)
        xnT_all = sb("xnT_all", B * S)
        gw = {l: sb(f"gw{l}", MOE[l][0]) for l in MOE}
        gb = sb("gb", 8)
        eb = sb("eb", 8)
        b1 = {l: sb(f"b1_{l}", MOE[l][0] * MOE[l][1]) for l in MOE}
        b2 = {l: sb(f"b2_{l}", P, parts=MOE[l][0]) for l in MOE}
        b1e = sb("b1e", 4)
        gates = {l: sb(f"gates{l}", B * W * MOE[l][0]) for l in MOE}
        gv = sb("gv", W * 16)
        ge = sb("ge", W * 16)
        gr = sb("gr", W * 16)
        gsel = sb("gsel", W * 16)
        gred = sb("gred", W * 8)
        gT = sb("gT", 512, parts=16)
        ring1 = {l: sb(f"ring1_{l}", 2 * MOE[l][1] * P) for l in MOE}
        ring2 = {l: sb(f"ring2_{l}", 2 * MOE[l][1] * P) for l in MOE}
        h_sb = sb("h_sb", 2 * 4 * S)
        wfc, wpj = sb("wfc", 512), sb("wpj", 512)
        ab = sb("ab", 512)
        t5 = sb("t5", 512)
        sc5 = sb("sc5", 16)
        wfcT, wpjT = sb("wfcT", 512), sb("wpjT", 512)
        fbT, v5, u5T = sb("fbT", 16, parts=16), sb("v5", P, parts=16), sb("u5T", 512, parts=16)
        t1 = sb("t1", P, parts=16)
        gate5 = sb("gate5", 1)
        r5 = sb("r5", 2 * S)
        raw = sb("raw", NT)
        sgq = sb("sgq", 2 * NT)
        rhs7 = sb("rhs7", CL + NT)
        csum = sb("csum", 2 * CL)
        cw1 = sb("cw1", COMP)
        cb1 = sb("cb1", 1, parts=COMP)
        cw2 = sb("cw2", 2, parts=COMP)
        cb2 = sb("cb2", 2)
        table = sb("table", TAB, parts=NT)
        knots = sb("knots", KNOTS)
        dknots = sb("dknots", KNOTS)
        temp = sb("temp", 2)
        oscale = sb("oscale", 1)
        gamma, beta = sb("gamma", P), sb("beta", P)
        sc7 = sb("sc7", W * (CL + NT))
        c7 = sb("c7", 10 * W * 8)
        sel7 = sb("sel7", W * NT)
        one7 = sb("one7", W * NT)
        oneT7 = sb("oneT7", 512, parts=NT)
        h7 = sb("h7", S, parts=COMP)
        comp7 = sb("comp7", 2 * W * 2)
        g7 = sb("g7", W * GRID)
        mag7 = sb("mag7", W)
        y7 = sb("y7", S)
        z7 = sb("z7", S)
        o7 = sb("o7", 2 * S)

        s_x = [sem(f"s_x{b}") for b in range(B)]
        s_c0 = sem("s_c0")
        s_ca = sem("s_ca")
        s_cm = sem("s_cm")
        s_c5 = sem("s_c5")
        s_c7 = sem("s_c7")
        s_set = sem("s_set")
        s_hc = sem("s_hc")
        s_pp = sem("s_pp")
        s_pv = sem("s_pv")
        s_pa = sem("s_pa")
        s_var = sem("s_var")
        s_rstd = sem("s_rstd")
        s_xn = sem("s_xn")
        s_xT = sem("s_xT")
        s_xnT = sem("s_xnT")
        s_q = sem("s_q")
        s_qT = sem("s_qT")
        s_s = sem("s_s")
        s_sub = sem("s_sub")
        s_exp = sem("s_exp")
        s_e = sem("s_e")
        s_eT = sem("s_eT")
        s_o = sem("s_o")
        s_on = sem("s_on")
        s_oP = sem("s_oP")
        s_oT = sem("s_oT")
        s_y = sem("s_y")
        s_res = sem("s_res")
        s_s0, s_sub0, s_exp0, s_p0, s_pP0, s_pT0 = (sem(n) for n in (
            "s_s0", "s_sub0", "s_exp0", "s_p0", "s_pP0", "s_pT0"))
        s_g = sem("s_g")
        s_gsub = sem("s_gsub")
        s_gexp = sem("s_gexp")
        s_gate = sem("s_gate")
        s_gP = sem("s_gP")
        s_gT = sem("s_gT")
        s_all = sem("s_all")
        s_w = {l: [sem(f"s_w{l}_{i}") for i in range(2)] for l in MOE}
        s_h = sem("s_h")
        s_hr = sem("s_hr")
        s_my = sem("s_my")
        s_free = sem("s_free")
        s_h5, s_r5, s_q5 = sem("s_h5"), sem("s_r5"), sem("s_q5")
        s_sc, s_hc7, s_hg7, s_cp7, s_cb7, s_th7 = (sem(n) for n in (
            "s_sc", "s_hc7", "s_hg7", "s_cp7", "s_cb7", "s_th7"))
        s_sg, s_ex, s_oh, s_ohP, s_ohT, s_tb, s_o7 = (sem(n) for n in (
            "s_sg", "s_ex", "s_oh", "s_ohP", "s_ohT", "s_tb", "s_o7"))
        s_out = [sem(f"s_out{i}") for i in range(2)]

        def tile_of(buf, i, n=P):
            return buf[:, i * n:(i + 1) * n]

        def batch_of(b):
            return x[:, bass.ds(b * S, S)]

        res_before = {0: 0, 1: 4, 2: 8, 3: 12, 4: 16, 5: 20, 6: 24}
        att_before = {2: 0, 4: 4, 6: 8}
        moe_before = {1: 0, 3: 4}
        unit_before = {1: 0, 3: 8 * B}
        chunk_before = {1: 0, 3: 8 * B * 4}

        loads = {}

        block = ctx.enter_context(nc.Block())

        @block.sync
        def _(sp):
            def load(s, dst, src):
                sp.dma_start(dst, src).then_inc(s, 16)
                loads[s.name] = loads.get(s.name, 0) + 16

            def rows(src, n=P):
                return src.partition_broadcast(n)

            load(s_c0, ctxT[:, :], A["ctxT"])
            load(s_c0, peT[:, :], A["peT"])
            load(s_c0, ident[:, :], A["ident"])
            load(s_c0, wk0[:, :], A["L0_xattn_Wk"])
            load(s_c0, wv0[:, :], A["L0_xattn_Wv"])
            load(s_c0, wq0T[:, :], A["wq0T"])
            load(s_c0, wo0[:, :], A["wo0"])
            load(s_c0, mask16[:, :], A["mask16"])
            load(s_c0, mask4[:, :], A["mask4"])
            load(s_c0, desc[:, :], A["desc"])
            load(s_c0, bo_row[0][:, :], A["bo0"])
            for b in range(B):
                load(s_x[b], tile_of(x, b, S).rearrange("p (w f) -> p w f", w=W),
                     A["x"][b].rearrange("(w p) f -> p w f", p=P))
            for l in AL:
                load(s_ca, wk[l][:, :], A[f"wk{l}"])
                load(s_ca, wv[l][:, :], A[f"wv{l}"])
                load(s_ca, wq[l][:, :], A[f"wq{l}"])
                load(s_ca, wo[l][:, :], A[f"wo{l}"])
            load(s_ca, bq[:, :], A["bq"])
            load(s_ca, bk[:, :], A["bk"])
            load(s_ca, bv_row[:, :], A["bv"])
            load(s_ca, bo_row[4][:, :], A["bo4"])
            load(s_ca, cap4[:, :], A["cap4"])
            load(s_ca, mask_u8[:, :].rearrange("p (t k) -> p t k", k=SK),
                 A["mask"].rearrange("(t p) k -> p t k", p=P))
            load(s_cm, gw[1][:, :], A["gw1"])
            load(s_cm, gw[3][:, :], A["L1_ffn_gate"])
            load(s_cm, gb[:, :], rows(A["L0_ffn_gate_b"]))
            load(s_cm, eb[:, :], rows(A["L0_ffn_expert_bias"]))
            load(s_cm, b1[1][:, :], A["b1_1"])
            load(s_cm, b1[3][:, :], A["b1_3"])
            load(s_cm, b2[1][:, :], A["L0_ffn_b2"])
            load(s_cm, b2[3][:, :], A["L1_ffn_b2"])
            load(s_c5, wfc[:, :].rearrange("p (c f) -> p c f", c=4),
                 A["L2_ffn_w_fc"].rearrange("(c p) f -> p c f", p=P))
            load(s_c5, wpj[:, :], A["L2_ffn_w_proj"])
            load(s_c5, fbT[:, :], A["fbT"])
            load(s_c5, v5[:, :], A["L2_ffn_v"])
            load(s_c5, u5T[:, :], A["uT"])
            load(s_c5, gate5[:, :], rows(A["gate5"]))
            load(s_c7, raw[:, :], A["rawT"])
            load(s_c7, cw1[:, :], A["L3_ffn_compress_w1"])
            load(s_c7, cb1[:, :], A["cb1"])
            load(s_c7, cw2[:, :], A["L3_ffn_compress_w2"])
            load(s_c7, cb2[:, :], rows(A["L3_ffn_compress_b2"]))
            load(s_c7, table[:, :], A["table"])
            load(s_c7, knots[:, :], rows(A["L3_ffn_knot_values"]))
            load(s_c7, temp[:, 0:1], rows(A["L3_ffn_temperature"]))
            load(s_c7, oscale[:, :], rows(A["L3_ffn_output_scale"]))
            load(s_c7, gamma[:, :], rows(A["L3_ffn_norm_gamma"]))
            load(s_c7, beta[:, :], rows(A["L3_ffn_norm_beta"]))
            for l in MOE:
                E, C = MOE[l]
                w1v = A[f"w1_{l}"].rearrange("e p f -> p e f")
                w2v = A[f"w2_{l}"].rearrange("e p f -> p e f")

                def expert(e, slot):
                    n = C * P
                    sp.dma_start(tile_of(ring1[l], slot, n), w1v[:, bass.ds(e, 1), :].rearrange("p e f -> p (e f)")).then_inc(s_w[l][slot], 16)
                    sp.dma_start(tile_of(ring2[l], slot, n), w2v[:, bass.ds(e, 1), :].rearrange("p e f -> p (e f)")).then_inc(s_w[l][slot], 16)

                expert(0, 0)
                expert(1, 1)
                with sp.Fori(1, E // 2) as i:
                    for slot in range(2):
                        sp.wait_ge(s_my, i * (2 * B) + (unit_before[l] + B * (slot - 1)))
                        expert(i * 2 + slot, slot)
            for b in range(B):
                sp.wait_ge(s_o7, b + 1)
                sp.dma_start(out[b].rearrange("(w p) f -> p w f", p=P),
                             tile_of(o7, b % 2, S).rearrange("p (w f) -> p w f", w=W)).then_inc(s_out[b % 2], 16)
            for i in range(2):
                sp.wait_ge(s_out[i], 32)

        @block.gpsimd
        def _(pool):
            nc.gpsimd.memset(mhalf[:, :], -0.5).then_inc(s_free, 2)
            nc.gpsimd.memset(onerow[:, :], 1.0).then_inc(s_set, 1)
            nc.gpsimd.memset(ones[:, :], 1.0).then_inc(s_res, 1)
            nc.gpsimd.memset(vZ[:, :], 0.0).then_inc(s_set, 1)
            nc.gpsimd.memset(neg3[:, :], NEG3).then_inc(s_set, 1)
            nc.gpsimd.memset(cap6[:, :], BIG).then_inc(s_set, 1)
            pool.wait_ge(s_set, 4)
            pool.wait_ge(s_free, 2)
            pool.wait_ge(s_res, 1)

            def power(n):
                pool.wait_ge(s_var, n + 1)
                nc.gpsimd.tensor_tensor(rstd[:, :], veps[:, :], mhalf[:, :], ALU.pow).then_inc(s_rstd, 1)

            def keep(n, b, l):
                pool.wait_ge(s_xnT, n + 1)
                nc.gpsimd.tensor_copy(xnT_all[:, bass.ds(b * S, S)], xnT[:, :]).then_inc(s_all, 1)

            power(0)
            with pool.Fori(0, B) as b:
                power(b + 1)
            for l in (1, 3):
                with pool.Fori(0, B - 1) as b:
                    keep(b + 4 * l, b, l)
                    power(b + (4 * l + 1))
                keep(4 * l + 3, 3, l)
                power(4 * l + 4)
                with pool.Fori(0, B) as b:
                    power(b + (4 * l + 5))
            with pool.Fori(0, 2 * B) as b:
                power(b + 21)
            with pool.Fori(0, B - 1) as b:
                power(b * 2 + 29)
                power(b * 2 + 30)
            power(35)

        @block.vector
        def _(dve):
            v = nc.vector

            def bn(src, var_n):
                for w in range(W):
                    v.bn_stats(stats[:, w * 6:w * 6 + 6], src(w))
                dve.drain()
                for w in range(W):
                    v.bn_aggr(mv[:, 2 * w:2 * w + 2], stats[:, w * 6:w * 6 + 6])
                dve.drain()
                v.tensor_scalar_add(veps[:, :], mv[:, 1:2 * W:2], EPS).then_inc(s_var, 1)

            def norm(n, b, var_n=None):
                var_n = n if var_n is None else var_n
                dve.drain()
                bn(lambda w: x[:, bass.ds(b * S + w * P, P)], var_n)
                dve.wait_ge(s_rstd, var_n + 1)
                if not (isinstance(n, int) and n == 0):
                    dve.wait_ge(s_xT, n)
                for w in range(W):
                    i = v.tensor_scalar(tile_of(xn, w), x[:, bass.ds(b * S + w * P, P)], mv[:, 2 * w:2 * w + 1],
                                        rstd[:, w:w + 1], ALU.subtract, ALU.mult)
                i.then_inc(s_xn, 1)

            def add_y(layer, b):
                k = res_before[layer]
                dve.wait_ge(s_y, b + (k + 1))
                v.tensor_tensor(batch_of(b), batch_of(b), y_ps[:, :], ALU.add).then_inc(s_res, 1)

            dve.wait_ge(s_c0, loads["s_c0"])
            v.tensor_tensor(hcT[:, :].rearrange("p (b j) -> p b j", b=B), ctxT[:, :].rearrange("p (b j) -> p b j", b=B),
                            peT[:, :].unsqueeze(1).to_broadcast([P, B, SK]), ALU.add)
            v.tensor_copy(ctxR[:, :].rearrange("p (b r j) -> p b r j", b=B, r=HC),
                          ctxT[:, :].rearrange("p (b j) -> p b j", b=B).unsqueeze(2).to_broadcast([P, B, HC, SK])).then_inc(s_hc, 1)
            dve.wait_ge(s_pp, 1)
            v.tensor_copy(kT0[:, :], bank[0][:, :]).then_inc(s_pv, 1)
            dve.wait_ge(s_pp, 2)
            dve.wait_ge(s_set, 4)
            vz = vZ[:, :].rearrange("p (c t h j) -> p c t h j", c=4, t=B * W, h=H0)
            for c in range(4):
                for r in range(2):
                    i = v.tensor_copy(vz[64 * r:64 * r + 64, c, :, 2 * c + r, :],
                                      bank[1][64 * r:64 * r + 64, c * P:(c + 1) * P].rearrange("p (t j) -> p t j", j=KW))
            i.then_inc(s_pv, 1)
            a0 = A0[:, :].rearrange("p (t h j) -> p h t j", h=H0, j=KW)
            for g in range(2):
                dve.wait_ge(s_pp, 3 + g)
                for h in range(4):
                    i = v.tensor_copy(a0[:, 2 * h + g], bank[2 + g][:, h * P:(h + 1) * P].rearrange("p (t j) -> p t j", j=KW))
                i.then_inc(s_pv, 1)
            for g in range(4):
                dve.wait_ge(s_pp, 5 + g)
                v.tensor_copy(VW0[:, g * 512:(g + 1) * 512], bank[4 + g][0:64, :]).then_inc(s_pv, 1)

            dve.wait_ge(s_ca, loads["s_ca"])
            v.copy_predicated(cap6[:, :], mask_u8[:, :], neg3[:, :])
            for i_l, l in enumerate(AL):
                dve.wait_ge(s_pa, i_l + 1)
                for b in range(B):
                    i = v.tensor_tensor(kB[l][:, b * 512:(b + 1) * 512].rearrange("p (h j) -> p h j", h=H),
                                        kT[:, b * SK:(b + 1) * SK].unsqueeze(1).to_broadcast([P, H, SK]),
                                        mask16[:, :].unsqueeze(2).to_broadcast([P, H, SK]), ALU.mult)
                i.then_inc(s_pv, 1)
                dve.wait_ge(s_pp, 10 + 2 * i_l)
                vb = vB[l][:, :].rearrange("p (t c) -> p t c", c=VC)
                v.tensor_tensor(vb[:, :, 0:HC * DH].rearrange("p t (h d) -> p t h d", h=HC),
                                bank[1][:, :].rearrange("p (t h d) -> p t h d", h=HC, d=DH),
                                mask4[:, :].unsqueeze(1).unsqueeze(3).to_broadcast([P, B * 4, HC, DH]), ALU.mult)
                v.tensor_copy(vb[:, :, HC * DH:VC], mask4[:, :].unsqueeze(1).to_broadcast([P, B * 4, HC])).then_inc(s_pv, 1)

            dve.wait_ge(s_c5, loads["s_c5"])

            def ternary(wt, s0, parts):
                n = 512 // parts
                v.scalar_tensor_tensor(ab[:, :], wt[:, :], -1.0, wt[:, :], ALU.mult, ALU.max)
                dve.drain()
                v.tensor_reduce(sc5[:, s0:s0 + parts], ab[:, :].rearrange("p (c f) -> p c f", c=parts), AX_X, ALU.add)
                dve.drain()
                v.tensor_scalar(sc5[:, s0:s0 + parts], sc5[:, s0:s0 + parts], 1.0 / n, 1e-5, ALU.mult, ALU.max)
                dve.drain()
                v.tensor_scalar(sc5[:, 4 + s0:4 + s0 + parts], sc5[:, s0:s0 + parts], 0.5, None, ALU.mult)
                v.tensor_scalar(sc5[:, 8 + s0:8 + s0 + parts], sc5[:, s0:s0 + parts], -0.5, None, ALU.mult)
                dve.drain()
                for c in range(parts):
                    k = s0 + c
                    v.tensor_scalar(ab[:, c * n:(c + 1) * n], wt[:, c * n:(c + 1) * n], sc5[:, 4 + k:5 + k], sc5[:, k:k + 1], ALU.is_gt, ALU.mult)
                    v.tensor_scalar(t5[:, c * n:(c + 1) * n], wt[:, c * n:(c + 1) * n], sc5[:, 8 + k:9 + k], sc5[:, k:k + 1], ALU.is_lt, ALU.mult)
                dve.drain()
                v.tensor_tensor(ab[:, :], ab[:, :], t5[:, :], ALU.subtract).then_inc(s_pv, 1)

            ternary(wfc, 0, 4)
            dve.wait_ge(s_pp, 15)
            v.tensor_copy(wfcT[:, :], bank[0][:, :])
            ternary(wpj, 0, 1)
            dve.wait_ge(s_pp, 16)
            v.tensor_copy(wpjT[:, :], bank[1][:, :])
            dve.wait_ge(s_pp, 17)
            v.tensor_copy(t1[:, :], bank[2][0:16, 0:P]).then_inc(s_pv, 1)
            dve.wait_ge(s_pp, 18)
            v.scalar_tensor_tensor(wfcT[:, :], bank[3][:, :], gate5[:, 0:1], wfcT[:, :], ALU.mult, ALU.add).then_inc(s_pv, 1)

            dve.wait_ge(s_c7, loads["s_c7"])
            v.tensor_scalar(sgq[:, 0:NT], raw[:, :], 0.3, None, ALU.is_gt)
            v.tensor_scalar(sgq[:, NT:2 * NT], raw[:, :], -0.3, None, ALU.is_lt)
            dve.drain()
            v.tensor_tensor(sgq[:, 0:NT], sgq[:, 0:NT], sgq[:, NT:2 * NT], ALU.subtract)
            dve.drain()
            v.tensor_tensor(sgq[:, 0:NT], sgq[:, 0:NT], raw[:, :], ALU.subtract)
            dve.drain()
            sigs = rhs7[:, CL:CL + NT]
            v.tensor_tensor(sigs, raw[:, :], sgq[:, 0:NT], ALU.add)
            dve.drain()
            sv = sigs.rearrange("p (c t) -> p t c", t=TPC)
            v.tensor_tensor(csum[:, 0:CL], sv[:, 0], sv[:, 1], ALU.add)
            for t in range(2, TPC):
                dve.drain()
                v.tensor_tensor(csum[:, 0:CL], csum[:, 0:CL], sv[:, t], ALU.add)
            dve.drain()
            v.tensor_scalar(csum[:, CL:2 * CL], csum[:, 0:CL], 0.0, None, ALU.is_lt)
            v.tensor_scalar(rhs7[:, 0:CL], csum[:, 0:CL], 0.0, None, ALU.is_gt)
            dve.drain()
            v.tensor_tensor(rhs7[:, 0:CL], rhs7[:, 0:CL], csum[:, CL:2 * CL], ALU.subtract)
            v.tensor_tensor(dknots[:, 0:KNOTS - 1], knots[:, 1:KNOTS], knots[:, 0:KNOTS - 1], ALU.subtract)
            v.tensor_scalar(temp[:, 1:2], temp[:, 0:1], 1e-6, None, ALU.add)
            dve.drain()
            v.reciprocal(temp[:, 0:1], temp[:, 1:2])
            dve.drain()
            v.tensor_scalar(temp[:, 1:2], temp[:, 0:1], -1.0, None, ALU.mult).then_inc(s_pv, 1)

            for b in range(B):
                dve.wait_ge(s_x[b], 16)
            norm(0, 0)

            def windows(b):
                s = s_ps[0][:, 0:256].rearrange("p (g j) -> p g j", j=KW)
                e = p0[:, :].rearrange("p (g j) -> p g j", j=KW)
                wide = [P, 32, KW]
                dve.wait_ge(s_s0, b + 1)
                v.tensor_reduce(m0[:, :], s, AX_X, ALU.max)
                dve.drain()
                v.tensor_tensor(e, s, m0[:, :].unsqueeze(2).to_broadcast(wide), ALU.subtract).then_inc(s_sub0, 1)
                norm(b + 1, (b + 1) % B)
                dve.wait_ge(s_exp0, b + 1)
                v.tensor_reduce(m0[:, :], e, AX_X, ALU.add)
                dve.drain()
                v.reciprocal(r0[:, :], m0[:, :])
                dve.drain()
                v.tensor_tensor(e, e, r0[:, :].unsqueeze(2).to_broadcast(wide), ALU.mult).then_inc(s_p0, 1)
                add_y(0, b)

            with dve.Fori(0, B - 1) as b:
                windows(b)

            windows(B - 1)

            def scores(l, n, w):
                t = n * 4 + w
                sp_ = s_ps[w % 2][:, :].rearrange("p (h j) -> p h j", h=H)
                m = mx[:, (w % 2) * H:(w % 2 + 1) * H]
                dve.wait_ge(s_s, t + 1)
                return t, sp_, m

            def max_sub(l, k, b, w):
                t = (b + k) * W + w
                s = s_ps[w % 2][:, :].rearrange("p (h j) -> p h j", h=H)
                m = mx[:, (w % 2) * H:(w % 2 + 1) * H]
                dve.wait_ge(s_s, t + 1)
                if l == 4 and w == 0:
                    v.tensor_tensor(s[0:SK], s[0:SK], cap4[0:SK, :].unsqueeze(1).to_broadcast([SK, H, SK]), ALU.min)
                    dve.drain()
                if l == 6:
                    v.tensor_tensor(s, s, cap6[:, bass.ds((b * W + w) * SK, SK)].unsqueeze(1).to_broadcast([P, H, SK]), ALU.min)
                    dve.drain()
                v.tensor_reduce(m, s, AX_X, ALU.max)
                dve.drain()
                v.tensor_tensor(tile_of(e_sb, w % 2, 512).rearrange("p (h j) -> p h j", h=H), s,
                                m.unsqueeze(2).to_broadcast([P, H, SK]), ALU.subtract).then_inc(s_sub, 1)

            def normalise(l, k, b, w):
                t = (b + k) * W + w
                o = o_ps[w % 2][:, 0:4 * VC].rearrange("p (c v) -> p c v", c=4)
                r = rs[:, (w % 2) * H:(w % 2 + 1) * H].rearrange("p (c h) -> p c h", c=4)
                dve.wait_ge(s_o, t + 1)
                v.reciprocal(r, o[:, :, HC * DH:VC])
                dve.drain()
                v.tensor_tensor(tile_of(on, w).rearrange("p (c h d) -> p c h d", c=4, h=HC),
                                o[:, :, 0:HC * DH].rearrange("p c (h d) -> p c h d", h=HC),
                                r.unsqueeze(3).to_broadcast([P, 4, HC, DH]), ALU.mult).then_inc(s_on, 1)

            def attention(l, b):
                k = att_before[l]
                max_sub(l, k, b, 0)
                max_sub(l, k, b, 1)
                max_sub(l, k, b, 2)
                normalise(l, k, b, 0)
                max_sub(l, k, b, 3)
                normalise(l, k, b, 1)
                norm(b + (4 * l + 1), (b + 1) % B)
                normalise(l, k, b, 2)
                normalise(l, k, b, 3)
                add_y(l, b)

            def first_largest(one, vals, n, red, out_op=None):
                v3 = vals
                e3 = one
                w_ = [P, W, n]
                v.tensor_reduce(red[:, 0:W], v3, AX_X, ALU.max)
                dve.drain()
                v.tensor_tensor(e3, v3, red[:, 0:W].unsqueeze(2).to_broadcast(w_), ALU.is_equal)
                dve.drain()
                v.tensor_tensor(e3, e3, desc[:, 16 - n:16].unsqueeze(1).to_broadcast(w_), ALU.mult)
                dve.drain()
                v.tensor_reduce(red[:, W:2 * W], e3, AX_X, ALU.max)
                dve.drain()
                v.tensor_tensor(e3, e3, red[:, W:2 * W].unsqueeze(2).to_broadcast(w_), ALU.is_equal)
                dve.drain()

            def gating(l, b, more):
                E, C = MOE[l]
                k = moe_before[l]
                w_ = [P, W, E]

                def three(buf):
                    return buf[:, 0:W * E].rearrange("p (w e) -> p w e", w=W)

                logit = q_ps[:, 0:W * E].rearrange("p (w e) -> p w e", w=W)
                gout = gates[l][:, bass.ds(b * (W * E), W * E)].rearrange("p (w e) -> p w e", w=W)
                dve.wait_ge(s_g, b + (k + 1))
                if l == 1:
                    v.tensor_tensor(three(gv), logit, gb[:, :].unsqueeze(1).to_broadcast(w_), ALU.add)
                    dve.drain()
                    v.tensor_tensor(three(gv), three(gv), eb[:, :].unsqueeze(1).to_broadcast(w_), ALU.add)
                    dve.drain()
                    first_largest(three(ge), three(gv), E, gred)
                    v.tensor_copy(gout, three(ge))
                    v.tensor_copy(three(gr), three(ge)).then_inc(s_gate, 1)
                else:
                    v.tensor_reduce(gred[:, 0:W], logit, AX_X, ALU.max)
                    dve.drain()
                    v.tensor_tensor(three(gv), logit, gred[:, 0:W].unsqueeze(2).to_broadcast(w_), ALU.subtract).then_inc(s_gsub, 1)
                    dve.wait_ge(s_gexp, b + 1)
                    v.tensor_reduce(gred[:, 0:W], three(gv), AX_X, ALU.add)
                    dve.drain()
                    v.reciprocal(gred[:, W:2 * W], gred[:, 0:W])
                    dve.drain()
                    v.tensor_tensor(three(gr), three(gv), gred[:, W:2 * W].unsqueeze(2).to_broadcast(w_), ALU.mult)
                    dve.drain()
                    v.tensor_copy(three(gv), three(gr))
                    dve.drain()
                    for k_ in range(3):
                        one = gsel if k_ == 0 else ge
                        first_largest(three(one), three(gv), E, gred)
                        if k_ < 2:
                            v.scalar_tensor_tensor(three(gv), three(one), -2.0, three(gv), ALU.mult, ALU.add)
                        if k_ > 0:
                            v.tensor_tensor(three(gsel), three(gsel), three(ge), ALU.add)
                        dve.drain()
                    v.tensor_tensor(three(gr), three(gr), three(gsel), ALU.mult)
                    dve.drain()
                    v.tensor_reduce(gred[:, 0:W], three(gr), AX_X, ALU.add)
                    dve.drain()
                    v.tensor_scalar(gred[:, W:2 * W], gred[:, 0:W], 1e-12, None, ALU.max)
                    dve.drain()
                    v.reciprocal(gred[:, 0:W], gred[:, W:2 * W])
                    dve.drain()
                    v.tensor_tensor(gout, three(gr), gred[:, 0:W].unsqueeze(2).to_broadcast(w_), ALU.mult)
                    v.tensor_tensor(three(ge), three(gr), gred[:, 0:W].unsqueeze(2).to_broadcast(w_), ALU.mult)
                    dve.drain()
                    v.tensor_copy(three(gr), three(ge)).then_inc(s_gate, 1)
                if more:
                    norm(b + (4 * l + 1), b + 1)
                add_y(l, b)

            def experts(l):
                E, C = MOE[l]
                dve.drain()
                with dve.Fori(0, E) as e:
                    for b in range(B):
                        u = e * B + (unit_before[l] + b)
                        dve.wait_ge(s_my, u + 1)
                        y = bank[6 + b % 2]
                        for w in range(W):
                            xt = x[:, b * S + w * P:b * S + (w + 1) * P]
                            i = v.scalar_tensor_tensor(xt, y[:, w * P:(w + 1) * P],
                                                       gates[l][:, bass.ds(e + (b * W + w) * E, 1)], xt, ALU.mult, ALU.add)
                        i.then_inc(s_free, 1)
                    dve.drain()

            def moe(l):
                with dve.Fori(0, B - 1) as b:
                    gating(l, b, True)
                gating(l, B - 1, False)
                experts(l)
                norm(4 * l + 4, 0)

            dve.wait_ge(s_cm, loads["s_cm"])
            moe(1)
            with dve.Fori(0, B) as b:
                attention(2, b)
            moe(3)
            with dve.Fori(0, B) as b:
                attention(4, b)

            with dve.Fori(0, B) as b:
                for c in range(4):
                    r = tile_of(r5, c % 2, S)
                    dve.wait_ge(s_r5, b * 4 + (c + 1))
                    v.tensor_tensor(tile_of(h_sb, c, S), r, r, ALU.mult).then_inc(s_q5, 1)
                with_b = (b + 1) % B
                norm(b + 21, with_b)
                add_y(5, b)

            with dve.Fori(0, B) as b:
                attention(6, b)

            def c7_(i, n=CL):
                return c7[:, i * W * 8:(i + 1) * W * 8]

            def calibrate(dst, fl):
                idx, low, dif, t = c7_(4), c7_(5), c7_(6), c7_(7)
                v.tensor_scalar(idx, fl, 1.0, None, ALU.is_ge)
                dve.drain()
                for k in range(2, KNOTS - 1):
                    v.scalar_tensor_tensor(idx, fl, float(k), idx, ALU.is_ge, ALU.add)
                    dve.drain()
                v.tensor_tensor(t, fl, idx, ALU.subtract)
                v.tensor_scalar(low, idx, 0.0, knots[:, 0:1], ALU.is_equal, ALU.mult)
                v.tensor_scalar(dif, idx, 0.0, dknots[:, 0:1], ALU.is_equal, ALU.mult)
                for k in range(1, KNOTS - 1):
                    dve.drain()
                    v.tensor_scalar(c7_(8), idx, float(k), knots[:, k:k + 1], ALU.is_equal, ALU.mult)
                    v.tensor_scalar(c7_(9), idx, float(k), dknots[:, k:k + 1], ALU.is_equal, ALU.mult)
                    dve.drain()
                    v.tensor_tensor(low, low, c7_(8), ALU.add)
                    v.tensor_tensor(dif, dif, c7_(9), ALU.add)
                dve.drain()
                v.tensor_tensor(t, t, dif, ALU.mult)
                dve.drain()
                v.tensor_tensor(dst, t, low, ALU.add)
                dve.drain()

            def splines(b, more):
                n_sc = CL + NT
                sc_ps = q_ps[:, 0:W * n_sc]
                dve.wait_ge(s_sc, b + 1)
                v.tensor_scalar(sc7[:, :], sc_ps, temp[:, 1:2], 88.0, ALU.mult, ALU.min).then_inc(s_sg, 1)
                dve.wait_ge(s_ex, b + 1)
                v.tensor_scalar(sc7[:, :], sc7[:, :], 1.0, None, ALU.add)
                dve.drain()
                v.reciprocal(sc7[:, :], sc7[:, :])
                dve.drain()
                v.tensor_scalar(sc7[:, :], sc7[:, :], float(KNOTS - 1), None, ALU.mult)
                dve.drain()
                sc = sc7[:, :].rearrange("p (w n) -> p w n", w=W)
                w8 = [P, W, 8]

                def four(i):
                    return c7_(i).rearrange("p (w n) -> p w n", w=W)

                v.tensor_copy(four(0), sc[:, :, 0:CL])
                dve.drain()
                calibrate(c7_(1), c7_(0))
                first_largest(four(2), four(1), CL, gred)
                sel = sel7[:, :].rearrange("p (w t c) -> p w t c", w=W, t=TPC)
                for w in range(W):
                    v.tensor_tensor(sel[:, w], sc[:, w, CL:].rearrange("p (c t) -> p t c", t=TPC),
                                    four(2)[:, w].unsqueeze(1).to_broadcast([P, TPC, CL]), ALU.mult)
                dve.drain()
                v.tensor_reduce(c7_(0), sel7[:, :].rearrange("p (n c) -> p n c", c=CL), AX_X, ALU.add)
                dve.drain()
                calibrate(c7_(1), c7_(0))
                first_largest(four(3), four(1), TPC, gred)
                for w in range(W):
                    i = v.tensor_tensor(one7[:, w * NT:(w + 1) * NT].rearrange("p (c t) -> p c t", t=TPC),
                                        four(2)[:, w].unsqueeze(2).to_broadcast([P, CL, TPC]),
                                        four(3)[:, w].unsqueeze(1).to_broadcast([P, CL, TPC]), ALU.mult)
                i.then_inc(s_oh, 1)
                cp = comp7[:, 0:2 * W].rearrange("p (w i) -> p w i", w=W)
                dve.wait_ge(s_cp7, b + 1)
                v.tensor_tensor(cp, bank[3][:, 0:2 * W].rearrange("p (w i) -> p w i", w=W),
                                cb2[:, :].unsqueeze(1).to_broadcast([P, W, 2]), ALU.add).then_inc(s_cb7, 1)
                dve.wait_ge(s_th7, b + 1)
                dve.wait_ge(s_tb, b + 1)

                def row(w, a, n):
                    return bank[4 + w // 2][:, (w % 2) * TAB + a:(w % 2) * TAB + a + n]

                def g(w):
                    return g7[:, w * GRID:(w + 1) * GRID]

                def co(w, i):
                    return comp7[:, 2 * W + 2 * w + i:2 * W + 2 * w + i + 1]

                for w in range(W):
                    v.tensor_scalar(g(w), row(w, 0, GRID), co(w, 0), None, ALU.mult)
                dve.drain()
                for w in range(W):
                    v.scalar_tensor_tensor(g(w), row(w, GRID, GRID), co(w, 1), g(w), ALU.mult, ALU.add)
                dve.drain()
                for w in range(W):
                    v.tensor_tensor(g(w), g(w), row(w, 2 * GRID, GRID), ALU.add)
                dve.drain()
                for w in range(W):
                    v.scalar_tensor_tensor(g(w), g(w), 0.0, row(w, 3 * GRID, GRID), ALU.max, ALU.mult)
                dve.drain()
                v.tensor_reduce(mag7[:, :], g7[:, :].rearrange("p (w g) -> p w g", w=W), AX_X, ALU.add)
                dve.drain()
                for w in range(W):
                    v.tensor_scalar(mag7[:, w:w + 1], row(w, 4 * GRID, 1), mag7[:, w:w + 1], oscale[:, 0:1], ALU.add, ALU.mult)
                dve.drain()
                for w in range(W):
                    v.scalar_tensor_tensor(tile_of(y7, w), row(w, 4 * GRID + 1, D), mag7[:, w:w + 1], tile_of(xn, w), ALU.mult, ALU.add)
                dve.drain()
                bn(lambda w: tile_of(y7, w), None)
                dve.wait_ge(s_rstd, b * 2 + 30)
                for w in range(W):
                    v.tensor_scalar(tile_of(y7, w), tile_of(y7, w), mv[:, 2 * w:2 * w + 1], rstd[:, w:w + 1], ALU.subtract, ALU.mult)
                dve.drain()
                if more:
                    norm(b + 29, b + 1, b * 2 + 30)
                wide = [P, W, D]

                def w3(a):
                    return a.rearrange("p (w f) -> p w f", w=W)

                v.tensor_tensor(w3(z7[:, :]), w3(y7[:, :]), gamma[:, :].unsqueeze(1).to_broadcast(wide), ALU.mult)
                dve.drain()
                v.tensor_tensor(w3(z7[:, :]), w3(z7[:, :]), beta[:, :].unsqueeze(1).to_broadcast(wide), ALU.add)
                dve.drain()
                if isinstance(b, int) and b >= 2:
                    dve.wait_ge(s_out[b % 2], 16)
                v.tensor_tensor(tile_of(o7, b % 2, S), z7[:, :], batch_of(b), ALU.add).then_inc(s_o7, 1)

            for b in range(B):
                splines(b, b < B - 1)

        @block.scalar
        def _(act):
            a = nc.scalar

            def copy_xT(n):
                act.wait_ge(s_xT, n + 1)
                a.copy(xnT[:, :], xT_ps[:, :]).then_inc(s_xnT, 1)

            act.wait_ge(s_ca, loads["s_ca"])
            for i, l in enumerate(AL):
                act.wait_ge(s_pp, 9 + 2 * i)
                if i:
                    act.wait_ge(s_pv, 8 + 2 * i - 1)
                if l == 4:
                    a.activation(kT[:, :], bank[0][:, 0:P], ACT.Identity, bias=bk[:, 0:1]).then_inc(s_pa, 1)
                else:
                    a.copy(kT[:, :], bank[0][:, 0:P]).then_inc(s_pa, 1)

            copy_xT(0)

            def windows(b):
                act.wait_ge(s_sub0, b + 1)
                a.activation(p0[:, :], p0[:, :], ACT.Exp, scale=DH0 ** -0.5).then_inc(s_exp0, 1)
                copy_xT(b + 1)
                act.wait_ge(s_pP0, b + 1)
                a.copy(pT0[:, :], e_ps[0][0:64, :]).then_inc(s_pT0, 1)

            with act.Fori(0, B) as b:
                windows(b)

            def attention(l, b):
                n = b + 4 * l
                k = att_before[l]
                scale = 1.0 if l == 2 else DH ** -0.5

                def exp(w):
                    act.wait_ge(s_sub, (b + k) * W + (w + 1))
                    e = tile_of(e_sb, w % 2, 512)
                    a.activation(e, e, ACT.Exp, scale=scale).then_inc(s_exp, 1)

                def copy(w):
                    act.wait_ge(s_e, (b + k) * W + (w + 1))
                    a.copy(tile_of(eT, w % 2, 512), e_ps[w % 2][:, :]).then_inc(s_eT, 1)

                act.wait_ge(s_q, b + (k + 1))
                if l == 4:
                    a.activation(qT[:, :], q_ps[:, :], ACT.Identity, bias=bq[:, 0:1]).then_inc(s_qT, 1)
                else:
                    a.copy(qT[:, :], q_ps[:, :]).then_inc(s_qT, 1)
                exp(0)
                exp(1)
                copy(0)
                exp(2)
                copy(1)
                exp(3)
                copy_xT(n + 1)
                copy(2)
                copy(3)
                act.wait_ge(s_oP, b + (k + 1))
                a.copy(oT[:, :], y_ps[:, :]).then_inc(s_oT, 1)

            def moe(l):
                E, C = MOE[l]
                k = moe_before[l]

                def gating(b, more):
                    if l == 3:
                        act.wait_ge(s_gsub, b + 1)
                        a.activation(gv[:, 0:W * E], gv[:, 0:W * E], ACT.Exp).then_inc(s_gexp, 1)
                    if more:
                        act.wait_ge(s_all, b + (k + 1))
                        copy_xT(b + (4 * l + 1))
                    act.wait_ge(s_gP, b + (k + 1))
                    a.copy(gT[0:E, :], e_ps[0][0:E, :]).then_inc(s_gT, 1)

                with act.Fori(0, B - 1) as b:
                    gating(b, True)
                gating(B - 1, False)
                with act.Fori(0, E) as e:
                    act.drain()
                    a.copy(b1e[:, 0:C], b1[l][:, bass.ds(e * C, C)])
                    act.drain()
                    for b in range(B):
                        for c in range(C):
                            i = e * (B * C) + (chunk_before[l] + b * C + c)
                            act.wait_ge(s_h, i + 1)
                            hb = bank[2 + (b * C + c) % 4]
                            a.activation(h_sb[:, ((b % 2) * 4 + c) * S:((b % 2) * 4 + c + 1) * S], hb[:, :], ACT.Relu,
                                         bias=b1e[:, c:c + 1]).then_inc(s_hr, 1)
                act.wait_ge(s_all, k + 4)
                copy_xT(4 * l + 4)

            def loop_attention(l):
                with act.Fori(0, B) as b:
                    attention(l, b)

            act.wait_ge(s_cm, loads["s_cm"])
            moe(1)
            loop_attention(2)
            moe(3)
            loop_attention(4)
            with act.Fori(0, B) as b:
                for c in range(4):
                    act.wait_ge(s_h5, b * 4 + (c + 1))
                    if c >= 2:
                        act.wait_ge(s_q5, b * 4 + (c - 1))
                    a.activation(tile_of(r5, c % 2, S), bank[2 + c][:, :], ACT.Relu).then_inc(s_r5, 1)
                copy_xT(b + 21)
            loop_attention(6)

            def splines(b, more):
                act.wait_ge(s_sg, b + 1)
                a.activation(sc7[:, :], sc7[:, :], ACT.Exp).then_inc(s_ex, 1)
                act.wait_ge(s_hc7, b + 1)
                a.activation(h7[:, :], bank[2][0:COMP, :], ACT.Gelu, bias=cb1[:, 0:1]).then_inc(s_hg7, 1)
                act.wait_ge(s_ohP, b + 1)
                a.copy(oneT7[:, :], bank[6][0:NT, :]).then_inc(s_ohT, 1)
                act.wait_ge(s_cb7, b + 1)
                a.activation(comp7[:, 2 * W:4 * W], comp7[:, 0:2 * W], ACT.Tanh).then_inc(s_th7, 1)
                if more:
                    copy_xT(b + 29)

            act.wait_ge(s_c7, loads["s_c7"])
            for b in range(B):
                splines(b, b < B - 1)

        @block.tensor
        def _(pe):
            mm = nc.tensor.matmul

            pe.wait_ge(s_c0, loads["s_c0"])
            pe.wait_ge(s_hc, 1)
            for c in range(4):
                i = mm(tile_of(bank[0], c), tile_of(wk0, c), hcT[:, :], start=True, stop=True)
            i.then_inc(s_pp, 1)
            for c in range(4):
                i = mm(tile_of(bank[1], c), tile_of(wv0, c), hcT[:, :], start=True, stop=True)
            i.then_inc(s_pp, 1)
            pe.wait_ge(s_pv, 1)
            for g in range(2):
                r = 64 * g
                for c in range(4):
                    i = mm(tile_of(bank[2 + g], c), wq0T[r:r + 64, c * P:(c + 1) * P], kT0[r:r + 64, c * P:(c + 1) * P],
                           start=True, stop=True)
                i.then_inc(s_pp, 1)
            pe.wait_ge(s_pv, 2)
            vz = vZ[:, :].rearrange("p (c t m) -> p c t m", c=4, t=B * W)
            for t in range(B * W):
                for c in range(4):
                    i = mm(tile_of(bank[4 + t // 4], t % 4)[0:64], vz[:, c, t, :], tile_of(wo0, c), start=(c == 0), stop=(c == 3))
                if t % 4 == 3:
                    i.then_inc(s_pp, 1)
            pe.wait_ge(s_ca, loads["s_ca"])
            for n, l in enumerate(AL):
                if n:
                    pe.wait_ge(s_pa, n)
                mm(bank[0][:, 0:P], wk[l][:, :], ctxT[:, :], start=True, stop=True).then_inc(s_pp, 1)
                if n:
                    pe.wait_ge(s_pv, 8 + 2 * n)
                for b in range(B):
                    i = mm(tile_of(bank[1], b), tile_of(ctxR, b), wv[l][:, :], start=True, stop=(l != 4))
                    if l == 4:
                        i = mm(tile_of(bank[1], b), onerow[0:1, :], bv_row[0:1, :], start=False, stop=True)
                i.then_inc(s_pp, 1)
            pe.wait_ge(s_c5, loads["s_c5"])
            for n in range(2):
                pe.wait_ge(s_pv, 15 + n)
                for c in range(4):
                    i = nc.tensor.transpose(tile_of(bank[n], c), tile_of(ab, c), ident[:, :])
                i.then_inc(s_pp, 1)
            mm(bank[2][0:16, 0:P], fbT[:, :], v5[:, :], start=True, stop=True).then_inc(s_pp, 1)
            pe.wait_ge(s_pv, 17)
            mm(bank[3][:, :], t1[:, :], u5T[:, :], start=True, stop=True).then_inc(s_pp, 1)
            pe.wait_ge(s_pv, 19)

            def transposes(n):
                pe.wait_ge(s_xn, n + 1)
                if not (isinstance(n, int) and n == 0):
                    pe.wait_ge(s_xnT, n)
                for w in range(W):
                    i = nc.tensor.transpose(tile_of(xT_ps, w), tile_of(xn, w), ident[:, :])
                i.then_inc(s_xT, 1)

            def bias_then(layer):
                if layer in bo_row:
                    mm(y_ps[:, :], onerow[0:1, :], bo_row[layer][0:1, :], start=True, stop=False, skip_group_check=True)

            def y_matmul(layer, w, lhsT, rhs, first=True, last=True):
                biased = layer in bo_row
                return mm(tile_of(y_ps, w), lhsT, rhs, start=(first and not biased), stop=last, skip_group_check=biased)

            transposes(0)

            def windows(b):
                pe.wait_ge(s_xnT, b + 1)
                for w in range(W):
                    i = mm(s_ps[0][:, w * 64:(w + 1) * 64], tile_of(xnT, w), A0[:, bass.ds((b * W + w) * 64, 64)], start=True, stop=True)
                i.then_inc(s_s0, 1)
                transposes(b + 1)
                pe.wait_ge(s_res, b + 1)
                pe.wait_ge(s_p0, b + 1)
                bias_then(0)
                for w in range(W):
                    i = nc.tensor.transpose(e_ps[0][0:64, w * P:(w + 1) * P], p0[:, w * 64:(w + 1) * 64], ident[:, :])
                i.then_inc(s_pP0, 1)
                pe.wait_ge(s_pT0, b + 1)
                for w in range(W):
                    i = y_matmul(0, w, pT0[:, w * P:(w + 1) * P], VW0[:, bass.ds((b * W + w) * P, P)])
                i.then_inc(s_y, 1)

            with pe.Fori(0, B) as b:
                windows(b)

            def attention(l, b):
                n = b + 4 * l
                k = att_before[l]

                def s(w):
                    t = (b + k) * W + w
                    mm(s_ps[w % 2][:, :], tile_of(qT, w), kB[l][:, bass.ds(b * 512, 512)], start=True, stop=True).then_inc(s_s, 1)

                def e(w):
                    t = (b + k) * W + w
                    pe.wait_ge(s_exp, t + 1)
                    for c in range(4):
                        i = nc.tensor.transpose(tile_of(e_ps[w % 2], c), e_sb[:, (w % 2) * 512 + c * P:(w % 2) * 512 + (c + 1) * P], ident[:, :])
                    i.then_inc(s_e, 1)

                def o(w):
                    t = (b + k) * W + w
                    pe.wait_ge(s_eT, t + 1)
                    if w >= 2:
                        pe.wait_ge(s_on, t - 1)
                    for c in range(4):
                        i = mm(o_ps[w % 2][:, c * VC:(c + 1) * VC],
                               eT[:, (w % 2) * 512 + c * P:(w % 2) * 512 + (c + 1) * P],
                               vB[l][:, bass.ds((b * 4 + c) * VC, VC)], start=True, stop=True)
                    i.then_inc(s_o, 1)

                pe.wait_ge(s_xnT, n + 1)
                mm(q_ps[:, :], wq[l][:, :], xnT[:, :], start=True, stop=True).then_inc(s_q, 1)
                pe.wait_ge(s_qT, b + (k + 1))
                s(0)
                s(1)
                e(0)
                s(2)
                o(0)
                e(1)
                s(3)
                o(1)
                transposes(n + 1)
                e(2)
                o(2)
                e(3)
                o(3)
                pe.wait_ge(s_on, (b + k + 1) * W)
                pe.wait_ge(s_res, b + (res_before[l] + 1))
                for w in range(W):
                    i = nc.tensor.transpose(tile_of(y_ps, w), tile_of(on, w), ident[:, :])
                i.then_inc(s_oP, 1)
                pe.wait_ge(s_oT, b + (k + 1))
                bias_then(l)
                for w in range(W):
                    i = y_matmul(l, w, tile_of(oT, w), wo[l][:, :])
                i.then_inc(s_y, 1)

            def moe(l):
                E, C = MOE[l]
                k = moe_before[l]

                def gating(b, more):
                    n = b + 4 * l
                    pe.wait_ge(s_xnT, n + 1)
                    for w in range(W):
                        i = mm(q_ps[:, w * E:(w + 1) * E], tile_of(xnT, w), gw[l][:, :], start=True, stop=True)
                    i.then_inc(s_g, 1)
                    if more:
                        transposes(n + 1)
                    pe.wait_ge(s_gate, b + (k + 1))
                    for w in range(W):
                        i = nc.tensor.transpose(e_ps[0][0:E, w * P:(w + 1) * P], gr[:, w * E:(w + 1) * E], ident[:, :])
                    i.then_inc(s_gP, 1)
                    pe.wait_ge(s_gT, b + (k + 1))
                    pe.wait_ge(s_res, b + (res_before[l] + 1))
                    for w in range(W):
                        i = mm(tile_of(y_ps, w), gT[0:E, w * P:(w + 1) * P], b2[l][:, :], start=True, stop=True)
                    i.then_inc(s_y, 1)

                with pe.Fori(0, B - 1) as b:
                    gating(b, True)
                gating(B - 1, False)
                pe.wait_ge(s_all, k + 4)
                pe.wait_ge(s_res, res_before[l] + 5)

                def hidden(e, b, slot, skip_first):
                    for c in range(C):
                        i = e * (B * C) + (chunk_before[l] + b * C + c)
                        if not skip_first:
                            pe.wait_ge(s_hr, i - 3)
                        mm(bank[2 + (b * C + c) % 4][:, :], ring1[l][:, (slot * C + c) * P:(slot * C + c + 1) * P],
                           tile_of(xnT_all, b, S), start=True, stop=True).then_inc(s_h, 1)

                def second(e, b, slot):
                    u = e * B + (unit_before[l] + b)
                    pe.wait_ge(s_hr, e * (B * C) + (chunk_before[l] + (b + 1) * C))
                    pe.wait_ge(s_free, u + 1)
                    for w in range(W):
                        for c in range(C):
                            h0 = ((b % 2) * 4 + c) * S + w * P
                            i = mm(tile_of(bank[6 + b % 2], w), h_sb[:, h0:h0 + P],
                                   ring2[l][:, (slot * C + c) * P:(slot * C + c + 1) * P], start=(c == 0), stop=(c == C - 1))
                    i.then_inc(s_my, 1)

                def pair(i, last):
                    for slot in range(2):
                        e = i * 2 + slot
                        for b in range(B):
                            if b < B - 1:
                                hidden(e, b + 1, slot, False)
                            elif slot == 0:
                                pe.wait_ge(s_w[l][1], i * 32 + 32)
                                hidden(i * 2 + 1, 0, 1, False)
                            elif not last:
                                pe.wait_ge(s_w[l][0], i * 32 + 64)
                                hidden(i * 2 + 2, 0, 0, False)
                            second(e, b, slot)

                pe.wait_ge(s_w[l][0], 32)
                if l == 1:
                    for c in range(C):
                        mm(bank[2 + c][:, :], ring1[l][:, c * P:(c + 1) * P], tile_of(xnT_all, 0, S), start=True, stop=True).then_inc(s_h, 1)
                else:
                    hidden(0, 0, 0, False)
                with pe.Fori(0, E // 2 - 1) as i:
                    pair(i, False)
                pair(E // 2 - 1, True)
                transposes(4 * l + 4)

            def loop_attention(l):
                with pe.Fori(0, B) as b:
                    attention(l, b)

            pe.wait_ge(s_cm, loads["s_cm"])
            moe(1)
            loop_attention(2)
            moe(3)
            loop_attention(4)

            with pe.Fori(0, B) as b:
                pe.wait_ge(s_xnT, b + 21)
                for c in range(4):
                    mm(bank[2 + c][:, :], tile_of(wfcT, c), xnT[:, :], start=True, stop=True).then_inc(s_h5, 1)
                pe.wait_ge(s_res, b + (res_before[5] + 1))
                pe.wait_ge(s_q5, b * 4 + 4)
                for w in range(W):
                    for c in range(4):
                        i = mm(tile_of(y_ps, w), h_sb[:, c * S + w * P:c * S + (w + 1) * P], tile_of(wpjT, c), start=(c == 0), stop=(c == 3))
                i.then_inc(s_y, 1)
                transposes(b + 21)

            loop_attention(6)

            def splines(b, more):
                pe.wait_ge(s_xnT, b + 29)
                n = CL + NT
                if b:
                    pe.wait_ge(s_o7, b)
                for w in range(W):
                    i = mm(q_ps[:, w * n:(w + 1) * n], tile_of(xnT, w), rhs7[:, :], start=True, stop=True)
                i.then_inc(s_sc, 1)
                mm(bank[2][0:COMP, :], cw1[:, :], xnT[:, :], start=True, stop=True).then_inc(s_hc7, 1)
                pe.wait_ge(s_hg7, b + 1)
                for w in range(W):
                    i = mm(bank[3][:, 2 * w:2 * w + 2], h7[:, w * P:(w + 1) * P], cw2[:, :], start=True, stop=True)
                i.then_inc(s_cp7, 1)
                pe.wait_ge(s_oh, b + 1)
                for w in range(W):
                    i = nc.tensor.transpose(bank[6][0:NT, w * P:(w + 1) * P], one7[:, w * NT:(w + 1) * NT], ident[:, :])
                i.then_inc(s_ohP, 1)
                pe.wait_ge(s_ohT, b + 1)
                for w in range(W):
                    i = mm(bank[4 + w // 2][:, (w % 2) * TAB:(w % 2 + 1) * TAB], oneT7[:, w * P:(w + 1) * P], table[:, :], start=True, stop=True)
                i.then_inc(s_tb, 1)
                if more:
                    transposes(b + 29)

            pe.wait_ge(s_c7, loads["s_c7"])
            for b in range(B):
                splines(b, b < B - 1)


def constants(np):
    f = np.float32
    rows = np.arange(P)
    pos = np.arange(SK, dtype=f)[:, None]
    denom = np.power(f(10000.0), f(2.0) * np.arange(D // 2, dtype=f) / f(D))
    ang = pos / denom
    pe = np.zeros((SK, D), f)
    pe[:, 0::2] = np.sin(ang)
    pe[:, 1::2] = np.cos(ang)
    q, k = np.arange(P)[:, None], np.arange(SK)[None, :]
    return {
        "ident": np.eye(P, dtype=f),
        "peT": np.ascontiguousarray(pe.T),
        "mask16": (rows[:, None] // DH == np.arange(H)[None, :]).astype(f),
        "mask4": (rows[:, None] // SK == np.arange(HC)[None, :]).astype(f),
        "desc": np.tile(np.arange(16, 0, -1).astype(f), (P, 1)),
        "cap4": np.where(k > q, f(-BIG), f(BIG)).astype(f),
    }


def kernel(**inputs):
    import numpy as np
    import concourse.bacc as bacc
    from concourse.bass_utils import run_bass_kernel_spmd

    I = {k: np.asarray(v) for k, v in inputs.items()}

    def lay(a):
        return np.ascontiguousarray(a)

    def by_chunk(w):
        return lay(w.reshape(-1, P, w.shape[1]).transpose(1, 0, 2).reshape(P, -1))

    A = constants(np)
    for name in ("x", "L0_xattn_Wk", "L0_xattn_Wv", "L0_ffn_gate_b", "L0_ffn_expert_bias", "L0_ffn_b2", "L1_ffn_b2",
                 "L1_ffn_gate", "L2_ffn_w_fc", "L2_ffn_w_proj", "L2_ffn_v", "L3_ffn_compress_w1", "L3_ffn_compress_w2",
                 "L3_ffn_compress_b2", "L3_ffn_knot_values", "L3_ffn_temperature", "L3_ffn_output_scale",
                 "L3_ffn_norm_gamma", "L3_ffn_norm_beta"):
        A[name] = lay(I[name])
    A["ctxT"] = lay(I["ctx_1024"].reshape(B * SK, D).T)
    A["wq0T"] = by_chunk(I["L0_xattn_Wq"].T)
    A["wo0"] = by_chunk(I["L0_xattn_Wo"])
    A["bo0"] = lay(np.tile(I["L0_xattn_bo"], W)[None])
    for l, name, flip in ((2, "L1", False), (4, "L2", True), (6, "L3", True)):
        for w in "qkvo":
            a = I[f"{name}_xattn_W{w}"]
            A[f"w{w}{l}"] = lay(a.T if flip else a)
    A["bq"] = lay(I["L2_xattn_bq"][:, None])
    A["bk"] = lay(I["L2_xattn_bk"][:, None])
    A["bv"] = lay(I["L2_xattn_bv"][None])
    A["bo4"] = lay(np.tile(I["L2_xattn_bo"], W)[None])
    A["mask"] = lay(I["mask_Bx1xSxS2_bk1"]).reshape(B * S, SK)
    A["gw1"] = lay(I["L0_ffn_gate_w"].T)
    for l, name in ((1, "L0_ffn_"), (3, "L1_ffn_")):
        E, C = MOE[l]
        u = "w" if l == 1 else "W"
        A[f"b1_{l}"] = lay(I[name + "b1"].reshape(E, C, P).transpose(2, 0, 1).reshape(P, E * C))
        A[f"w1_{l}"] = lay(I[name + u + "1"])
        A[f"w2_{l}"] = lay(I[name + u + "2"].reshape(E, C, P, D).transpose(0, 2, 1, 3).reshape(E, P, C * D))
    A["fbT"] = lay(I["L2_ffn_fast_b"].T)
    A["uT"] = lay(I["L2_ffn_u"].T)
    A["gate5"] = lay(I["L2_ffn_gate"].reshape(1))
    A["rawT"] = lay(I["L3_ffn_signatures_raw"].T)
    A["cb1"] = lay(I["L3_ffn_compress_b1"][:, None])
    A["table"] = lay(np.concatenate([I["L3_ffn_spline_w1"].reshape(NT, 2 * GRID), I["L3_ffn_spline_b1"],
                                     I["L3_ffn_spline_w2"].reshape(NT, GRID), I["L3_ffn_spline_b2"],
                                     I["L3_ffn_directions"]], axis=1))

    nc = bacc.Bacc("TRN2", target_bir_lowering=False, num_devices=1)
    handles = {k: nc.dram_tensor(f"in_{k}", a.shape, mybir.dt.from_np(a.dtype), kind="ExternalInput").ap() for k, a in A.items()}
    out = nc.dram_tensor("out_0", (B, S, D), F32, kind="ExternalOutput").ap()
    build(nc, handles, out)
    r = run_bass_kernel_spmd(nc, [{f"in_{k}": a for k, a in A.items()}], core_ids=[0])
    return r.results[0]["out_0"]
```

```python
from contextlib import ExitStack

import concourse.bass as bass
from concourse import mybir

F32 = mybir.dt.float32
F32R = mybir.dt.float32r
U8 = mybir.dt.uint8
ALU = mybir.AluOpType
ACT = mybir.ActivationFunctionType
AX_X = mybir.AxisListType.X

P = 128
B, S, D = 4, 512, 128
W = S // P
SK = 32
H0, DH0, KW = 8, 64, 8
H, DH = 16, 8
HC = 4
VC = HC * DH + HC
EPS = 1e-5
BIG = 3.0e38
MOE = {1: (8, 4), 3: (16, 2)}
NEG3 = -1.0e9 * DH ** 0.5
KNOTS = 8
CL, TPC = 8, 8
NT = CL * TPC
T = B * W
GRID = 16
TAB = 4 * GRID + 1 + D
COMP = 32


def build(nc, A, out):
    ctx = ExitStack()
    with ctx:
        def sb(name, cols, parts=P, dt=F32):
            return ctx.enter_context(nc.sbuf_tensor(name, [parts, cols], dt))

        def sem(name):
            return ctx.enter_context(nc.semaphore(name))

        x = sb("x", B * S)
        bank = [ctx.enter_context(nc.psum_tensor(f"bank{i}", [P, 512], F32)) for i in range(8)]
        xT_ps, s_ps, e_ps, o_ps, y_ps = bank[0], bank[2:4], bank[4:6], [bank[6], bank[1]], bank[7]
        ident = sb("ident", P)
        ones = sb("ones", P)
        onerow = sb("onerow", P, parts=1)
        mask16 = sb("mask16", H)
        mask4 = sb("mask4", HC)
        desc = sb("desc", 16)
        mhalf = sb("mhalf", W)
        stats = sb("stats", W * 6)
        mv = sb("mv", W * 2)
        veps = sb("veps", W)
        rstd = sb("rstd", W)
        xn = sb("xn", S)
        xnT = sb("xnT", S)
        ctxT = sb("ctxT", B * SK)
        peT = sb("peT", SK)
        hcT = sb("hcT", B * SK)
        ctxR = sb("ctxR", B * P)
        wk0, wv0 = sb("wk0", 512), sb("wv0", 512)
        wq0T, wo0 = sb("wq0T", 512), sb("wo0", 512)
        kT0 = sb("kT0", 512)
        vZ = sb("vZ", 4 * 16 * 64)
        A0 = sb("A0", B * 256)
        VW0 = sb("VW0", B * W * P)
        bo_row = {0: sb("bo0", 512, parts=1), 4: sb("bo4", 512, parts=1)}
        m0 = sb("m0", 32)
        r0 = sb("r0", 32)
        AL = (2, 4, 6)
        wq = {l: sb(f"wq{l}", P) for l in AL}
        wk = {l: sb(f"wk{l}", P) for l in AL}
        wv = {l: sb(f"wv{l}", P) for l in AL}
        wo = {l: sb(f"wo{l}", P) for l in AL}
        bq, bk = sb("bq", 1), sb("bk", 1)
        bv_row = sb("bv_row", P, parts=1)
        kT = sb("kT", B * SK)
        kB = sb("kB", B * 512)
        aB = {l: sb(f"aB{l}", B * 512) for l in (2, 6)}
        aB[4] = aB[2]
        cf = VW0[0:1, :]
        chi, clo = sb("chi", B * 512, parts=1, dt=F32R), sb("clo", B * 512, parts=1, dt=F32R)
        oner = sb("oner", P, parts=1, dt=F32R)
        vB = {l: sb(f"vB{l}", B * 4 * VC) for l in AL}
        cap4 = sb("cap4", SK)
        cap6 = sb("cap6", B * W * SK)
        mask_u8 = sb("mask_u8", B * W * SK, dt=U8)
        neg3 = sb("neg3", B * W * SK)
        mx = sb("mx", 2 * H)
        e_sb = sb("e_sb", 2 * 512)
        eT = sb("eT", 2 * 512)
        p0, pT0 = e_sb[:, 0:2 * 256], eT[0:64, :]
        rs = sb("rs", 2 * H)
        on = sb("on", S)
        oT = sb("oT", S)
        xnT_all = sb("xnT_all", B * S)
        gw = {l: sb(f"gw{l}", MOE[l][0]) for l in MOE}
        gb = sb("gb", 8)
        eb = sb("eb", 8)
        b1 = {l: sb(f"b1_{l}", MOE[l][0] * MOE[l][1]) for l in MOE}
        b2 = {l: sb(f"b2_{l}", P, parts=MOE[l][0]) for l in MOE}
        b1e = sb("b1e", 4)
        gates = {l: sb(f"gates{l}", B * W * MOE[l][0]) for l in MOE}
        gv = sb("gv", T * 16)
        ge = sb("ge", T * 16)
        gr = sb("gr", T * 16)
        gsel = sb("gsel", T * 16)
        gred = sb("gred", T * 2)
        gT = sb("gT", 512, parts=16)
        ring1 = {l: sb(f"ring1_{l}", 2 * MOE[l][1] * P) for l in MOE}
        ring2 = {l: sb(f"ring2_{l}", 2 * MOE[l][1] * P) for l in MOE}
        h_sb = sb("h_sb", 2 * 4 * S)
        wfc, wpj = sb("wfc", 512), sb("wpj", 512)
        ab = sb("ab", 512)
        t5 = sb("t5", 512)
        sc5 = sb("sc5", 16)
        wfcT, wpjT = sb("wfcT", 512), sb("wpjT", 512)
        fbT, v5, u5T = sb("fbT", 16, parts=16), sb("v5", P, parts=16), sb("u5T", 512, parts=16)
        t1 = sb("t1", P, parts=16)
        gate5 = sb("gate5", 1)
        r5 = sb("r5", 2 * S)
        raw = sb("raw", NT)
        sgq = sb("sgq", 2 * NT)
        rhs7 = sb("rhs7", CL + NT)
        csum = sb("csum", 2 * CL)
        cw1 = sb("cw1", COMP)
        cb1 = sb("cb1", 1, parts=COMP)
        cw2 = sb("cw2", 2, parts=COMP)
        cb2 = sb("cb2", 2)
        table = sb("table", TAB, parts=NT)
        knots = sb("knots", KNOTS)
        dknots = sb("dknots", KNOTS)
        temp = sb("temp", 2)
        oscale = sb("oscale", 1)
        gamma, beta = sb("gamma", P), sb("beta", P)
        sc7 = aB[4][:, 0:T * (CL + NT)]
        c7 = xnT_all[:, 0:12 * T * 8]
        sel7 = ring1[1][:, 0:T * NT]
        one7 = ring2[1][:, 0:T * NT]
        oneT7 = eT[0:NT, 0:2 * S]
        h7 = e_sb[0:COMP, 0:2 * S]
        comp7 = sb("comp7", T * 2)
        par7 = kB[:, 0:T * (TAB - D)]
        g7 = sb("g7", T * GRID)
        g7b = sb("g7b", T * GRID)
        mag7 = sb("mag7", T)
        y7 = h_sb[:, 0:B * S]
        xb7 = h_sb[:, B * S:2 * B * S]
        xn7 = vZ[:, 0:B * S]

        s_x = [sem(f"s_x{b}") for b in range(B)]
        s_c0 = sem("s_c0")
        s_ca = sem("s_ca")
        s_cm = sem("s_cm")
        s_c5 = sem("s_c5")
        s_c7 = sem("s_c7")
        s_set = sem("s_set")
        s_hc = sem("s_hc")
        s_pp = sem("s_pp")
        s_pv = sem("s_pv")
        s_pa = sem("s_pa")
        s_var = sem("s_var")
        s_rstd = sem("s_rstd")
        s_xn = sem("s_xn")
        s_xT = sem("s_xT")
        s_xnT = sem("s_xnT")
        s_k = sem("s_k")
        s_kT = sem("s_kT")
        s_v = sem("s_v")
        s_vB = sem("s_vB")
        s_kB = sem("s_kB")
        s_a = sem("s_a")
        s_aB = sem("s_aB")
        s_c = sem("s_c")
        s_cf = sem("s_cf")
        s_cr = sem("s_cr")
        s_cap = sem("s_cap")
        s_s = sem("s_s")
        s_sub = sem("s_sub")
        s_exp = sem("s_exp")
        s_e = sem("s_e")
        s_eT = sem("s_eT")
        s_o = sem("s_o")
        s_on = sem("s_on")
        s_oP = sem("s_oP")
        s_oT = sem("s_oT")
        s_y = sem("s_y")
        s_res = sem("s_res")
        s_s0, s_sub0, s_exp0, s_p0, s_pP0, s_pT0 = (sem(n) for n in (
            "s_s0", "s_sub0", "s_exp0", "s_p0", "s_pP0", "s_pT0"))
        s_g = sem("s_g")
        s_gsub = sem("s_gsub")
        s_gexp = sem("s_gexp")
        s_gate = sem("s_gate")
        s_gP = sem("s_gP")
        s_gT = sem("s_gT")
        s_b2 = sem("s_b2")
        s_b2x = sem("s_b2x")
        s_w = {l: [sem(f"s_w{l}_{i}") for i in range(2)] for l in MOE}
        s_h = sem("s_h")
        s_hr = sem("s_hr")
        s_my = sem("s_my")
        s_free = sem("s_free")
        s_h5, s_r5, s_q5 = sem("s_h5"), sem("s_r5"), sem("s_q5")
        s_sc, s_hc7, s_hg7, s_cp7, s_cb7, s_th7 = (sem(n) for n in (
            "s_sc", "s_hc7", "s_hg7", "s_cp7", "s_cb7", "s_th7"))
        s_sg, s_ex, s_oh, s_ohP, s_ohT, s_tb, s_par, s_yd, s_o7 = (sem(n) for n in (
            "s_sg", "s_ex", "s_oh", "s_ohP", "s_ohT", "s_tb", "s_par", "s_yd", "s_o7"))
        s_xb = sem("s_xb")
        s_out = sem("s_out")

        def tile_of(buf, i, n=P):
            return buf[:, i * n:(i + 1) * n]

        def one_bank(b):
            return bank[(0, 1, 6, 7)[b]]

        def table_bank(w):
            return bank[(2, 3, 4, 5, 0, 1, 6, 7)[w // 2]]

        def batch_of(b):
            return x[:, bass.ds(b * S, S)]

        res_before = {0: 0, 2: 4, 4: 8, 5: 12, 6: 16}
        att_before = {2: 0, 4: 4, 6: 8}
        moe_before = {1: 0, 3: 4}
        unit_before = {1: 0, 3: 8 * B}
        chunk_before = {1: 0, 3: 8 * B * 4}

        loads = {}

        block = ctx.enter_context(nc.Block())

        @block.sync
        def _(sp):
            def load(s, dst, src):
                sp.dma_start(dst, src).then_inc(s, 16)
                loads[s.name] = loads.get(s.name, 0) + 16

            def rows(src, n=P):
                return src.partition_broadcast(n)

            load(s_c0, ctxT[:, :], A["ctxT"])
            load(s_c0, peT[:, :], A["peT"])
            load(s_c0, ident[:, :], A["ident"])
            load(s_c0, wk0[:, :], A["L0_xattn_Wk"])
            load(s_c0, wv0[:, :], A["L0_xattn_Wv"])
            load(s_c0, wq0T[:, :], A["wq0T"])
            load(s_c0, wo0[:, :], A["wo0"])
            load(s_c0, mask16[:, :], A["mask16"])
            load(s_c0, mask4[:, :], A["mask4"])
            load(s_c0, desc[:, :], A["desc"])
            load(s_c0, bo_row[0][:, :], A["bo0"])
            for b in range(B):
                load(s_x[b], tile_of(x, b, S).rearrange("p (w f) -> p w f", w=W),
                     A["x"][b].rearrange("(w p) f -> p w f", p=P))
            for l in AL:
                load(s_ca, wk[l][:, :], A[f"wk{l}"])
                load(s_ca, wv[l][:, :], A[f"wv{l}"])
                load(s_ca, wq[l][:, :], A[f"wq{l}"])
                load(s_ca, wo[l][:, :], A[f"wo{l}"])
            load(s_ca, bq[:, :], A["bq"])
            load(s_ca, bk[:, :], A["bk"])
            load(s_ca, bv_row[:, :], A["bv"])
            load(s_ca, bo_row[4][:, :], A["bo4"])
            load(s_ca, cap4[:, :], A["cap4"])
            load(s_ca, mask_u8[:, :].rearrange("p (t k) -> p t k", k=SK),
                 A["mask"].rearrange("(t p) k -> p t k", p=P))
            load(s_cm, gw[1][:, :], A["gw1"])
            load(s_cm, gw[3][:, :], A["L1_ffn_gate"])
            load(s_cm, gb[:, :], rows(A["L0_ffn_gate_b"]))
            load(s_cm, eb[:, :], rows(A["L0_ffn_expert_bias"]))
            load(s_cm, b1[1][:, :], A["b1_1"])
            load(s_cm, b1[3][:, :], A["b1_3"])
            load(s_cm, b2[1][:, :], A["L0_ffn_b2"])
            load(s_cm, b2[3][:, :], A["L1_ffn_b2"])
            load(s_c5, wfc[:, :].rearrange("p (c f) -> p c f", c=4),
                 A["L2_ffn_w_fc"].rearrange("(c p) f -> p c f", p=P))
            load(s_c5, wpj[:, :], A["L2_ffn_w_proj"])
            load(s_c5, fbT[:, :], A["fbT"])
            load(s_c5, v5[:, :], A["L2_ffn_v"])
            load(s_c5, u5T[:, :], A["uT"])
            load(s_c5, gate5[:, :], rows(A["gate5"]))
            load(s_c7, raw[:, :], A["rawT"])
            load(s_c7, cw1[:, :], A["L3_ffn_compress_w1"])
            load(s_c7, cb1[:, :], A["cb1"])
            load(s_c7, cw2[:, :], A["L3_ffn_compress_w2"])
            load(s_c7, cb2[:, :], rows(A["L3_ffn_compress_b2"]))
            load(s_c7, table[:, :], A["table"])
            load(s_c7, knots[:, :], rows(A["L3_ffn_knot_values"]))
            load(s_c7, temp[:, 0:1], rows(A["L3_ffn_temperature"]))
            load(s_c7, oscale[:, :], rows(A["L3_ffn_output_scale"]))
            load(s_c7, gamma[:, :], rows(A["L3_ffn_norm_gamma"]))
            load(s_c7, beta[:, :], rows(A["L3_ffn_norm_beta"]))
            for l in MOE:
                E, C = MOE[l]
                w1v = A[f"w1_{l}"].rearrange("e p f -> p e f")
                w2v = A[f"w2_{l}"].rearrange("e p f -> p e f")

                def expert(e, slot):
                    n = C * P
                    sp.dma_start(tile_of(ring1[l], slot, n), w1v[:, bass.ds(e, 1), :].rearrange("p e f -> p (e f)")).then_inc(s_w[l][slot], 16)
                    sp.dma_start(tile_of(ring2[l], slot, n), w2v[:, bass.ds(e, 1), :].rearrange("p e f -> p (e f)")).then_inc(s_w[l][slot], 16)

                expert(0, 0)
                expert(1, 1)
                with sp.Fori(1, E // 2) as i:
                    for slot in range(2):
                        sp.wait_ge(s_my, i * (2 * B) + (unit_before[l] + B * (slot - 1)))
                        expert(i * 2 + slot, slot)
            for b in range(B):
                sp.wait_ge(s_o7, b + 1)
                sp.dma_start(out[b].rearrange("(w p) f -> p w f", p=P),
                             tile_of(y7, b, S).rearrange("p (w f) -> p w f", w=W)).then_inc(s_out, 16)
            sp.wait_ge(s_out, 16 * B)

        @block.gpsimd
        def _(pool):
            nc.gpsimd.memset(mhalf[:, :], -0.5).then_inc(s_free, 2)
            nc.gpsimd.memset(onerow[:, :], 1.0).then_inc(s_set, 1)
            nc.gpsimd.memset(ones[:, :], 1.0).then_inc(s_res, 1)
            nc.gpsimd.memset(vZ[:, :], 0.0).then_inc(s_set, 1)
            nc.gpsimd.memset(neg3[:, :], NEG3).then_inc(s_set, 1)
            nc.gpsimd.memset(cap6[:, :], BIG).then_inc(s_set, 1)
            pool.wait_ge(s_set, 4)
            pool.wait_ge(s_free, 2)
            pool.wait_ge(s_res, 1)

            def power(n):
                pool.wait_ge(s_var, n + 1)
                nc.gpsimd.tensor_tensor(rstd[:, :], veps[:, :], mhalf[:, :], ALU.pow).then_inc(s_rstd, 1)

            power(0)
            with pool.Fori(1, 8 * B) as n:
                power(n)
            pool.wait_ge(s_c7, loads["s_c7"])
            for b in range(B):
                pool.wait_ge(s_res, 21)
                nc.gpsimd.tensor_tensor(tile_of(xb7, b, S).rearrange("p (w f) -> p w f", w=W),
                                        tile_of(x, b, S).rearrange("p (w f) -> p w f", w=W),
                                        beta[:, :].unsqueeze(1).to_broadcast([P, W, D]), ALU.add).then_inc(s_xb, 1)
            for b in range(B):
                power(32 + b)

        @block.vector
        def _(dve):
            v = nc.vector

            def bn(src):
                for w in range(W):
                    v.bn_stats(stats[:, w * 6:w * 6 + 6], src(w))
                dve.drain()
                for w in range(W):
                    v.bn_aggr(mv[:, 2 * w:2 * w + 2], stats[:, w * 6:w * 6 + 6])
                dve.drain()
                v.tensor_scalar_add(veps[:, :], mv[:, 1:2 * W:2], EPS).then_inc(s_var, 1)

            def stats_of(b):
                dve.drain()
                bn(lambda w: x[:, bass.ds(b * S + w * P, P)])

            def normed(n, b, dst=None):
                dve.wait_ge(s_rstd, n + 1)
                if not (isinstance(n, int) and n == 0):
                    dve.wait_ge(s_xT, n)
                for w in range(W):
                    i = v.tensor_scalar(tile_of(xn if dst is None else dst, w), x[:, bass.ds(b * S + w * P, P)], mv[:, 2 * w:2 * w + 1],
                                        rstd[:, w:w + 1], ALU.subtract, ALU.mult)
                i.then_inc(s_xn, 1)

            def norm(n, b, dst=None):
                stats_of(b)
                normed(n, b, dst)

            def add_y(layer, b):
                k = res_before[layer]
                dve.wait_ge(s_y, b + (k + 1))
                v.tensor_tensor(batch_of(b), batch_of(b), y_ps[:, :], ALU.add).then_inc(s_res, 1)

            dve.wait_ge(s_x[0], 16)
            norm(0, 0)
            dve.wait_ge(s_c0, loads["s_c0"])
            v.tensor_tensor(hcT[:, :].rearrange("p (b j) -> p b j", b=B), ctxT[:, :].rearrange("p (b j) -> p b j", b=B),
                            peT[:, :].unsqueeze(1).to_broadcast([P, B, SK]), ALU.add)
            v.tensor_copy(ctxR[:, :].rearrange("p (b r j) -> p b r j", b=B, r=HC),
                          ctxT[:, :].rearrange("p (b j) -> p b j", b=B).unsqueeze(2).to_broadcast([P, B, HC, SK])).then_inc(s_hc, 1)
            dve.wait_ge(s_pp, 1)
            v.tensor_copy(kT0[:, :], bank[0][:, :]).then_inc(s_pv, 1)
            dve.wait_ge(s_pp, 2)
            dve.wait_ge(s_set, 4)
            vz = vZ[:, :].rearrange("p (c t h j) -> p c t h j", c=4, t=B * W, h=H0)
            for c in range(4):
                for r in range(2):
                    i = v.tensor_copy(vz[64 * r:64 * r + 64, c, :, 2 * c + r, :],
                                      bank[1][64 * r:64 * r + 64, c * P:(c + 1) * P].rearrange("p (t j) -> p t j", j=KW))
            i.then_inc(s_pv, 1)
            a0 = A0[:, :].rearrange("p (t h j) -> p h t j", h=H0, j=KW)
            for g in range(2):
                dve.wait_ge(s_pp, 3 + g)
                for h in range(4):
                    i = v.tensor_copy(a0[:, 2 * h + g], bank[2 + g][:, h * P:(h + 1) * P].rearrange("p (t j) -> p t j", j=KW))
                i.then_inc(s_pv, 1)
            for g in range(4):
                dve.wait_ge(s_pp, 5 + g)
                v.tensor_copy(VW0[0:64, g * 512:(g + 1) * 512], bank[4 + g][0:64, :]).then_inc(s_pv, 1)

            def prepare(l):
                i_l = AL.index(l)
                if l == 2:
                    dve.wait_ge(s_ca, loads["s_ca"])
                dve.wait_ge(s_kT, i_l + 1)
                if l != 2:
                    dve.wait_ge(s_a, 4 * i_l)
                if l == 6:
                    dve.wait_ge(s_c, 4)
                for b in range(B):
                    v.tensor_tensor(kB[:, b * 512:(b + 1) * 512].rearrange("p (h j) -> p h j", h=H),
                                    kT[:, b * SK:(b + 1) * SK].unsqueeze(1).to_broadcast([P, H, SK]),
                                    mask16[:, :].unsqueeze(2).to_broadcast([P, H, SK]), ALU.mult).then_inc(s_kB, 1)
                dve.wait_ge(s_v, i_l + 1)
                vb = vB[l][:, :].rearrange("p (t c) -> p t c", c=VC)
                v.tensor_tensor(vb[:, :, 0:HC * DH].rearrange("p t (h d) -> p t h d", h=HC),
                                bank[1][:, :].rearrange("p (t h d) -> p t h d", h=HC, d=DH),
                                mask4[:, :].unsqueeze(1).unsqueeze(3).to_broadcast([P, B * 4, HC, DH]), ALU.mult)
                v.tensor_copy(vb[:, :, HC * DH:VC], mask4[:, :].unsqueeze(1).to_broadcast([P, B * 4, HC])).then_inc(s_vB, 1)

            def split_c():
                dve.wait_ge(s_cf, 4)
                v.tensor_copy(chi[:, :], cf[:, :])
                v.tensor_copy(oner[:, :], ones[0:1, :])
                dve.drain()
                v.tensor_tensor(clo[:, :], cf[:, :], chi[:, :].bitcast(F32), ALU.subtract).then_inc(s_cr, 1)

            def ternary(wt, s0, parts):
                n = 512 // parts
                v.scalar_tensor_tensor(ab[:, :], wt[:, :], -1.0, wt[:, :], ALU.mult, ALU.max)
                dve.drain()
                v.tensor_reduce(sc5[:, s0:s0 + parts], ab[:, :].rearrange("p (c f) -> p c f", c=parts), AX_X, ALU.add)
                dve.drain()
                v.tensor_scalar(sc5[:, s0:s0 + parts], sc5[:, s0:s0 + parts], 1.0 / n, 1e-5, ALU.mult, ALU.max)
                dve.drain()
                v.tensor_scalar(sc5[:, 4 + s0:4 + s0 + parts], sc5[:, s0:s0 + parts], 0.5, None, ALU.mult)
                v.tensor_scalar(sc5[:, 8 + s0:8 + s0 + parts], sc5[:, s0:s0 + parts], -0.5, None, ALU.mult)
                dve.drain()
                for c in range(parts):
                    k = s0 + c
                    v.tensor_scalar(ab[:, c * n:(c + 1) * n], wt[:, c * n:(c + 1) * n], sc5[:, 4 + k:5 + k], sc5[:, k:k + 1], ALU.is_gt, ALU.mult)
                    v.tensor_scalar(t5[:, c * n:(c + 1) * n], wt[:, c * n:(c + 1) * n], sc5[:, 8 + k:9 + k], sc5[:, k:k + 1], ALU.is_lt, ALU.mult)
                dve.drain()
                v.tensor_tensor(ab[:, :], ab[:, :], t5[:, :], ALU.subtract).then_inc(s_pv, 1)

            def prepare5(stage):
                if stage == 0:
                    dve.wait_ge(s_c5, loads["s_c5"])
                    ternary(wfc, 0, 4)
                elif stage == 1:
                    dve.wait_ge(s_pp, 9)
                    v.tensor_copy(wfcT[:, :], bank[0][:, :])
                    ternary(wpj, 0, 1)
                elif stage == 2:
                    dve.wait_ge(s_pp, 10)
                    v.tensor_copy(wpjT[:, :], bank[1][:, :]).then_inc(s_pv, 1)
                    dve.wait_ge(s_pp, 11)
                    v.tensor_copy(t1[:, :], bank[0][0:16, 0:P]).then_inc(s_pv, 1)
                else:
                    dve.wait_ge(s_pp, 12)
                    v.scalar_tensor_tensor(wfcT[:, :], bank[1][:, :], gate5[:, 0:1], wfcT[:, :], ALU.mult, ALU.add).then_inc(s_pv, 1)

            def prepare7():
                dve.wait_ge(s_c7, loads["s_c7"])
                v.tensor_scalar(sgq[:, 0:NT], raw[:, :], 0.3, None, ALU.is_gt)
                v.tensor_scalar(sgq[:, NT:2 * NT], raw[:, :], -0.3, None, ALU.is_lt)
                dve.drain()
                v.tensor_tensor(sgq[:, 0:NT], sgq[:, 0:NT], sgq[:, NT:2 * NT], ALU.subtract)
                dve.drain()
                v.tensor_tensor(sgq[:, 0:NT], sgq[:, 0:NT], raw[:, :], ALU.subtract)
                dve.drain()
                sigs = rhs7[:, CL:CL + NT]
                v.tensor_tensor(sigs, raw[:, :], sgq[:, 0:NT], ALU.add)
                dve.drain()
                sv = sigs.rearrange("p (c t) -> p t c", t=TPC)
                v.tensor_tensor(csum[:, 0:CL], sv[:, 0], sv[:, 1], ALU.add)
                for t in range(2, TPC):
                    dve.drain()
                    v.tensor_tensor(csum[:, 0:CL], csum[:, 0:CL], sv[:, t], ALU.add)
                dve.drain()
                v.tensor_scalar(csum[:, CL:2 * CL], csum[:, 0:CL], 0.0, None, ALU.is_lt)
                v.tensor_scalar(rhs7[:, 0:CL], csum[:, 0:CL], 0.0, None, ALU.is_gt)
                dve.drain()
                v.tensor_tensor(rhs7[:, 0:CL], rhs7[:, 0:CL], csum[:, CL:2 * CL], ALU.subtract)
                v.tensor_tensor(dknots[:, 0:KNOTS - 1], knots[:, 1:KNOTS], knots[:, 0:KNOTS - 1], ALU.subtract)
                v.tensor_scalar(temp[:, 1:2], temp[:, 0:1], 1e-6, None, ALU.add)
                dve.drain()
                v.reciprocal(temp[:, 0:1], temp[:, 1:2])
                dve.drain()
                v.tensor_scalar(temp[:, 1:2], temp[:, 0:1], -1.0, None, ALU.mult).then_inc(s_pv, 1)

            wide = [P, 32, KW]

            def w_scores(b):
                s = s_ps[b % 2][:, 0:256].rearrange("p (g j) -> p g j", j=KW)
                dve.wait_ge(s_s0, b + 1)
                v.tensor_reduce(m0[:, :], s, AX_X, ALU.max)
                dve.drain()
                v.tensor_tensor(tile_of(p0, b % 2, 256).rearrange("p (g j) -> p g j", j=KW), s,
                                m0[:, :].unsqueeze(2).to_broadcast(wide), ALU.subtract).then_inc(s_sub0, 1)

            def w_probs(b):
                e = tile_of(p0, b % 2, 256).rearrange("p (g j) -> p g j", j=KW)
                dve.wait_ge(s_exp0, b + 1)
                v.tensor_reduce(r0[:, :], e, AX_X, ALU.add)
                dve.drain()
                v.reciprocal(r0[:, :], r0[:, :])
                dve.drain()
                v.tensor_tensor(e, e, r0[:, :].unsqueeze(2).to_broadcast(wide), ALU.mult).then_inc(s_p0, 1)

            for b in range(1, B):
                dve.wait_ge(s_x[b], 16)
            norm(1, 1)
            w_scores(0)
            norm(2, 2)
            w_scores(1)
            w_probs(0)
            norm(3, 3)
            w_scores(2)
            w_probs(1)
            add_y(0, 0)
            w_scores(3)
            w_probs(2)
            norm(4, 0)
            add_y(0, 1)
            w_probs(3)
            norm(5, 1)
            add_y(0, 2)
            norm(6, 2)
            add_y(0, 3)
            norm(7, 3)

            def max_sub(l, k, b, w):
                t = (b + k) * W + w
                s = s_ps[w % 2][:, :].rearrange("p (h j) -> p h j", h=H)
                m = mx[:, (w % 2) * H:(w % 2 + 1) * H]
                dve.wait_ge(s_s, t + 1)
                if l == 4 and w == 0:
                    v.tensor_tensor(s[0:SK], s[0:SK], cap4[0:SK, :].unsqueeze(1).to_broadcast([SK, H, SK]), ALU.min)
                    dve.drain()
                if l == 6:
                    v.tensor_tensor(s, s, cap6[:, bass.ds((b * W + w) * SK, SK)].unsqueeze(1).to_broadcast([P, H, SK]), ALU.min)
                    dve.drain()
                v.tensor_reduce(m, s, AX_X, ALU.max)
                dve.drain()
                v.tensor_tensor(tile_of(e_sb, w % 2, 512).rearrange("p (h j) -> p h j", h=H), s,
                                m.unsqueeze(2).to_broadcast([P, H, SK]), ALU.subtract).then_inc(s_sub, 1)

            def normalise(l, k, b, w):
                t = (b + k) * W + w
                o = o_ps[w % 2][:, 0:4 * VC].rearrange("p (c v) -> p c v", c=4)
                r = rs[:, (w % 2) * H:(w % 2 + 1) * H].rearrange("p (c h) -> p c h", c=4)
                dve.wait_ge(s_o, t + 1)
                v.reciprocal(r, o[:, :, HC * DH:VC])
                dve.drain()
                v.tensor_tensor(tile_of(on, w).rearrange("p (c h d) -> p c h d", c=4, h=HC),
                                o[:, :, 0:HC * DH].rearrange("p c (h d) -> p c h d", h=HC),
                                r.unsqueeze(3).to_broadcast([P, 4, HC, DH]), ALU.mult).then_inc(s_on, 1)

            def attention(l, b, more, dst=None):
                k = att_before[l]
                n = b + 4 * l
                nb = b + 1 if more else 0
                stats_of(nb)
                max_sub(l, k, b, 2)
                normed(n + 1, nb, dst)
                normalise(l, k, b, 0)
                max_sub(l, k, b, 3)
                normalise(l, k, b, 1)
                normalise(l, k, b, 2)
                if more:
                    max_sub(l, k, nb, 0)
                normalise(l, k, b, 3)
                if more:
                    max_sub(l, k, nb, 1)
                add_y(l, b)

            def attention_layer(l, dst=None):
                k = att_before[l]
                max_sub(l, k, 0, 0)
                max_sub(l, k, 0, 1)
                with dve.Fori(0, B - 1) as b:
                    attention(l, b, True)
                attention(l, B - 1, False, dst)

            def first_largest(one, vals, n):
                w_ = [P, T, n]
                most, first = gred[:, 0:T], gred[:, T:2 * T]
                v.tensor_reduce(most, vals, AX_X, ALU.max)
                dve.drain()
                v.tensor_tensor(one, vals, most.unsqueeze(2).to_broadcast(w_), ALU.is_equal)
                dve.drain()
                v.tensor_tensor(one, one, desc[:, 16 - n:16].unsqueeze(1).to_broadcast(w_), ALU.mult)
                dve.drain()
                v.tensor_reduce(first, one, AX_X, ALU.max)
                dve.drain()
                v.tensor_tensor(one, one, first.unsqueeze(2).to_broadcast(w_), ALU.is_equal)
                dve.drain()

            def gating(l):
                E, C = MOE[l]
                w_ = [P, T, E]

                def three(buf):
                    return buf[:, 0:T * E].rearrange("p (w e) -> p w e", w=T)

                logit = three(bank[1])
                gout = three(gates[l])
                dve.wait_ge(s_g, moe_before[l] + B)
                if l == 1:
                    dve.wait_ge(s_cm, loads["s_cm"])
                    v.tensor_tensor(three(gv), logit, gb[:, :].unsqueeze(1).to_broadcast(w_), ALU.add)
                    dve.drain()
                    v.tensor_tensor(three(gv), three(gv), eb[:, :].unsqueeze(1).to_broadcast(w_), ALU.add)
                    dve.drain()
                    first_largest(gout, three(gv), E)
                    v.tensor_copy(three(gr), gout).then_inc(s_gate, 1)
                    return
                most, total = gred[:, 0:T], gred[:, T:2 * T]
                v.tensor_reduce(most, logit, AX_X, ALU.max)
                dve.drain()
                v.tensor_tensor(three(gv), logit, most.unsqueeze(2).to_broadcast(w_), ALU.subtract).then_inc(s_gsub, 1)
                dve.wait_ge(s_gexp, 1)
                v.tensor_reduce(total, three(gv), AX_X, ALU.add)
                dve.drain()
                v.reciprocal(total, total)
                dve.drain()
                v.tensor_tensor(three(gr), three(gv), total.unsqueeze(2).to_broadcast(w_), ALU.mult)
                dve.drain()
                v.tensor_copy(three(gv), three(gr))
                dve.drain()
                for k_ in range(3):
                    one = gsel if k_ == 0 else ge
                    first_largest(three(one), three(gv), E)
                    if k_ < 2:
                        v.scalar_tensor_tensor(three(gv), three(one), -2.0, three(gv), ALU.mult, ALU.add)
                    if k_ > 0:
                        v.tensor_tensor(three(gsel), three(gsel), three(ge), ALU.add)
                    dve.drain()
                v.tensor_tensor(three(gr), three(gr), three(gsel), ALU.mult)
                dve.drain()
                v.tensor_reduce(total, three(gr), AX_X, ALU.add)
                dve.drain()
                v.tensor_scalar(total, total, 1e-12, None, ALU.max)
                dve.drain()
                v.reciprocal(total, total)
                dve.drain()
                v.tensor_tensor(gout, three(gr), total.unsqueeze(2).to_broadcast(w_), ALU.mult)
                dve.drain()
                v.tensor_copy(three(gr), gout).then_inc(s_gate, 1)

            def moe(l):
                E, C = MOE[l]

                def units(e):
                    for b in range(B):
                        u = e * B + (unit_before[l] + b)
                        dve.wait_ge(s_my, u + 1)
                        y = bank[6 + b % 2]
                        for w in range(W):
                            xt = x[:, b * S + w * P:b * S + (w + 1) * P]
                            i = v.scalar_tensor_tensor(xt, y[:, w * P:(w + 1) * P],
                                                       gates[l][:, bass.ds(e + (b * W + w) * E, 1)], xt, ALU.mult, ALU.add)
                        i.then_inc(s_free, 1)
                        yield b
                    dve.drain()

                for e in range(2):
                    for b in units(e):
                        if e == 0:
                            dve.drain()
                            dve.wait_ge(s_b2, moe_before[l] + b + 1)
                            v.tensor_tensor(tile_of(x, b, S), tile_of(x, b, S), bank[1][:, :], ALU.add).then_inc(s_b2x, 1)
                        elif b == 0:
                            prepare(2 if l == 1 else 4)
                        elif b == 3 and l == 3:
                            pass
                with dve.Fori(2, E - 2) as e:
                    for b in units(e):
                        pass
                for e in (E - 2, E - 1):
                    for b in units(e):
                        if e == E - 2:
                            if l == 1:
                                prepare5(b)
                            elif b == 0:
                                split_c()
                                prepare(6)
                        elif b == 1:
                            norm(4 * l + 4, 0)
                        elif b == 2 and l == 1:
                            prepare7()
                        elif b == 2:
                            v.copy_predicated(cap6[:, :], mask_u8[:, :], neg3[:, :])

            gating(1)
            moe(1)
            attention_layer(2)
            for b in range(1, B):
                norm(12 + b, b)
            gating(3)
            moe(3)
            attention_layer(4)

            def squares(b, nb):
                norm(b + 21, nb)
                for c in range(4):
                    r = tile_of(r5, c % 2, S)
                    dve.wait_ge(s_r5, b * 4 + (c + 1))
                    v.tensor_tensor(tile_of(h_sb, c, S), r, r, ALU.mult).then_inc(s_q5, 1)
                add_y(5, b)

            with dve.Fori(0, B - 1) as b:
                squares(b, b + 1)
            squares(B - 1, 0)
            attention_layer(6, dst=tile_of(xn7, 0, S))

            def c7_(i):
                return c7[:, i * T * 8:(i + 1) * T * 8]

            def per_tile(i):
                return c7_(i).rearrange("p (w n) -> p w n", w=T)

            def calibrate(dst, fl):
                idx, low, dif, t = c7_(4), c7_(5), c7_(6), c7_(7)
                v.tensor_scalar(idx, fl, 1.0, None, ALU.is_ge)
                for k in range(2, KNOTS - 1):
                    dve.drain()
                    v.scalar_tensor_tensor(idx, fl, float(k), idx, ALU.is_ge, ALU.add)
                dve.drain()
                v.tensor_tensor(t, fl, idx, ALU.subtract)
                v.tensor_scalar(low, idx, 0.0, knots[:, 0:1], ALU.is_equal, ALU.mult)
                v.tensor_scalar(dif, idx, 0.0, dknots[:, 0:1], ALU.is_equal, ALU.mult)
                for k in range(1, KNOTS - 1):
                    u = 8 + 2 * (k % 2)
                    v.tensor_scalar(c7_(u), idx, float(k), knots[:, k:k + 1], ALU.is_equal, ALU.mult)
                    v.tensor_scalar(c7_(u + 1), idx, float(k), dknots[:, k:k + 1], ALU.is_equal, ALU.mult)
                    dve.drain()
                    v.tensor_tensor(low, low, c7_(u), ALU.add)
                    v.tensor_tensor(dif, dif, c7_(u + 1), ALU.add)
                dve.drain()
                v.tensor_tensor(t, t, dif, ALU.mult)
                dve.drain()
                v.tensor_tensor(dst, t, low, ALU.add)
                dve.drain()

            n_sc = CL + NT

            def scaled(b):
                dve.wait_ge(s_sc, b + 1)
                v.tensor_scalar(tile_of(sc7, b, W * n_sc), s_ps[b % 2][:, 0:W * n_sc], temp[:, 1:2], 88.0, ALU.mult, ALU.min).then_inc(s_sg, 1)

            def sigmoid(b):
                s = tile_of(sc7, b, W * n_sc)
                dve.wait_ge(s_ex, b + 1)
                v.tensor_scalar(s, s, 1.0, None, ALU.add)
                dve.drain()
                v.reciprocal(s, s)
                dve.drain()
                v.tensor_scalar(s, s, float(KNOTS - 1), None, ALU.mult)

            for b in range(B):
                scaled(b)
                if b < B - 1:
                    norm(29 + b, b + 1, dst=tile_of(xn7, b + 1, S))
                sigmoid(b)
            dve.drain()
            sc = sc7[:, :].rearrange("p (w n) -> p w n", w=T)
            v.tensor_copy(per_tile(0), sc[:, :, 0:CL])
            dve.drain()
            calibrate(c7_(1), c7_(0))
            first_largest(per_tile(2), per_tile(1), CL)
            sel = sel7[:, :].rearrange("p (w t c) -> p w t c", w=T, t=TPC)
            for t in range(TPC):
                v.tensor_tensor(sel[:, :, t], sc[:, :, CL:].rearrange("p w (c t) -> p w t c", t=TPC)[:, :, t], per_tile(2), ALU.mult)
            dve.drain()
            v.tensor_reduce(c7_(0), sel7[:, :].rearrange("p (n c) -> p n c", c=CL), AX_X, ALU.add)
            dve.drain()
            calibrate(c7_(1), c7_(0))
            first_largest(per_tile(3), per_tile(1), TPC)
            for b in range(B):
                for w in range(b * W, (b + 1) * W):
                    i = v.tensor_tensor(one7[:, w * NT:(w + 1) * NT].rearrange("p (c t) -> p c t", t=TPC),
                                        per_tile(2)[:, w].unsqueeze(2).to_broadcast([P, CL, TPC]),
                                        per_tile(3)[:, w].unsqueeze(1).to_broadcast([P, CL, TPC]), ALU.mult)
                i.then_inc(s_oh, 1)
            dve.wait_ge(s_cp7, B)
            v.tensor_tensor(comp7[:, :].rearrange("p (w i) -> p w i", w=T), bank[1][:, 0:2 * T].rearrange("p (w i) -> p w i", w=T),
                            cb2[:, :].unsqueeze(1).to_broadcast([P, T, 2]), ALU.add).then_inc(s_cb7, 1)
            dve.wait_ge(s_th7, 1)
            par = par7[:, :].rearrange("p (w n) -> p w n", w=T)
            co = comp7[:, :].rearrange("p (w i) -> p w i", w=T)

            def half(buf, hf, n):
                return buf[:, hf * (T // 2) * n:(hf + 1) * (T // 2) * n].rearrange("p (w n) -> p w n", n=n)

            for hf in range(2):
                ws = slice(hf * T // 2, (hf + 1) * T // 2)
                wide = [P, T // 2, GRID]
                g, g2 = half(g7, hf, GRID), half(g7b, hf, GRID)
                dve.wait_ge(s_par, 4 * hf + 4)
                v.tensor_tensor(g, par[:, ws, 0:GRID], co[:, ws, 0:1].to_broadcast(wide), ALU.mult)
                v.tensor_tensor(g2, par[:, ws, GRID:2 * GRID], co[:, ws, 1:2].to_broadcast(wide), ALU.mult)
                dve.drain()
                v.tensor_tensor(g, g, g2, ALU.add)
                dve.drain()
                v.tensor_tensor(g, g, par[:, ws, 2 * GRID:3 * GRID], ALU.add)
                dve.drain()
                v.scalar_tensor_tensor(g, g, 0.0, par[:, ws, 3 * GRID:4 * GRID], ALU.max, ALU.mult)
                dve.drain()
                m = mag7[:, ws]
                v.tensor_reduce(m, g, AX_X, ALU.add)
                dve.drain()
                v.tensor_tensor(m, m, par[:, ws, 4 * GRID], ALU.add)
                dve.drain()
                v.tensor_scalar(m, m, oscale[:, 0:1], None, ALU.mult)
                dve.drain()
                for w in range(hf * T // 2, (hf + 1) * T // 2):
                    i = v.scalar_tensor_tensor(tile_of(y7, w), table_bank(w)[:, (w % 2) * TAB + TAB - D:(w % 2 + 1) * TAB],
                                               mag7[:, w:w + 1], tile_of(xn7, w), ALU.mult, ALU.add)
            for b in range(B):
                y = tile_of(y7, b, S)
                dve.drain()
                bn(lambda w: tile_of(y, w))
                dve.wait_ge(s_rstd, 33 + b)
                for w in range(W):
                    v.tensor_scalar(tile_of(y, w), tile_of(y, w), mv[:, 2 * w:2 * w + 1], rstd[:, w:w + 1], ALU.subtract, ALU.mult)
                dve.drain()
                y3 = y.rearrange("p (w f) -> p w f", w=W)
                v.tensor_tensor(y3, y3, gamma[:, :].unsqueeze(1).to_broadcast([P, W, D]), ALU.mult)
                dve.drain()
                dve.wait_ge(s_xb, b + 1)
                v.tensor_tensor(y, y, tile_of(xb7, b, S), ALU.add).then_inc(s_o7, 1)

        @block.scalar
        def _(act):
            a = nc.scalar

            def copy_xT(n, dst=None):
                act.wait_ge(s_xT, n + 1)
                a.copy(xnT[:, :] if dst is None else dst, xT_ps[:, :]).then_inc(s_xnT, 1)

            def all_of(b):
                return tile_of(xnT_all, b, S)

            def w_exp(b):
                act.wait_ge(s_sub0, b + 1)
                p = tile_of(p0, b % 2, 256)
                a.activation(p, p, ACT.Exp, scale=DH0 ** -0.5).then_inc(s_exp0, 1)

            def w_copy(b):
                act.wait_ge(s_pP0, b + 1)
                a.copy(tile_of(pT0, b % 2, 512), e_ps[b % 2][0:64, :]).then_inc(s_pT0, 1)

            copy_xT(0, all_of(0))
            copy_xT(1, all_of(1))
            w_exp(0)
            copy_xT(2, all_of(2))
            w_exp(1)
            w_copy(0)
            copy_xT(3, all_of(3))
            w_exp(2)
            w_copy(1)
            w_exp(3)
            w_copy(2)
            copy_xT(4, all_of(0))
            w_copy(3)
            copy_xT(5, all_of(1))
            copy_xT(6, all_of(2))
            copy_xT(7, all_of(3))

            def attention(l, b, more, dst=None):
                n = b + 4 * l
                k = att_before[l]
                nb = b + 1

                copy(l, b, 0)
                exp(l, b, 2)
                copy(l, b, 1)
                copy_xT(n + 1, dst)
                exp(l, b, 3)
                copy(l, b, 2)
                if more:
                    exp(l, nb, 0)
                copy(l, b, 3)
                if more:
                    exp(l, nb, 1)
                act.wait_ge(s_oP, b + (k + 1))
                a.copy(oT[:, :], y_ps[:, :]).then_inc(s_oT, 1)

            def exp(l, b, w):
                act.wait_ge(s_sub, (b + att_before[l]) * W + (w + 1))
                e = tile_of(e_sb, w % 2, 512)
                a.activation(e, e, ACT.Exp, scale=1.0 if l == 2 else DH ** -0.5).then_inc(s_exp, 1)

            def copy(l, b, w):
                act.wait_ge(s_e, (b + att_before[l]) * W + (w + 1))
                a.copy(tile_of(eT, w % 2, 512), e_ps[w % 2][:, :]).then_inc(s_eT, 1)

            def attention_layer(l, dst=None):
                exp(l, 0, 0)
                exp(l, 0, 1)
                with act.Fori(0, B - 1) as b:
                    attention(l, b, True)
                attention(l, B - 1, False, dst)

            def prepare(l, stage):
                i_l = AL.index(l)
                if stage == 0:
                    if l == 2:
                        act.wait_ge(s_ca, loads["s_ca"])
                    act.wait_ge(s_k, i_l + 1)
                    if l == 4:
                        a.activation(kT[:, :], bank[0][:, 0:P], ACT.Identity, bias=bk[:, 0:1]).then_inc(s_kT, 1)
                    else:
                        a.copy(kT[:, :], bank[0][:, 0:P]).then_inc(s_kT, 1)
                elif stage <= B:
                    b = stage - 1
                    act.wait_ge(s_a, 4 * i_l + b + 1)
                    a.copy(aB[l][:, b * 512:(b + 1) * 512], bank[b % 2][:, :]).then_inc(s_aB, 1)
                else:
                    b = stage - 1 - B
                    act.wait_ge(s_c, b + 1)
                    a.copy(cf[:, b * 512:(b + 1) * 512], bank[b % 2][0:1, :]).then_inc(s_cf, 1)

            def moe(l):
                E, C = MOE[l]
                k = moe_before[l]

                def units(e):
                    act.drain()
                    a.copy(b1e[:, 0:C], b1[l][:, bass.ds(e * C, C)])
                    act.drain()
                    for b in range(B):
                        for c in range(C):
                            i = e * (B * C) + (chunk_before[l] + b * C + c)
                            act.wait_ge(s_h, i + 1)
                            hb = bank[2 + (b * C + c) % 4]
                            a.activation(h_sb[:, ((b % 2) * 4 + c) * S:((b % 2) * 4 + c + 1) * S], hb[:, :], ACT.Relu,
                                         bias=b1e[:, c:c + 1]).then_inc(s_hr, 1)
                        yield b

                for e in range(2):
                    for b in units(e):
                        if e == 0 and b > 0:
                            bias(l, b - 1)
                        if e == 1:
                            if b == 0:
                                bias(l, 3)
                                prepare(2 if l == 1 else 4, 0)
                            else:
                                prepare(2 if l == 1 else 4, b)
                                if b == 3:
                                    prepare(2 if l == 1 else 4, 4)
                with act.Fori(2, E - 2) as e:
                    for b in units(e):
                        pass
                for e in (E - 2, E - 1):
                    for b in units(e):
                        if l == 3 and e == E - 2:
                            if b == 0:
                                for stage in range(5, 9):
                                    prepare(4, stage)
                                prepare(6, 0)
                            else:
                                prepare(6, b)
                                if b == 3:
                                    prepare(6, 4)
                copy_xT(4 * l + 4)

            def bias(l, b):
                E = MOE[l][0]
                act.wait_ge(s_gP, moe_before[l] + b + 1)
                a.copy(gT[0:E, :], bank[0][0:E, :]).then_inc(s_gT, 1)

            act.wait_ge(s_cm, loads["s_cm"])
            moe(1)
            attention_layer(2, all_of(0))
            for b in range(1, B):
                copy_xT(12 + b, all_of(b))
            act.wait_ge(s_gsub, 1)
            a.activation(gv[:, :], gv[:, :], ACT.Exp).then_inc(s_gexp, 1)
            moe(3)
            attention_layer(4)
            with act.Fori(0, B) as b:
                for c in range(4):
                    act.wait_ge(s_h5, b * 4 + (c + 1))
                    if c >= 2:
                        act.wait_ge(s_q5, b * 4 + (c - 1))
                    a.activation(tile_of(r5, c % 2, S), bank[2 + c][:, :], ACT.Relu).then_inc(s_r5, 1)
                copy_xT(b + 21)
            attention_layer(6)
            act.wait_ge(s_c7, loads["s_c7"])
            for b in range(B):
                act.wait_ge(s_sg, b + 1)
                e = tile_of(sc7, b, W * (CL + NT))
                a.activation(e, e, ACT.Exp).then_inc(s_ex, 1)
                if b < B - 1:
                    copy_xT(29 + b)
            for b in range(B):
                act.wait_ge(s_hc7, b + 1)
                if b >= 2:
                    act.wait_ge(s_cp7, b - 1)
                a.activation(tile_of(h7, b % 2, S), bank[4 + b][0:COMP, :], ACT.Gelu, bias=cb1[:, 0:1]).then_inc(s_hg7, 1)
            act.wait_ge(s_cb7, 1)
            a.activation(comp7[:, :], comp7[:, :], ACT.Tanh).then_inc(s_th7, 1)
            for b in range(B):
                act.wait_ge(s_ohP, b + 1)
                a.copy(tile_of(oneT7, b % 2, S), one_bank(b)[0:NT, :]).then_inc(s_ohT, 1)
                for w in range(2 * b, 2 * b + 2):
                    act.wait_ge(s_tb, w + 1)
                    a.copy(par7[:, 2 * w * (TAB - D):(2 * w + 2) * (TAB - D)].rearrange("p (w n) -> p w n", w=2),
                           table_bank(2 * w)[:, 0:2 * TAB].rearrange("p (w n) -> p w n", w=2)[:, :, 0:TAB - D]).then_inc(s_par, 1)

        @block.tensor
        def _(pe):
            mm = nc.tensor.matmul

            pe.wait_ge(s_c0, loads["s_c0"])
            pe.wait_ge(s_hc, 1)
            for c in range(4):
                i = mm(tile_of(bank[0], c), tile_of(wk0, c), hcT[:, :], start=True, stop=True)
            i.then_inc(s_pp, 1)
            for c in range(4):
                i = mm(tile_of(bank[1], c), tile_of(wv0, c), hcT[:, :], start=True, stop=True)
            i.then_inc(s_pp, 1)
            pe.wait_ge(s_pv, 1)
            for g in range(2):
                r = 64 * g
                for c in range(4):
                    i = mm(tile_of(bank[2 + g], c), wq0T[r:r + 64, c * P:(c + 1) * P], kT0[r:r + 64, c * P:(c + 1) * P],
                           start=True, stop=True)
                i.then_inc(s_pp, 1)
            pe.wait_ge(s_pv, 2)
            vz = vZ[:, :].rearrange("p (c t m) -> p c t m", c=4, t=B * W)
            for t in range(B * W):
                for c in range(4):
                    i = mm(tile_of(bank[4 + t // 4], t % 4)[0:64], vz[:, c, t, :], tile_of(wo0, c), start=(c == 0), stop=(c == 3))
                if t % 4 == 3:
                    i.then_inc(s_pp, 1)
            def transposes(n, src=None):
                pe.wait_ge(s_xn, n + 1)
                if not (isinstance(n, int) and n == 0):
                    pe.wait_ge(s_xnT, n)
                for w in range(W):
                    i = nc.tensor.transpose(tile_of(xT_ps, w), tile_of(xn if src is None else src, w), ident[:, :])
                i.then_inc(s_xT, 1)

            def bias_then(layer):
                if layer in bo_row:
                    mm(y_ps[:, :], onerow[0:1, :], bo_row[layer][0:1, :], start=True, stop=False, skip_group_check=True)

            def y_matmul(layer, w, lhsT, rhs, first=True, last=True):
                biased = layer in bo_row
                return mm(tile_of(y_ps, w), lhsT, rhs, start=(first and not biased), stop=last, skip_group_check=biased)

            def w_scores(b):
                pe.wait_ge(s_xnT, b + 1)
                for w in range(W):
                    i = mm(s_ps[b % 2][:, w * 64:(w + 1) * 64], tile_of(xnT_all, b * W + w), A0[:, (b * W + w) * 64:(b * W + w + 1) * 64], start=True, stop=True)
                i.then_inc(s_s0, 1)

            def w_turn(b):
                pe.wait_ge(s_p0, b + 1)
                for w in range(W):
                    i = nc.tensor.transpose(e_ps[b % 2][0:64, w * P:(w + 1) * P], p0[:, (b % 2) * 256 + w * 64:(b % 2) * 256 + (w + 1) * 64], ident[:, :])
                i.then_inc(s_pP0, 1)

            def w_out(b):
                pe.wait_ge(s_res, b + 1)
                bias_then(0)
                pe.wait_ge(s_pT0, b + 1)
                for w in range(W):
                    i = y_matmul(0, w, pT0[:, (b % 2) * 512 + w * P:(b % 2) * 512 + (w + 1) * P], VW0[0:64, (b * W + w) * P:(b * W + w + 1) * P])
                i.then_inc(s_y, 1)

            def logits(l, b):
                E = MOE[l][0]
                pe.wait_ge(s_xnT, 4 * l + b + 1)
                for t in range(b * W, (b + 1) * W):
                    i = mm(bank[1][:, t * E:(t + 1) * E], tile_of(xnT_all, t), gw[l][:, :], start=True, stop=True)
                i.then_inc(s_g, 1)

            pe.wait_ge(s_pv, 8)
            transposes(0)
            transposes(1)
            w_scores(0)
            transposes(2)
            w_scores(1)
            w_turn(0)
            transposes(3)
            w_scores(2)
            w_turn(1)
            w_out(0)
            w_scores(3)
            w_turn(2)
            w_out(1)
            transposes(4)
            w_turn(3)
            w_out(2)
            transposes(5)
            pe.wait_ge(s_cm, loads["s_cm"])
            logits(1, 0)
            w_out(3)
            transposes(6)
            logits(1, 1)
            transposes(7)
            logits(1, 2)
            logits(1, 3)

            def scores(l, b, w):
                split = l == 4
                i = mm(s_ps[w % 2][:, :], tile_of(xnT, w), aB[l][:, bass.ds(b * 512, 512)], start=True, stop=not split)
                if split:
                    mm(s_ps[w % 2][:, :], oner[0:1, :], chi[0:1, bass.ds(b * 512, 512)], start=False, stop=False)
                    i = mm(s_ps[w % 2][:, :], oner[0:1, :], clo[0:1, bass.ds(b * 512, 512)], start=False, stop=True)
                i.then_inc(s_s, 1)

            def attention(l, b, more, src=None):
                n = b + 4 * l
                k = att_before[l]

                def e(w):
                    t = (b + k) * W + w
                    pe.wait_ge(s_exp, t + 1)
                    for c in range(4):
                        i = nc.tensor.transpose(tile_of(e_ps[w % 2], c), e_sb[:, (w % 2) * 512 + c * P:(w % 2) * 512 + (c + 1) * P], ident[:, :])
                    i.then_inc(s_e, 1)

                def o(w):
                    t = (b + k) * W + w
                    pe.wait_ge(s_eT, t + 1)
                    if w >= 2:
                        pe.wait_ge(s_on, t - 1)
                    for c in range(4):
                        i = mm(o_ps[w % 2][:, c * VC:(c + 1) * VC],
                               eT[:, (w % 2) * 512 + c * P:(w % 2) * 512 + (c + 1) * P],
                               vB[l][:, bass.ds((b * 4 + c) * VC, VC)], start=True, stop=True)
                    i.then_inc(s_o, 1)

                e(0)
                scores(l, b, 2)
                e(1)
                o(0)
                scores(l, b, 3)
                o(1)
                transposes(n + 1, src)
                e(2)
                o(2)
                e(3)
                if more:
                    pe.wait_ge(s_xnT, n + 2)
                    scores(l, b + 1, 0)
                o(3)
                if more:
                    scores(l, b + 1, 1)
                pe.wait_ge(s_on, (b + k + 1) * W)
                pe.wait_ge(s_res, b + (res_before[l] + 1))
                for w in range(W):
                    i = nc.tensor.transpose(tile_of(y_ps, w), tile_of(on, w), ident[:, :])
                i.then_inc(s_oP, 1)
                pe.wait_ge(s_oT, b + (k + 1))
                bias_then(l)
                for w in range(W):
                    i = y_matmul(l, w, tile_of(oT, w), wo[l][:, :])
                i.then_inc(s_y, 1)

            def attention_layer(l, src=None):
                i_l = AL.index(l)
                pe.wait_ge(s_aB, 4 * i_l + 4)
                if l == 4:
                    pe.wait_ge(s_cr, 1)
                pe.wait_ge(s_xnT, 4 * l + 1)
                scores(l, 0, 0)
                scores(l, 0, 1)
                with pe.Fori(0, B - 1) as b:
                    attention(l, b, True)
                attention(l, B - 1, False, src)

            def prepare(l, stage):
                i_l = AL.index(l)
                if stage == 0:
                    if l == 2:
                        pe.wait_ge(s_ca, loads["s_ca"])
                    mm(bank[0][:, 0:P], wk[l][:, :], ctxT[:, :], start=True, stop=True).then_inc(s_k, 1)
                    for b in range(B):
                        i = mm(tile_of(bank[1], b), tile_of(ctxR, b), wv[l][:, :], start=True, stop=(l != 4), skip_group_check=(l == 4))
                        if l == 4:
                            i = mm(tile_of(bank[1], b), onerow[0:1, :], bv_row[0:1, :], start=False, stop=True, skip_group_check=True)
                    i.then_inc(s_v, 1)
                elif stage <= B:
                    b = stage - 1
                    pe.wait_ge(s_kB, 4 * i_l + b + 1)
                    if b == 1:
                        pe.wait_ge(s_vB, i_l + 1)
                    elif b > 1:
                        pe.wait_ge(s_aB, 4 * i_l + b - 1)
                    mm(bank[b % 2][:, :], wq[l][:, :], kB[:, b * 512:(b + 1) * 512], start=True, stop=True).then_inc(s_a, 1)
                else:
                    b = stage - 1 - B
                    if b < 2:
                        pe.wait_ge(s_aB, 4 * i_l + 3 + b)
                    else:
                        pe.wait_ge(s_cf, b - 1)
                    mm(bank[b % 2][0:1, :], bq[:, 0:1], kB[:, b * 512:(b + 1) * 512], start=True, stop=True).then_inc(s_c, 1)

            def prepare5(stage):
                if stage < 2:
                    if stage == 0:
                        pe.wait_ge(s_c5, loads["s_c5"])
                        pe.wait_ge(s_aB, 4)
                    pe.wait_ge(s_pv, 9 + stage)
                    for c in range(4):
                        i = nc.tensor.transpose(tile_of(bank[stage], c), tile_of(ab, c), ident[:, :])
                    i.then_inc(s_pp, 1)
                    if stage == 1:
                        mm(bank[0][0:16, 0:P], fbT[:, :], v5[:, :], start=True, stop=True).then_inc(s_pp, 1)
                else:
                    pe.wait_ge(s_pv, 12)
                    mm(bank[1][:, :], t1[:, :], u5T[:, :], start=True, stop=True).then_inc(s_pp, 1)

            def moe(l):
                E, C = MOE[l]
                k = moe_before[l]

                def hidden(e, b, slot, waits=True):
                    for c in range(C):
                        i = e * (B * C) + (chunk_before[l] + b * C + c)
                        if waits:
                            pe.wait_ge(s_hr, i - 3)
                        mm(bank[2 + (b * C + c) % 4][:, :], ring1[l][:, (slot * C + c) * P:(slot * C + c + 1) * P],
                           tile_of(xnT_all, b, S), start=True, stop=True).then_inc(s_h, 1)

                def second(e, b, slot):
                    u = e * B + (unit_before[l] + b)
                    pe.wait_ge(s_hr, e * (B * C) + (chunk_before[l] + (b + 1) * C))
                    pe.wait_ge(s_free, u + 1)
                    for w in range(W):
                        for c in range(C):
                            h0 = ((b % 2) * 4 + c) * S + w * P
                            i = mm(tile_of(bank[6 + b % 2], w), h_sb[:, h0:h0 + P],
                                   ring2[l][:, (slot * C + c) * P:(slot * C + c + 1) * P], start=(c == 0), stop=(c == C - 1))
                    i.then_inc(s_my, 1)

                def pair(i, extra, last=False):
                    for slot in range(2):
                        e = i * 2 + slot
                        for b in range(B):
                            if b < B - 1:
                                hidden(e, b + 1, slot)
                            elif slot == 0:
                                pe.wait_ge(s_w[l][1], i * 32 + 32)
                                hidden(i * 2 + 1, 0, 1)
                            elif not last:
                                pe.wait_ge(s_w[l][0], i * 32 + 64)
                                hidden(i * 2 + 2, 0, 0)
                            second(e, b, slot)
                            extra(slot, b)

                def bias(b):
                    pe.wait_ge(s_gT, k + b + 1)
                    if b:
                        pe.wait_ge(s_b2x, k + b)
                    for w in range(W):
                        i = mm(tile_of(bank[1], w), gT[0:E, w * P:(w + 1) * P], b2[l][:, :], start=True, stop=True)
                    i.then_inc(s_b2, 1)

                def turn(b):
                    if b == 0:
                        pe.wait_ge(s_gate, 1 if l == 1 else 2)
                    for w in range(W):
                        t = b * W + w
                        i = nc.tensor.transpose(bank[0][0:E, w * P:(w + 1) * P], gr[:, t * E:(t + 1) * E], ident[:, :])
                    i.then_inc(s_gP, 1)

                def first(slot, b):
                    if slot == 0:
                        if b:
                            bias(b - 1)
                        turn(b)
                    else:
                        if b == 0:
                            bias(3)
                            pe.wait_ge(s_b2x, k + 4)
                            prepare(2 if l == 1 else 4, 0)
                        else:
                            prepare(2 if l == 1 else 4, b)
                            if b == 3:
                                prepare(2 if l == 1 else 4, 4)

                def final(slot, b):
                    if slot == 0:
                        if l == 1:
                            if b < 3:
                                prepare5(b)
                        elif b == 0:
                            for stage in range(5, 9):
                                prepare(4, stage)
                            pe.wait_ge(s_cf, 4)
                            prepare(6, 0)
                        else:
                            prepare(6, b)
                            if b == 3:
                                prepare(6, 4)

                pe.wait_ge(s_w[l][0], 32)
                hidden(0, 0, 0, waits=(l == 3))
                pair(0, first)
                if E // 2 > 2:
                    with pe.Fori(1, E // 2 - 1) as i:
                        pair(i, lambda slot, b: None)
                pair(E // 2 - 1, final, last=True)
                if l == 1:
                    pe.wait_ge(s_pv, 13)
                else:
                    pe.wait_ge(s_aB, 12)
                transposes(4 * l + 4)

            moe(1)
            attention_layer(2)
            for b in range(1, B):
                logits(3, b - 1)
                transposes(12 + b)
            logits(3, 3)
            moe(3)
            attention_layer(4)

            with pe.Fori(0, B) as b:
                pe.wait_ge(s_xnT, b + 21)
                for c in range(4):
                    mm(bank[2 + c][:, :], tile_of(wfcT, c), xnT[:, :], start=True, stop=True).then_inc(s_h5, 1)
                transposes(b + 21)
                pe.wait_ge(s_res, b + (res_before[5] + 1))
                pe.wait_ge(s_q5, b * 4 + 4)
                for w in range(W):
                    for c in range(4):
                        i = mm(tile_of(y_ps, w), h_sb[:, c * S + w * P:c * S + (w + 1) * P], tile_of(wpjT, c), start=(c == 0), stop=(c == 3))
                i.then_inc(s_y, 1)

            attention_layer(6, tile_of(xn7, 0, S))

            pe.wait_ge(s_c7, loads["s_c7"])
            n = CL + NT
            for b in range(B):
                pe.wait_ge(s_xnT, b + 29)
                if b >= 2:
                    pe.wait_ge(s_sg, b - 1)
                for w in range(W):
                    i = mm(s_ps[b % 2][:, w * n:(w + 1) * n], tile_of(xnT, w), rhs7[:, :], start=True, stop=True)
                i.then_inc(s_sc, 1)
                if b == B - 1:
                    pe.wait_ge(s_res, 21)
                mm(bank[4 + b][0:COMP, :], cw1[:, :], xnT[:, :], start=True, stop=True).then_inc(s_hc7, 1)
                if b < B - 1:
                    transposes(29 + b, tile_of(xn7, b + 1, S))
            for b in range(B):
                pe.wait_ge(s_hg7, b + 1)
                for w in range(W):
                    t = b * W + w
                    i = mm(bank[1][:, 2 * t:2 * t + 2], h7[:, (b % 2) * S + w * P:(b % 2) * S + (w + 1) * P], cw2[:, :], start=True, stop=True)
                i.then_inc(s_cp7, 1)
            for b in range(B):
                pe.wait_ge(s_oh, b + 1)
                if b == 1:
                    pe.wait_ge(s_cb7, 1)
                for w in range(W):
                    t = b * W + w
                    i = nc.tensor.transpose(one_bank(b)[0:NT, w * P:(w + 1) * P], one7[:, t * NT:(t + 1) * NT], ident[:, :])
                i.then_inc(s_ohP, 1)
            for b in range(B):
                pe.wait_ge(s_ohT, b + 1)
                for w in range(W):
                    t = b * W + w
                    i = mm(table_bank(t)[:, (t % 2) * TAB:(t % 2 + 1) * TAB], oneT7[:, (b % 2) * S + w * P:(b % 2) * S + (w + 1) * P], table[:, :], start=True, stop=True)
                    if w % 2:
                        i.then_inc(s_tb, 1)


def constants(np):
    f = np.float32
    rows = np.arange(P)
    pos = np.arange(SK, dtype=f)[:, None]
    denom = np.power(f(10000.0), f(2.0) * np.arange(D // 2, dtype=f) / f(D))
    ang = pos / denom
    pe = np.zeros((SK, D), f)
    pe[:, 0::2] = np.sin(ang)
    pe[:, 1::2] = np.cos(ang)
    q, k = np.arange(P)[:, None], np.arange(SK)[None, :]
    return {
        "ident": np.eye(P, dtype=f),
        "peT": np.ascontiguousarray(pe.T),
        "mask16": (rows[:, None] // DH == np.arange(H)[None, :]).astype(f),
        "mask4": (rows[:, None] // SK == np.arange(HC)[None, :]).astype(f),
        "desc": np.tile(np.arange(16, 0, -1).astype(f), (P, 1)),
        "cap4": np.where(k > q, f(-BIG), f(BIG)).astype(f),
    }


def kernel(**inputs):
    import numpy as np
    import concourse.bacc as bacc
    from concourse.bass_utils import run_bass_kernel_spmd

    I = {k: np.asarray(v) for k, v in inputs.items()}

    def lay(a):
        return np.ascontiguousarray(a)

    def by_chunk(w):
        return lay(w.reshape(-1, P, w.shape[1]).transpose(1, 0, 2).reshape(P, -1))

    A = constants(np)
    for name in ("x", "L0_xattn_Wk", "L0_xattn_Wv", "L0_ffn_gate_b", "L0_ffn_expert_bias", "L0_ffn_b2", "L1_ffn_b2",
                 "L1_ffn_gate", "L2_ffn_w_fc", "L2_ffn_w_proj", "L2_ffn_v", "L3_ffn_compress_w1", "L3_ffn_compress_w2",
                 "L3_ffn_compress_b2", "L3_ffn_knot_values", "L3_ffn_temperature", "L3_ffn_output_scale",
                 "L3_ffn_norm_gamma", "L3_ffn_norm_beta"):
        A[name] = lay(I[name])
    A["ctxT"] = lay(I["ctx_1024"].reshape(B * SK, D).T)
    A["wq0T"] = by_chunk(I["L0_xattn_Wq"].T)
    A["wo0"] = by_chunk(I["L0_xattn_Wo"])
    A["bo0"] = lay(np.tile(I["L0_xattn_bo"], W)[None])
    for l, name, flip in ((2, "L1", False), (4, "L2", True), (6, "L3", True)):
        for w in "qkvo":
            a = I[f"{name}_xattn_W{w}"]
            A[f"w{w}{l}"] = lay(a.T if flip != (w == "q") else a)
    A["bq"] = lay(I["L2_xattn_bq"][:, None])
    A["bk"] = lay(I["L2_xattn_bk"][:, None])
    A["bv"] = lay(I["L2_xattn_bv"][None])
    A["bo4"] = lay(np.tile(I["L2_xattn_bo"], W)[None])
    A["mask"] = lay(I["mask_Bx1xSxS2_bk1"]).reshape(B * S, SK)
    A["gw1"] = lay(I["L0_ffn_gate_w"].T)
    for l, name in ((1, "L0_ffn_"), (3, "L1_ffn_")):
        E, C = MOE[l]
        u = "w" if l == 1 else "W"
        A[f"b1_{l}"] = lay(I[name + "b1"].reshape(E, C, P).transpose(2, 0, 1).reshape(P, E * C))
        A[f"w1_{l}"] = lay(I[name + u + "1"])
        A[f"w2_{l}"] = lay(I[name + u + "2"].reshape(E, C, P, D).transpose(0, 2, 1, 3).reshape(E, P, C * D))
    A["fbT"] = lay(I["L2_ffn_fast_b"].T)
    A["uT"] = lay(I["L2_ffn_u"].T)
    A["gate5"] = lay(I["L2_ffn_gate"].reshape(1))
    A["rawT"] = lay(I["L3_ffn_signatures_raw"].T)
    A["cb1"] = lay(I["L3_ffn_compress_b1"][:, None])
    A["table"] = lay(np.concatenate([I["L3_ffn_spline_w1"].reshape(NT, 2 * GRID), I["L3_ffn_spline_b1"],
                                     I["L3_ffn_spline_w2"].reshape(NT, GRID), I["L3_ffn_spline_b2"],
                                     I["L3_ffn_directions"]], axis=1))

    nc = bacc.Bacc("TRN2", target_bir_lowering=False, num_devices=1)
    handles = {k: nc.dram_tensor(f"in_{k}", a.shape, mybir.dt.from_np(a.dtype), kind="ExternalInput").ap() for k, a in A.items()}
    out = nc.dram_tensor("out_0", (B, S, D), F32, kind="ExternalOutput").ap()
    build(nc, handles, out)
    r = run_bass_kernel_spmd(nc, [{f"in_{k}": a for k, a in A.items()}], core_ids=[0])
    return r.results[0]["out_0"]
```

```python
from contextlib import ExitStack

import concourse.bass as bass
from concourse import mybir

F32 = mybir.dt.float32
F32R = mybir.dt.float32r
U8 = mybir.dt.uint8
I32 = mybir.dt.int32
ALU = mybir.AluOpType
ACT = mybir.ActivationFunctionType
AX_X = mybir.AxisListType.X

P = 128
B, S, D = 4, 512, 128
W = S // P
SK = 32
H0, DH0, KW = 8, 64, 8
H, DH = 16, 8
HC = 4
VC = HC * DH + HC
EPS = 1e-5
BIG = 3.0e38
MOE = {1: (8, 4), 3: (16, 2)}
TOPK = {1: 1, 3: 3}
NEG3 = -1.0e9 * DH ** 0.5
KNOTS = 8
CL, TPC = 8, 8
NT = CL * TPC
T = B * W
GT = 4
BODY = 2 * GT
SLOT_TILES = {l: -(-(T * TOPK[l] + MOE[l][0] - 1) // BODY) * BODY for l in MOE}
RING = {l: 8 // MOE[l][1] for l in MOE}
GRID = 16
TAB = 4 * GRID + 1 + D
COMP = 32


def build(nc, A, out):
    ctx = ExitStack()
    with ctx:
        def sb(name, cols, parts=P, dt=F32):
            return ctx.enter_context(nc.sbuf_tensor(name, [parts, cols], dt))

        def sem(name):
            return ctx.enter_context(nc.semaphore(name))

        x = sb("x", B * S)
        bank = [ctx.enter_context(nc.psum_tensor(f"bank{i}", [P, 512], F32)) for i in range(8)]
        xT_ps, s_ps, e_ps, o_ps, y_ps = bank[0], bank[2:4], bank[4:6], [bank[6], bank[1]], bank[7]
        ident = sb("ident", P)
        ones = sb("ones", P)
        onerow = sb("onerow", P, parts=1)
        mask16 = sb("mask16", H)
        mask4 = sb("mask4", HC)
        desc = sb("desc", 16)
        mhalf = sb("mhalf", W)
        stats = sb("stats", W * 6)
        mv = sb("mv", W * 2)
        veps = sb("veps", W)
        rstd = sb("rstd", W)
        xn = sb("xn", S)
        xnT = sb("xnT", S)
        ctxT = sb("ctxT", B * SK)
        peT = sb("peT", SK)
        hcT = sb("hcT", B * SK)
        ctxR = sb("ctxR", B * P)
        b2all = sb("b2all", 16 * P)
        wk0, wv0, wq0T, wo0 = (b2all[:, i * 512:(i + 1) * 512] for i in range(4))
        kT0 = sb("kT0", 512)
        vZ = sb("vZ", 4 * 16 * 64)
        A0 = sb("A0", B * 256)
        VW0 = sb("VW0", B * W * P)
        bo_row = {0: sb("bo0", 512, parts=1), 4: sb("bo4", 512, parts=1)}
        m0 = sb("m0", 32)
        r0 = sb("r0", 32)
        AL = (2, 4, 6)
        wq = {l: sb(f"wq{l}", P) for l in AL}
        wk = {l: sb(f"wk{l}", P) for l in AL}
        wv = {l: sb(f"wv{l}", P) for l in AL}
        wo = {l: sb(f"wo{l}", P) for l in AL}
        bq, bk = sb("bq", 1), sb("bk", 1)
        bv_row = sb("bv_row", P, parts=1)
        kT = sb("kT", B * SK)
        kB = vZ[:, B * 512:2 * B * 512]
        aB = {2: VW0, 4: VW0, 6: sb("aB6", B * 512)}
        cf = vZ[0:1, 0:B * 512]
        chi, clo = sb("chi", B * 512, parts=1, dt=F32R), sb("clo", B * 512, parts=1, dt=F32R)
        oner = sb("oner", P, parts=1, dt=F32R)
        vB = {l: sb(f"vB{l}", B * 4 * VC) for l in AL}
        cap4 = sb("cap4", SK)
        cap6 = sb("cap6", B * W * SK)
        mask_u8 = sb("mask_u8", B * W * SK, dt=U8)
        neg3 = sb("neg3", B * W * SK)
        mx = sb("mx", 2 * H)
        e_sb = sb("e_sb", 2 * 512)
        eT = sb("eT", 2 * 512)
        p0, pT0 = e_sb[:, 0:2 * 256], eT[0:64, :]
        rs = sb("rs", 2 * H)
        on = sb("on", S)
        oT = sb("oT", S)
        xnT_all = sb("xnT_all", B * S)
        gw = {l: sb(f"gw{l}", MOE[l][0]) for l in MOE}
        gb = sb("gb", 8)
        eb = sb("eb", 8)
        b1 = {l: sb(f"b1_{l}", MOE[l][0] * MOE[l][1]) for l in MOE}
        r5 = sb("r5", 2 * S)
        gates = {l: sb(f"gates{l}", T * MOE[l][0]) for l in MOE}
        gv = sb("gv", T * 16)
        ge = sb("ge", T * 16)
        gr = sb("gr", T * 16)
        gsel = sb("gsel", (T + 1) * 16)
        choice = [sb(f"choice{k}", T * 16) for k in range(3)]
        gk = sb("gk", 3 * T)
        gred = sb("gred", T * 2)
        tri = sb("tri", P)
        before = sb("before", 16 * 16)
        full = sb("full", 16)
        number = sb("number", 64, parts=1)
        ntile = sb("ntile", 16)
        first = sb("first", 16)
        ends = sb("ends", 16)
        base = sb("base", 16)
        cmp_ = sb("cmp_", 256)
        slot_at = sb("slot_at", T * 16)
        slot_of = [gv, ge, gr]
        slot_f = sb("slot_f", 3 * T)
        slots = sb("slots", 3 * T, dt=I32)
        esc = A0[0:1, 0:64 * 16]
        es_f = sb("es_f", 64, parts=1)
        es = sb("es", 64, parts=1, dt=I32)
        zero = sb("zero", GT * P)
        wall = sb("wall", 2 * 4096)
        WHALF = 4096
        w1s, w2s = e_sb, eT
        b1s = sb("b1s", 8 * 2)
        b2s = oT
        xsT = on
        hT = r5
        h_sb = sb("h_sb", 2 * 4 * S)
        xs, ys = h_sb[:, 0:BODY * P], h_sb[:, BODY * P:2 * BODY * P]
        xn_all = h_sb[:, B * S:2 * B * S]
        yg = wall
        wfc, wpj = sb("wfc", 512), sb("wpj", 512)
        ab = sb("ab", 512)
        t5 = kT0
        sc5 = sb("sc5", 16)
        wfcT, wpjT = sb("wfcT", 512), sb("wpjT", 512)
        fbT, v5, u5T = sb("fbT", 16, parts=16), sb("v5", P, parts=16), sb("u5T", 512, parts=16)
        t1 = sb("t1", P, parts=16)
        gate5 = sb("gate5", 1)
        raw = sb("raw", NT)
        sgq = sb("sgq", 2 * NT)
        rhs7 = sb("rhs7", CL + NT)
        csum = sb("csum", 2 * CL)
        cw1 = sb("cw1", COMP)
        cb1 = sb("cb1", 1, parts=COMP)
        cw2 = sb("cw2", 2, parts=COMP)
        cb2 = sb("cb2", 2)
        table = sb("table", TAB, parts=NT)
        knots = sb("knots", KNOTS)
        dknots = sb("dknots", KNOTS)
        temp = sb("temp", 2)
        oscale = sb("oscale", 1)
        gamma, beta = sb("gamma", P), sb("beta", P)
        sc7 = aB[4][:, 0:T * (CL + NT)]
        c7 = xnT_all[:, 0:12 * T * 8]
        sel7 = wall[:, 0:T * NT]
        one7 = wall[:, T * NT:2 * T * NT]
        oneT7 = eT[0:NT, 0:2 * S]
        h7 = e_sb[0:COMP, 0:2 * S]
        comp7 = sb("comp7", T * 2)
        par7 = kB[:, 0:T * (TAB - D)]
        g7, g7b = (kB[:, T * (TAB - D) + i * T * GRID:T * (TAB - D) + (i + 1) * T * GRID] for i in range(2))
        mag7 = sb("mag7", T)
        y7 = h_sb[:, 0:B * S]
        xb7 = h_sb[:, B * S:2 * B * S]
        xn7 = vZ[:, 0:B * S]

        s_x = [sem(f"s_x{b}") for b in range(B)]
        s_c0 = sem("s_c0")
        s_ca = sem("s_ca")
        s_cm = sem("s_cm")
        s_c5 = sem("s_c5")
        s_c7 = sem("s_c7")
        s_set = sem("s_set")
        s_hc = sem("s_hc")
        s_pp = sem("s_pp")
        s_pv = sem("s_pv")
        s_pa = sem("s_pa")
        s_var = sem("s_var")
        s_rstd = sem("s_rstd")
        s_xn = sem("s_xn")
        s_xT = sem("s_xT")
        s_xnT = sem("s_xnT")
        s_k = sem("s_k")
        s_kT = sem("s_kT")
        s_v = sem("s_v")
        s_vB = sem("s_vB")
        s_kB = sem("s_kB")
        s_a = sem("s_a")
        s_aB = sem("s_aB")
        s_c = sem("s_c")
        s_cf = sem("s_cf")
        s_cr = sem("s_cr")
        s_cap = sem("s_cap")
        s_s = sem("s_s")
        s_sub = sem("s_sub")
        s_exp = sem("s_exp")
        s_e = sem("s_e")
        s_eT = sem("s_eT")
        s_o = sem("s_o")
        s_on = sem("s_on")
        s_oP = sem("s_oP")
        s_oT = sem("s_oT")
        s_y = sem("s_y")
        s_res = sem("s_res")
        s_s0, s_sub0, s_exp0, s_p0, s_pP0, s_pT0 = (sem(n) for n in (
            "s_s0", "s_sub0", "s_exp0", "s_p0", "s_pP0", "s_pT0"))
        s_g = sem("s_g")
        s_gsub = sem("s_gsub")
        s_gexp = sem("s_gexp")
        s_gate = sem("s_gate")
        s_rank = sem("s_rank")
        s_sel = sem("s_sel")
        s_slot = sem("s_slot")
        s_zero = sem("s_zero")
        s_wall = sem("s_wall")
        s_b2l = sem("s_b2l")
        s_sc_x = sem("s_sc_x")
        s_xs = [sem(f"s_xs{r}") for r in range(2)]
        s_xt = sem("s_xt")
        s_xc = sem("s_xc")
        s_wc = sem("s_wc")
        s_wd = sem("s_wd")
        s_hh = sem("s_hh")
        s_hr = sem("s_hr")
        s_my = sem("s_my")
        s_yb = sem("s_yb")
        s_ys = [sem(f"s_ys{r}") for r in range(2)]
        s_gat = sem("s_gat")
        s_gad = sem("s_gad")
        s_h5, s_r5, s_q5 = sem("s_h5"), sem("s_r5"), sem("s_q5")
        s_sc, s_hc7, s_hg7, s_cp7, s_cb7, s_th7 = (sem(n) for n in (
            "s_sc", "s_hc7", "s_hg7", "s_cp7", "s_cb7", "s_th7"))
        s_sg, s_ex, s_oh, s_ohP, s_ohT, s_tb, s_par, s_yd, s_o7 = (sem(n) for n in (
            "s_sg", "s_ex", "s_oh", "s_ohP", "s_ohT", "s_tb", "s_par", "s_yd", "s_o7"))
        s_xb = sem("s_xb")
        s_out = sem("s_out")

        def tile_of(buf, i, n=P):
            return buf[:, i * n:(i + 1) * n]

        def one_bank(b):
            return bank[(0, 1, 6, 7)[b]]

        def table_bank(w):
            return bank[(2, 3, 4, 5, 0, 1, 6, 7)[w // 2]]

        def batch_of(b):
            return x[:, bass.ds(b * S, S)]

        res_before = {0: 0, 2: 4, 4: 8, 5: 12, 6: 16}
        att_before = {2: 0, 4: 4, 6: 8}
        moe_before = {1: 0, 3: 4}
        tile_before = {1: 0, 3: SLOT_TILES[1]}
        gather_before = {1: 0, 3: 16 * T * TOPK[1]}
        NSL = max(SLOT_TILES.values())
        xbuf = nc.dram_tensor("xbuf", (NSL * P, D), F32, kind="Internal").ap()
        ybuf = nc.dram_tensor("ybuf", (NSL * P, D), F32, kind="Internal").ap()

        def groups(buf):
            return buf.rearrange("(g w p) f -> p g w f", w=GT, p=P)

        loads = {}

        block = ctx.enter_context(nc.Block())

        @block.sync
        def _(sp):
            def load(s, dst, src):
                sp.dma_start(dst, src).then_inc(s, 16)
                loads[s.name] = loads.get(s.name, 0) + 16

            def rows(src, n=P):
                return src.partition_broadcast(n)

            load(s_c0, ctxT[:, :], A["ctxT"])
            load(s_c0, peT[:, :], A["peT"])
            load(s_c0, ident[:, :], A["ident"])
            load(s_c0, wk0[:, :], A["L0_xattn_Wk"])
            load(s_c0, wv0[:, :], A["L0_xattn_Wv"])
            load(s_c0, wq0T[:, :], A["wq0T"])
            load(s_c0, wo0[:, :], A["wo0"])
            load(s_c0, mask16[:, :], A["mask16"])
            load(s_c0, mask4[:, :], A["mask4"])
            load(s_c0, desc[:, :], A["desc"])
            load(s_c0, bo_row[0][:, :], A["bo0"])
            load(s_c0, tri[:, :], A["tri"])
            load(s_c0, before[:, :], A["before"])
            load(s_c0, full[:, :], A["full"])
            load(s_c0, number[:, :], A["number"])
            for b in range(B):
                load(s_x[b], tile_of(x, b, S).rearrange("p (w f) -> p w f", w=W),
                     A["x"][b].rearrange("(w p) f -> p w f", p=P))
            for l in AL:
                load(s_ca, wk[l][:, :], A[f"wk{l}"])
                load(s_ca, wv[l][:, :], A[f"wv{l}"])
                load(s_ca, wq[l][:, :], A[f"wq{l}"])
                load(s_ca, wo[l][:, :], A[f"wo{l}"])
            load(s_ca, bq[:, :], A["bq"])
            load(s_ca, bk[:, :], A["bk"])
            load(s_ca, bv_row[:, :], A["bv"])
            load(s_ca, bo_row[4][:, :], A["bo4"])
            load(s_ca, cap4[:, :], A["cap4"])
            load(s_ca, mask_u8[:, :].rearrange("p (t k) -> p t k", k=SK),
                 A["mask"].rearrange("(t p) k -> p t k", p=P))
            load(s_cm, gw[1][:, :], A["gw1"])
            load(s_cm, gw[3][:, :], A["L1_ffn_gate"])
            load(s_cm, gb[:, :], rows(A["L0_ffn_gate_b"]))
            load(s_cm, eb[:, :], rows(A["L0_ffn_expert_bias"]))
            load(s_cm, b1[1][:, :], A["b1_1"])
            load(s_cm, b1[3][:, :], A["b1_3"])
            load(s_c5, wfc[:, :].rearrange("p (c f) -> p c f", c=4),
                 A["L2_ffn_w_fc"].rearrange("(c p) f -> p c f", p=P))
            load(s_c5, wpj[:, :], A["L2_ffn_w_proj"])
            load(s_c5, fbT[:, :], A["fbT"])
            load(s_c5, v5[:, :], A["L2_ffn_v"])
            load(s_c5, u5T[:, :], A["uT"])
            load(s_c5, gate5[:, :], rows(A["gate5"]))
            load(s_c7, raw[:, :], A["rawT"])
            load(s_c7, cw1[:, :], A["L3_ffn_compress_w1"])
            load(s_c7, cb1[:, :], A["cb1"])
            load(s_c7, cw2[:, :], A["L3_ffn_compress_w2"])
            load(s_c7, cb2[:, :], rows(A["L3_ffn_compress_b2"]))
            load(s_c7, table[:, :], A["table"])
            load(s_c7, knots[:, :], rows(A["L3_ffn_knot_values"]))
            load(s_c7, temp[:, 0:1], rows(A["L3_ffn_temperature"]))
            load(s_c7, oscale[:, :], rows(A["L3_ffn_output_scale"]))
            load(s_c7, gamma[:, :], rows(A["L3_ffn_norm_gamma"]))
            load(s_c7, beta[:, :], rows(A["L3_ffn_norm_beta"]))
            sp.wait_ge(s_set, 7)
            for g in range(NSL // GT):
                load(s_zero, groups(xbuf)[:, g], zero[:, :].rearrange("p (w f) -> p w f", w=GT))

            def group_load(l, g, r):
                sp.dma_start(xs[:, r * GT * P:(r + 1) * GT * P].rearrange("p (w f) -> p w f", w=GT),
                             groups(xbuf)[:, bass.ds(g, 1)].rearrange("p g w f -> p (g w) f")).then_inc(s_xs[r], 16)

            def group_store(l, g, r):
                sp.dma_start(groups(ybuf)[:, bass.ds(g, 1)].rearrange("p g w f -> p (g w) f"),
                             ys[:, r * GT * P:(r + 1) * GT * P].rearrange("p (w f) -> p w f", w=GT)).then_inc(s_ys[r], 16)

            for l in MOE:
                E, C = MOE[l]
                tb = tile_before[l]
                if l == 1:
                    load(s_wall, wall[:, 0:E * C * P].rearrange("p (e f) -> p e f", e=E), A[f"w1_{l}"].rearrange("e p f -> p e f"))
                    load(s_wall, wall[:, WHALF:WHALF + E * C * P].rearrange("p (e f) -> p e f", e=E), A[f"w2_{l}"].rearrange("e p f -> p e f"))
                    sp.wait_ge(s_pp, 8)
                else:
                    sp.wait_ge(s_gad, 4)
                    load(s_wall, wall[:, 0:E * C * P].rearrange("p (e f) -> p e f", e=E), A[f"w1_{l}"].rearrange("e p f -> p e f"))
                    load(s_wall, wall[:, WHALF:WHALF + E * C * P].rearrange("p (e f) -> p e f", e=E), A[f"w2_{l}"].rearrange("e p f -> p e f"))
                load(s_b2l, b2all[:, 0:E * P], rows(A["L0_ffn_b2" if l == 1 else "L1_ffn_b2"].rearrange("e f -> (e f)")))
                sp.wait_ge(s_sc_x, gather_before[l] + 16 * T * TOPK[l])
                for r in range(2):
                    group_load(l, r, r)
                with sp.Fori(1, SLOT_TILES[l] // BODY) as i:
                    for r in range(2):
                        sp.wait_ge(s_xt, i * BODY + (tb - BODY + GT * (r + 1)))
                        group_load(l, i * 2 + r, r)
                        sp.wait_ge(s_yb, i * BODY + (tb - BODY + GT * (r + 1)))
                        group_store(l, i * 2 + (r - 2), r)
                for r in range(2):
                    sp.wait_ge(s_yb, tb + SLOT_TILES[l] - BODY + GT * (r + 1))
                    group_store(l, SLOT_TILES[l] // GT - 2 + r, r)
            for b in range(B):
                sp.wait_ge(s_o7, b + 1)
                sp.dma_start(out[b].rearrange("(w p) f -> p w f", p=P),
                             tile_of(y7, b, S).rearrange("p (w f) -> p w f", w=W)).then_inc(s_out, 16)
            sp.wait_ge(s_out, 16 * B)

        @block.gpsimd
        def _(pool):
            nc.gpsimd.memset(mhalf[:, :], -0.5).then_inc(s_set, 1)
            nc.gpsimd.memset(onerow[:, :], 1.0).then_inc(s_set, 1)
            nc.gpsimd.memset(ones[:, :], 1.0).then_inc(s_res, 1)
            nc.gpsimd.memset(vZ[:, :], 0.0).then_inc(s_set, 1)
            nc.gpsimd.memset(neg3[:, :], NEG3).then_inc(s_set, 1)
            nc.gpsimd.memset(cap6[:, :], BIG).then_inc(s_set, 1)
            nc.gpsimd.memset(zero[:, :], 0.0).then_inc(s_set, 1)
            nc.gpsimd.memset(gsel[:, :], 0.0).then_inc(s_set, 1)
            pool.wait_ge(s_set, 7)
            pool.wait_ge(s_res, 1)

            def power(n):
                pool.wait_ge(s_var, n + 1)
                nc.gpsimd.tensor_tensor(rstd[:, :], veps[:, :], mhalf[:, :], ALU.pow).then_inc(s_rstd, 1)

            def scatter(l):
                pool.wait_ge(s_slot, 1 if l == 1 else 2)
                pool.wait_ge(s_zero, loads["s_zero"])
                for k in range(TOPK[l]):
                    for t in range(T):
                        c = k * T + t
                        nc.gpsimd.indirect_dma_start(xbuf[0:SLOT_TILES[l] * P], bass.IndirectOffsetOnAxis(slots[:, c:c + 1], 0), tile_of(xn_all, t), None).then_inc(s_sc_x, 16)

            def gather(l, b):
                K = TOPK[l]
                if b:
                    pool.wait_ge(s_gat, gather_before[l] + 16 * W * K * b)
                for t in range(b * W, (b + 1) * W):
                    for k in range(K):
                        c = k * T + t
                        nc.gpsimd.indirect_dma_start(tile_of(yg, t * K + k), None, ybuf[0:SLOT_TILES[l] * P], bass.IndirectOffsetOnAxis(slots[:, c:c + 1], 0)).then_inc(s_gat, 16)

            power(0)
            with pool.Fori(1, 2 * B) as n:
                power(n)
            for l in MOE:
                scatter(l)
                for r in range(2):
                    pool.wait_ge(s_ys[r], 16 * (tile_before[l] + SLOT_TILES[l]) // BODY)
                gather(l, 0)
                for b in range(1, B):
                    gather(l, b)
                    power(4 * l + 3 + b)
                if l == 1:
                    with pool.Fori(11, 16) as n:
                        power(n)
            with pool.Fori(19, 8 * B) as n:
                power(n)
            pool.wait_ge(s_c7, loads["s_c7"])
            for b in range(B):
                pool.wait_ge(s_res, 21)
                nc.gpsimd.tensor_tensor(tile_of(xb7, b, S).rearrange("p (w f) -> p w f", w=W),
                                        tile_of(x, b, S).rearrange("p (w f) -> p w f", w=W),
                                        beta[:, :].unsqueeze(1).to_broadcast([P, W, D]), ALU.add).then_inc(s_xb, 1)
            for b in range(B):
                power(32 + b)

        @block.vector
        def _(dve):
            v = nc.vector

            def bn(src):
                for w in range(W):
                    v.bn_stats(stats[:, w * 6:w * 6 + 6], src(w))
                dve.drain()
                for w in range(W):
                    v.bn_aggr(mv[:, 2 * w:2 * w + 2], stats[:, w * 6:w * 6 + 6])
                dve.drain()
                v.tensor_scalar_add(veps[:, :], mv[:, 1:2 * W:2], EPS).then_inc(s_var, 1)

            def stats_of(b):
                dve.drain()
                bn(lambda w: x[:, bass.ds(b * S + w * P, P)])

            def normed(n, b, dst=None):
                dve.wait_ge(s_rstd, n + 1)
                if not (isinstance(n, int) and n == 0):
                    dve.wait_ge(s_xT, n)
                for w in range(W):
                    i = v.tensor_scalar(tile_of(xn if dst is None else dst, w), x[:, bass.ds(b * S + w * P, P)], mv[:, 2 * w:2 * w + 1],
                                        rstd[:, w:w + 1], ALU.subtract, ALU.mult)
                i.then_inc(s_xn, 1)

            def norm(n, b, dst=None):
                stats_of(b)
                normed(n, b, dst)

            def add_y(layer, b):
                k = res_before[layer]
                dve.wait_ge(s_y, b + (k + 1))
                v.tensor_tensor(batch_of(b), batch_of(b), y_ps[:, :], ALU.add).then_inc(s_res, 1)

            dve.wait_ge(s_x[0], 16)
            norm(0, 0)
            dve.wait_ge(s_c0, loads["s_c0"])
            v.tensor_tensor(hcT[:, :].rearrange("p (b j) -> p b j", b=B), ctxT[:, :].rearrange("p (b j) -> p b j", b=B),
                            peT[:, :].unsqueeze(1).to_broadcast([P, B, SK]), ALU.add)
            v.tensor_copy(ctxR[:, :].rearrange("p (b r j) -> p b r j", b=B, r=HC),
                          ctxT[:, :].rearrange("p (b j) -> p b j", b=B).unsqueeze(2).to_broadcast([P, B, HC, SK])).then_inc(s_hc, 1)
            dve.wait_ge(s_pp, 1)
            v.tensor_copy(kT0[:, :], bank[0][:, :]).then_inc(s_pv, 1)
            dve.wait_ge(s_pp, 2)
            dve.wait_ge(s_set, 7)
            vz = vZ[:, :].rearrange("p (c t h j) -> p c t h j", c=4, t=B * W, h=H0)
            for c in range(4):
                for r in range(2):
                    i = v.tensor_copy(vz[64 * r:64 * r + 64, c, :, 2 * c + r, :],
                                      bank[1][64 * r:64 * r + 64, c * P:(c + 1) * P].rearrange("p (t j) -> p t j", j=KW))
            i.then_inc(s_pv, 1)
            a0 = A0[:, :].rearrange("p (t h j) -> p h t j", h=H0, j=KW)
            for g in range(2):
                dve.wait_ge(s_pp, 3 + g)
                for h in range(4):
                    i = v.tensor_copy(a0[:, 2 * h + g], bank[2 + g][:, h * P:(h + 1) * P].rearrange("p (t j) -> p t j", j=KW))
                i.then_inc(s_pv, 1)
            for g in range(4):
                dve.wait_ge(s_pp, 5 + g)
                v.tensor_copy(VW0[0:64, g * 512:(g + 1) * 512], bank[4 + g][0:64, :]).then_inc(s_pv, 1)

            def prepare(l):
                i_l = AL.index(l)
                if l == 2:
                    dve.wait_ge(s_ca, loads["s_ca"])
                dve.wait_ge(s_kT, i_l + 1)
                if l != 2:
                    dve.wait_ge(s_a, 4 * i_l)
                if l == 6:
                    dve.wait_ge(s_c, 4)
                for b in range(B):
                    v.tensor_tensor(kB[:, b * 512:(b + 1) * 512].rearrange("p (h j) -> p h j", h=H),
                                    kT[:, b * SK:(b + 1) * SK].unsqueeze(1).to_broadcast([P, H, SK]),
                                    mask16[:, :].unsqueeze(2).to_broadcast([P, H, SK]), ALU.mult).then_inc(s_kB, 1)
                dve.wait_ge(s_v, i_l + 1)
                vb = vB[l][:, :].rearrange("p (t c) -> p t c", c=VC)
                v.tensor_tensor(vb[:, :, 0:HC * DH].rearrange("p t (h d) -> p t h d", h=HC),
                                bank[1][:, :].rearrange("p (t h d) -> p t h d", h=HC, d=DH),
                                mask4[:, :].unsqueeze(1).unsqueeze(3).to_broadcast([P, B * 4, HC, DH]), ALU.mult)
                v.tensor_copy(vb[:, :, HC * DH:VC], mask4[:, :].unsqueeze(1).to_broadcast([P, B * 4, HC])).then_inc(s_vB, 1)

            def split_c():
                dve.wait_ge(s_cf, 4)
                v.tensor_copy(chi[:, :], cf[:, :])
                v.tensor_copy(oner[:, :], ones[0:1, :])
                dve.drain()
                v.tensor_tensor(clo[:, :], cf[:, :], chi[:, :].bitcast(F32), ALU.subtract).then_inc(s_cr, 1)

            def ternary(wt, s0, parts):
                n = 512 // parts
                v.scalar_tensor_tensor(ab[:, :], wt[:, :], -1.0, wt[:, :], ALU.mult, ALU.max)
                dve.drain()
                v.tensor_reduce(sc5[:, s0:s0 + parts], ab[:, :].rearrange("p (c f) -> p c f", c=parts), AX_X, ALU.add)
                dve.drain()
                v.tensor_scalar(sc5[:, s0:s0 + parts], sc5[:, s0:s0 + parts], 1.0 / n, 1e-5, ALU.mult, ALU.max)
                dve.drain()
                v.tensor_scalar(sc5[:, 4 + s0:4 + s0 + parts], sc5[:, s0:s0 + parts], 0.5, None, ALU.mult)
                v.tensor_scalar(sc5[:, 8 + s0:8 + s0 + parts], sc5[:, s0:s0 + parts], -0.5, None, ALU.mult)
                dve.drain()
                for c in range(parts):
                    k = s0 + c
                    v.tensor_scalar(ab[:, c * n:(c + 1) * n], wt[:, c * n:(c + 1) * n], sc5[:, 4 + k:5 + k], sc5[:, k:k + 1], ALU.is_gt, ALU.mult)
                    v.tensor_scalar(t5[:, c * n:(c + 1) * n], wt[:, c * n:(c + 1) * n], sc5[:, 8 + k:9 + k], sc5[:, k:k + 1], ALU.is_lt, ALU.mult)
                dve.drain()
                v.tensor_tensor(ab[:, :], ab[:, :], t5[:, :], ALU.subtract).then_inc(s_pv, 1)

            def prepare5(stage):
                if stage == 0:
                    dve.wait_ge(s_c5, loads["s_c5"])
                    ternary(wfc, 0, 4)
                elif stage == 1:
                    dve.wait_ge(s_pp, 9)
                    v.tensor_copy(wfcT[:, :], bank[0][:, :])
                    ternary(wpj, 0, 1)
                elif stage == 2:
                    dve.wait_ge(s_pp, 10)
                    v.tensor_copy(wpjT[:, :], bank[1][:, :]).then_inc(s_pv, 1)
                    dve.wait_ge(s_pp, 11)
                    v.tensor_copy(t1[:, :], bank[0][0:16, 0:P]).then_inc(s_pv, 1)
                else:
                    dve.wait_ge(s_pp, 12)
                    v.scalar_tensor_tensor(wfcT[:, :], bank[1][:, :], gate5[:, 0:1], wfcT[:, :], ALU.mult, ALU.add).then_inc(s_pv, 1)

            def prepare7():
                dve.wait_ge(s_c7, loads["s_c7"])
                v.tensor_scalar(sgq[:, 0:NT], raw[:, :], 0.3, None, ALU.is_gt)
                v.tensor_scalar(sgq[:, NT:2 * NT], raw[:, :], -0.3, None, ALU.is_lt)
                dve.drain()
                v.tensor_tensor(sgq[:, 0:NT], sgq[:, 0:NT], sgq[:, NT:2 * NT], ALU.subtract)
                dve.drain()
                v.tensor_tensor(sgq[:, 0:NT], sgq[:, 0:NT], raw[:, :], ALU.subtract)
                dve.drain()
                sigs = rhs7[:, CL:CL + NT]
                v.tensor_tensor(sigs, raw[:, :], sgq[:, 0:NT], ALU.add)
                dve.drain()
                sv = sigs.rearrange("p (c t) -> p t c", t=TPC)
                v.tensor_tensor(csum[:, 0:CL], sv[:, 0], sv[:, 1], ALU.add)
                for t in range(2, TPC):
                    dve.drain()
                    v.tensor_tensor(csum[:, 0:CL], csum[:, 0:CL], sv[:, t], ALU.add)
                dve.drain()
                v.tensor_scalar(csum[:, CL:2 * CL], csum[:, 0:CL], 0.0, None, ALU.is_lt)
                v.tensor_scalar(rhs7[:, 0:CL], csum[:, 0:CL], 0.0, None, ALU.is_gt)
                dve.drain()
                v.tensor_tensor(rhs7[:, 0:CL], rhs7[:, 0:CL], csum[:, CL:2 * CL], ALU.subtract)
                v.tensor_tensor(dknots[:, 0:KNOTS - 1], knots[:, 1:KNOTS], knots[:, 0:KNOTS - 1], ALU.subtract)
                v.tensor_scalar(temp[:, 1:2], temp[:, 0:1], 1e-6, None, ALU.add)
                dve.drain()
                v.reciprocal(temp[:, 0:1], temp[:, 1:2])
                dve.drain()
                v.tensor_scalar(temp[:, 1:2], temp[:, 0:1], -1.0, None, ALU.mult).then_inc(s_pv, 1)

            wide = [P, 32, KW]

            def w_scores(b):
                s = s_ps[b % 2][:, 0:256].rearrange("p (g j) -> p g j", j=KW)
                dve.wait_ge(s_s0, b + 1)
                v.tensor_reduce(m0[:, :], s, AX_X, ALU.max)
                dve.drain()
                v.tensor_tensor(tile_of(p0, b % 2, 256).rearrange("p (g j) -> p g j", j=KW), s,
                                m0[:, :].unsqueeze(2).to_broadcast(wide), ALU.subtract).then_inc(s_sub0, 1)

            def w_probs(b):
                e = tile_of(p0, b % 2, 256).rearrange("p (g j) -> p g j", j=KW)
                dve.wait_ge(s_exp0, b + 1)
                v.tensor_reduce(r0[:, :], e, AX_X, ALU.add)
                dve.drain()
                v.reciprocal(r0[:, :], r0[:, :])
                dve.drain()
                v.tensor_tensor(e, e, r0[:, :].unsqueeze(2).to_broadcast(wide), ALU.mult).then_inc(s_p0, 1)

            for b in range(1, B):
                dve.wait_ge(s_x[b], 16)
            norm(1, 1)
            w_scores(0)
            norm(2, 2)
            w_scores(1)
            w_probs(0)
            norm(3, 3)
            w_scores(2)
            w_probs(1)
            add_y(0, 0)
            w_scores(3)
            w_probs(2)
            norm(4, 0, tile_of(xn_all, 0, S))
            add_y(0, 1)
            w_probs(3)
            norm(5, 1, tile_of(xn_all, 1, S))
            add_y(0, 2)
            norm(6, 2, tile_of(xn_all, 2, S))
            add_y(0, 3)
            norm(7, 3, tile_of(xn_all, 3, S))

            def max_sub(l, k, b, w):
                t = (b + k) * W + w
                s = s_ps[w % 2][:, :].rearrange("p (h j) -> p h j", h=H)
                m = mx[:, (w % 2) * H:(w % 2 + 1) * H]
                dve.wait_ge(s_s, t + 1)
                if l == 4 and w == 0:
                    v.tensor_tensor(s[0:SK], s[0:SK], cap4[0:SK, :].unsqueeze(1).to_broadcast([SK, H, SK]), ALU.min)
                    dve.drain()
                if l == 6:
                    v.tensor_tensor(s, s, cap6[:, bass.ds((b * W + w) * SK, SK)].unsqueeze(1).to_broadcast([P, H, SK]), ALU.min)
                    dve.drain()
                v.tensor_reduce(m, s, AX_X, ALU.max)
                dve.drain()
                v.tensor_tensor(tile_of(e_sb, w % 2, 512).rearrange("p (h j) -> p h j", h=H), s,
                                m.unsqueeze(2).to_broadcast([P, H, SK]), ALU.subtract).then_inc(s_sub, 1)

            def normalise(l, k, b, w):
                t = (b + k) * W + w
                o = o_ps[w % 2][:, 0:4 * VC].rearrange("p (c v) -> p c v", c=4)
                r = rs[:, (w % 2) * H:(w % 2 + 1) * H].rearrange("p (c h) -> p c h", c=4)
                dve.wait_ge(s_o, t + 1)
                v.reciprocal(r, o[:, :, HC * DH:VC])
                dve.drain()
                v.tensor_tensor(tile_of(on, w).rearrange("p (c h d) -> p c h d", c=4, h=HC),
                                o[:, :, 0:HC * DH].rearrange("p c (h d) -> p c h d", h=HC),
                                r.unsqueeze(3).to_broadcast([P, 4, HC, DH]), ALU.mult).then_inc(s_on, 1)

            def attention(l, b, more, dst=None, ahead=False):
                k = att_before[l]
                n = b + 4 * l
                nb = b + 1 if more else 0
                stats_of(nb)
                max_sub(l, k, b, 2)
                normed(n + 1, nb, dst)
                normalise(l, k, b, 0)
                max_sub(l, k, b, 3)
                normalise(l, k, b, 1)
                normalise(l, k, b, 2)
                if more:
                    max_sub(l, k, nb, 0)
                normalise(l, k, b, 3)
                if more:
                    max_sub(l, k, nb, 1)
                if ahead and l in (2, 4):
                    add_experts(l - 1, b + 2)
                add_y(l, b)

            def attention_layer(l, dst=None):
                k = att_before[l]
                max_sub(l, k, 0, 0)
                max_sub(l, k, 0, 1)
                if l in (2, 4):
                    add_experts(l - 1, 1)
                with dve.Fori(0, B - 2) as b:
                    attention(l, b, True, ahead=True)
                attention(l, B - 2, True)
                attention(l, B - 1, False, dst)

            def first_largest(one, vals, n):
                w_ = [P, T, n]
                most, first = gred[:, 0:T], gred[:, T:2 * T]
                v.tensor_reduce(most, vals, AX_X, ALU.max)
                dve.drain()
                v.tensor_tensor(one, vals, most.unsqueeze(2).to_broadcast(w_), ALU.is_equal)
                dve.drain()
                v.tensor_tensor(one, one, desc[:, 16 - n:16].unsqueeze(1).to_broadcast(w_), ALU.mult)
                dve.drain()
                v.tensor_reduce(first, one, AX_X, ALU.max)
                dve.drain()
                v.tensor_tensor(one, one, first.unsqueeze(2).to_broadcast(w_), ALU.is_equal)
                dve.drain()

            def gating(l):
                E, C = MOE[l]
                w_ = [P, T, E]

                def three(buf):
                    return buf[:, 0:T * E].rearrange("p (w e) -> p w e", w=T)

                logit = three(bank[1])
                gout = three(gates[l])
                dve.wait_ge(s_g, moe_before[l] + B)
                if l == 1:
                    dve.wait_ge(s_cm, loads["s_cm"])
                    v.tensor_tensor(three(gv), logit, gb[:, :].unsqueeze(1).to_broadcast(w_), ALU.add)
                    dve.drain()
                    v.tensor_tensor(three(gv), three(gv), eb[:, :].unsqueeze(1).to_broadcast(w_), ALU.add)
                    dve.drain()
                    first_largest(three(choice[0]), three(gv), E)
                    v.tensor_copy(three(gsel), three(choice[0])).then_inc(s_sel, 1)
                    return
                most, total = gred[:, 0:T], gred[:, T:2 * T]
                v.tensor_reduce(most, logit, AX_X, ALU.max)
                dve.drain()
                v.tensor_tensor(three(gv), logit, most.unsqueeze(2).to_broadcast(w_), ALU.subtract).then_inc(s_gsub, 1)
                dve.wait_ge(s_gexp, 1)
                v.tensor_reduce(total, three(gv), AX_X, ALU.add)
                dve.drain()
                v.reciprocal(total, total)
                dve.drain()
                v.tensor_tensor(three(gr), three(gv), total.unsqueeze(2).to_broadcast(w_), ALU.mult)
                dve.drain()
                v.tensor_copy(three(gv), three(gr))
                dve.drain()
                for k_ in range(3):
                    one = three(choice[k_])
                    first_largest(one, three(gv), E)
                    if k_ < 2:
                        v.scalar_tensor_tensor(three(gv), one, -2.0, three(gv), ALU.mult, ALU.add)
                        dve.drain()
                v.tensor_tensor(three(gsel), three(choice[0]), three(choice[1]), ALU.add)
                dve.drain()
                v.tensor_tensor(three(gsel), three(gsel), three(choice[2]), ALU.add).then_inc(s_sel, 1)
                dve.drain()
                v.tensor_tensor(three(gr), three(gr), three(gsel), ALU.mult)
                dve.drain()
                v.tensor_reduce(total, three(gr), AX_X, ALU.add)
                dve.drain()
                v.tensor_scalar(total, total, 1e-12, None, ALU.max)
                dve.drain()
                v.reciprocal(total, total)
                dve.drain()
                v.tensor_tensor(gout, three(gr), total.unsqueeze(2).to_broadcast(w_), ALU.mult)
                dve.drain()
                for k_ in range(3):
                    v.tensor_tensor(three(slot_of[k_]), gout, three(choice[k_]), ALU.mult)
                dve.drain()
                for k_ in range(3):
                    v.tensor_reduce(gk[:, k_ * T:(k_ + 1) * T], three(slot_of[k_]), AX_X, ALU.add)
                dve.drain()

            def route(l):
                E, C = MOE[l]
                K, NS = TOPK[l], SLOT_TILES[l]
                rank = bank[2][:, 0:T * E].rearrange("p (t e) -> p t e", e=E)
                total = bank[2][:, T * E:(T + 1) * E]
                dve.wait_ge(s_rank, 1 if l == 1 else 2)
                over = cmp_[:, 0:E * 16].rearrange("p (e m) -> p e m", e=E)
                v.tensor_tensor(over, total.unsqueeze(2).to_broadcast([P, E, 16]), full[:, :].unsqueeze(1).to_broadcast([P, E, 16]), ALU.is_gt)
                dve.drain()
                v.tensor_reduce(ntile[:, 0:E], over, AX_X, ALU.add)
                dve.drain()
                earlier = cmp_[:, 0:E * E].rearrange("p (e f) -> p e f", e=E)
                v.tensor_tensor(earlier, ntile[:, 0:E].unsqueeze(1).to_broadcast([P, E, E]),
                                before[:, :].rearrange("p (e f) -> p e f", e=16)[:, 0:E, 0:E], ALU.mult)
                dve.drain()
                v.tensor_reduce(first[:, 0:E], earlier, AX_X, ALU.add)
                dve.drain()
                v.tensor_tensor(ends[:, 0:E], first[:, 0:E], ntile[:, 0:E], ALU.add)
                v.tensor_scalar(base[:, 0:E], first[:, 0:E], float(P), -1.0, ALU.mult, ALU.add)
                dve.drain()
                at = slot_at[:, 0:T * E].rearrange("p (t e) -> p t e", e=E)
                v.tensor_tensor(at, rank, base[:, 0:E].unsqueeze(1).to_broadcast([P, T, E]), ALU.add)
                past = esc[:, 0:NS * E].rearrange("p (s e) -> p s e", e=E)
                v.tensor_tensor(past, number[:, 0:NS].unsqueeze(2).to_broadcast([1, NS, E]), ends[0:1, 0:E].unsqueeze(1).to_broadcast([1, NS, E]), ALU.is_ge)
                dve.drain()
                for k in range(K):
                    v.tensor_tensor(slot_of[k][:, 0:T * E], slot_at[:, 0:T * E], choice[k][:, 0:T * E], ALU.mult)
                v.tensor_reduce(es_f[:, 0:NS], past, AX_X, ALU.add)
                dve.drain()
                for k in range(K):
                    v.tensor_reduce(slot_f[:, k * T:(k + 1) * T], slot_of[k][:, 0:T * E].rearrange("p (t e) -> p t e", e=E), AX_X, ALU.add)
                v.tensor_scalar(es_f[:, 0:NS], es_f[:, 0:NS], float(E - 1), None, ALU.min)
                dve.drain()
                v.tensor_copy(es[:, 0:NS], es_f[:, 0:NS])
                v.tensor_copy(slots[:, 0:K * T], slot_f[:, 0:K * T]).then_inc(s_slot, 1)
                dve.drain()

            def add_experts(l, b):
                K = TOPK[l]
                dve.drain()
                dve.wait_ge(s_gat, b * (16 * W * K) + (gather_before[l] + 16 * W * K))
                if l == 1:
                    i = v.tensor_tensor(batch_of(b), batch_of(b), yg[:, bass.ds(b * S, S)], ALU.add)
                else:
                    for k in range(K):
                        if k:
                            dve.drain()
                        for w in range(W):
                            xt = x[:, bass.ds(b * S + w * P, P)]
                            i = v.scalar_tensor_tensor(xt, yg[:, bass.ds(b * (K * S) + (w * K + k) * P, P)],
                                                       gk[:, bass.ds(b * W + (k * T + w), 1)], xt, ALU.mult, ALU.add)
                i.then_inc(s_gad, 1)

            def moe(l):
                E, C = MOE[l]
                tb, R, n = tile_before[l], RING[l], MOE[l][1] * P

                def add_bias(s, u):
                    dve.wait_ge(s_my, s + (tb + 1))
                    v.tensor_tensor(tile_of(ys, u), bank[6 + u % 2][:, 0:P], tile_of(b2s, u % 4), ALU.add).then_inc(s_yb, 1)

                def body(i, peeled):
                    experts = v_loads(es[0:1, bass.ds(i * BODY, BODY)], E)
                    for u in range(BODY):
                        s = i * BODY + u
                        e = experts[u]
                        if not (peeled and u < R):
                            dve.wait_ge(s_hr, s + (tb + 1 - R))
                        v.tensor_copy(w1s[:, (u % R) * n:(u % R + 1) * n], wall[:, bass.ds(e * n, n)])
                        v.tensor_copy(b1s[:, (u % R) * C:(u % R + 1) * C], b1[l][:, bass.ds(e * C, C)]).then_inc(s_wc, 1)
                        if not peeled or u >= 2:
                            if (u - 2) % GT == 0 and not peeled:
                                dve.wait_ge(s_ys[(u - 2) // GT], i * 16 + 16 * (tb // BODY))
                            add_bias(s - 2, (u - 2) % BODY)
                        v.tensor_copy(w2s[:, (u % R) * n:(u % R + 1) * n], wall[:, bass.ds(e * n + WHALF, n)])
                        v.tensor_copy(tile_of(b2s, u % 4), b2all[:, bass.ds(e * P, P)]).then_inc(s_wd, 1)
                        if u % 2:
                            dve.drain()

                if l == 1:
                    dve.wait_ge(s_wall, 32)
                    dve.wait_ge(s_b2l, 16)
                else:
                    dve.wait_ge(s_wall, 64)
                    dve.wait_ge(s_b2l, 32)
                body(0, True)
                with dve.Fori(1, SLOT_TILES[l] // BODY) as i:
                    body(i, False)
                for u in range(BODY - 2, BODY):
                    add_bias(SLOT_TILES[l] - BODY + u, u)
                add_experts(l, 0)
                norm(4 * l + 4, 0)

            def v_loads(src, E):
                _, values = nc.values_load_multi_w_load_instructions(src, engines=(mybir.EngineType.DVE,), min_val=0, max_val=E - 1,
                                                                        skip_runtime_bounds_check_because="a minimum on the chip bounds them")
                return values

            gating(1)
            route(1)
            prepare(2)
            for stage in range(4):
                prepare5(stage)
            prepare7()
            moe(1)
            attention_layer(2, tile_of(xn_all, 0, S))
            for b in range(1, B):
                norm(12 + b, b, tile_of(xn_all, b, S))
            gating(3)
            route(3)
            prepare(4)
            split_c()
            prepare(6)
            v.copy_predicated(cap6[:, :], mask_u8[:, :], neg3[:, :])
            moe(3)
            attention_layer(4)

            def squares(b, nb):
                norm(b + 21, nb)
                for c in range(4):
                    r = tile_of(r5, c % 2, S)
                    dve.wait_ge(s_r5, b * 4 + (c + 1))
                    v.tensor_tensor(tile_of(h_sb, c, S), r, r, ALU.mult).then_inc(s_q5, 1)
                add_y(5, b)

            with dve.Fori(0, B - 1) as b:
                squares(b, b + 1)
            squares(B - 1, 0)
            attention_layer(6, dst=tile_of(xn7, 0, S))

            def c7_(i):
                return c7[:, i * T * 8:(i + 1) * T * 8]

            def per_tile(i):
                return c7_(i).rearrange("p (w n) -> p w n", w=T)

            def calibrate(dst, fl):
                idx, low, dif, t = c7_(4), c7_(5), c7_(6), c7_(7)
                v.tensor_scalar(idx, fl, 1.0, None, ALU.is_ge)
                for k in range(2, KNOTS - 1):
                    dve.drain()
                    v.scalar_tensor_tensor(idx, fl, float(k), idx, ALU.is_ge, ALU.add)
                dve.drain()
                v.tensor_tensor(t, fl, idx, ALU.subtract)
                v.tensor_scalar(low, idx, 0.0, knots[:, 0:1], ALU.is_equal, ALU.mult)
                v.tensor_scalar(dif, idx, 0.0, dknots[:, 0:1], ALU.is_equal, ALU.mult)
                for k in range(1, KNOTS - 1):
                    u = 8 + 2 * (k % 2)
                    v.tensor_scalar(c7_(u), idx, float(k), knots[:, k:k + 1], ALU.is_equal, ALU.mult)
                    v.tensor_scalar(c7_(u + 1), idx, float(k), dknots[:, k:k + 1], ALU.is_equal, ALU.mult)
                    dve.drain()
                    v.tensor_tensor(low, low, c7_(u), ALU.add)
                    v.tensor_tensor(dif, dif, c7_(u + 1), ALU.add)
                dve.drain()
                v.tensor_tensor(t, t, dif, ALU.mult)
                dve.drain()
                v.tensor_tensor(dst, t, low, ALU.add)
                dve.drain()

            n_sc = CL + NT

            def scaled(b):
                dve.wait_ge(s_sc, b + 1)
                v.tensor_scalar(tile_of(sc7, b, W * n_sc), s_ps[b % 2][:, 0:W * n_sc], temp[:, 1:2], 88.0, ALU.mult, ALU.min).then_inc(s_sg, 1)

            def sigmoid(b):
                s = tile_of(sc7, b, W * n_sc)
                dve.wait_ge(s_ex, b + 1)
                v.tensor_scalar(s, s, 1.0, None, ALU.add)
                dve.drain()
                v.reciprocal(s, s)
                dve.drain()
                v.tensor_scalar(s, s, float(KNOTS - 1), None, ALU.mult)

            for b in range(B):
                scaled(b)
                if b < B - 1:
                    norm(29 + b, b + 1, dst=tile_of(xn7, b + 1, S))
                sigmoid(b)
            dve.drain()
            sc = sc7[:, :].rearrange("p (w n) -> p w n", w=T)
            v.tensor_copy(per_tile(0), sc[:, :, 0:CL])
            dve.drain()
            calibrate(c7_(1), c7_(0))
            first_largest(per_tile(2), per_tile(1), CL)
            sel = sel7[:, :].rearrange("p (w t c) -> p w t c", w=T, t=TPC)
            for t in range(TPC):
                v.tensor_tensor(sel[:, :, t], sc[:, :, CL:].rearrange("p w (c t) -> p w t c", t=TPC)[:, :, t], per_tile(2), ALU.mult)
            dve.drain()
            v.tensor_reduce(c7_(0), sel7[:, :].rearrange("p (n c) -> p n c", c=CL), AX_X, ALU.add)
            dve.drain()
            calibrate(c7_(1), c7_(0))
            first_largest(per_tile(3), per_tile(1), TPC)
            for b in range(B):
                for w in range(b * W, (b + 1) * W):
                    i = v.tensor_tensor(one7[:, w * NT:(w + 1) * NT].rearrange("p (c t) -> p c t", t=TPC),
                                        per_tile(2)[:, w].unsqueeze(2).to_broadcast([P, CL, TPC]),
                                        per_tile(3)[:, w].unsqueeze(1).to_broadcast([P, CL, TPC]), ALU.mult)
                i.then_inc(s_oh, 1)
            dve.wait_ge(s_cp7, B)
            v.tensor_tensor(comp7[:, :].rearrange("p (w i) -> p w i", w=T), bank[1][:, 0:2 * T].rearrange("p (w i) -> p w i", w=T),
                            cb2[:, :].unsqueeze(1).to_broadcast([P, T, 2]), ALU.add).then_inc(s_cb7, 1)
            dve.wait_ge(s_th7, 1)
            par = par7[:, :].rearrange("p (w n) -> p w n", w=T)
            co = comp7[:, :].rearrange("p (w i) -> p w i", w=T)

            def half(buf, hf, n):
                return buf[:, hf * (T // 2) * n:(hf + 1) * (T // 2) * n].rearrange("p (w n) -> p w n", n=n)

            for hf in range(2):
                ws = slice(hf * T // 2, (hf + 1) * T // 2)
                wide = [P, T // 2, GRID]
                g, g2 = half(g7, hf, GRID), half(g7b, hf, GRID)
                dve.wait_ge(s_par, 4 * hf + 4)
                v.tensor_tensor(g, par[:, ws, 0:GRID], co[:, ws, 0:1].to_broadcast(wide), ALU.mult)
                v.tensor_tensor(g2, par[:, ws, GRID:2 * GRID], co[:, ws, 1:2].to_broadcast(wide), ALU.mult)
                dve.drain()
                v.tensor_tensor(g, g, g2, ALU.add)
                dve.drain()
                v.tensor_tensor(g, g, par[:, ws, 2 * GRID:3 * GRID], ALU.add)
                dve.drain()
                v.scalar_tensor_tensor(g, g, 0.0, par[:, ws, 3 * GRID:4 * GRID], ALU.max, ALU.mult)
                dve.drain()
                m = mag7[:, ws]
                v.tensor_reduce(m, g, AX_X, ALU.add)
                dve.drain()
                v.tensor_tensor(m, m, par[:, ws, 4 * GRID], ALU.add)
                dve.drain()
                v.tensor_scalar(m, m, oscale[:, 0:1], None, ALU.mult)
                dve.drain()
                for w in range(hf * T // 2, (hf + 1) * T // 2):
                    i = v.scalar_tensor_tensor(tile_of(y7, w), table_bank(w)[:, (w % 2) * TAB + TAB - D:(w % 2 + 1) * TAB],
                                               mag7[:, w:w + 1], tile_of(xn7, w), ALU.mult, ALU.add)
            for b in range(B):
                y = tile_of(y7, b, S)
                dve.drain()
                bn(lambda w: tile_of(y, w))
                dve.wait_ge(s_rstd, 33 + b)
                for w in range(W):
                    v.tensor_scalar(tile_of(y, w), tile_of(y, w), mv[:, 2 * w:2 * w + 1], rstd[:, w:w + 1], ALU.subtract, ALU.mult)
                dve.drain()
                y3 = y.rearrange("p (w f) -> p w f", w=W)
                v.tensor_tensor(y3, y3, gamma[:, :].unsqueeze(1).to_broadcast([P, W, D]), ALU.mult)
                dve.drain()
                dve.wait_ge(s_xb, b + 1)
                v.tensor_tensor(y, y, tile_of(xb7, b, S), ALU.add).then_inc(s_o7, 1)

        @block.scalar
        def _(act):
            a = nc.scalar

            def copy_xT(n, dst=None):
                act.wait_ge(s_xT, n + 1)
                a.copy(xnT[:, :] if dst is None else dst, xT_ps[:, :]).then_inc(s_xnT, 1)

            def all_of(b):
                return tile_of(xnT_all, b, S)

            def w_exp(b):
                act.wait_ge(s_sub0, b + 1)
                p = tile_of(p0, b % 2, 256)
                a.activation(p, p, ACT.Exp, scale=DH0 ** -0.5).then_inc(s_exp0, 1)

            def w_copy(b):
                act.wait_ge(s_pP0, b + 1)
                a.copy(tile_of(pT0, b % 2, 512), e_ps[b % 2][0:64, :]).then_inc(s_pT0, 1)

            copy_xT(0, all_of(0))
            copy_xT(1, all_of(1))
            w_exp(0)
            copy_xT(2, all_of(2))
            w_exp(1)
            w_copy(0)
            copy_xT(3, all_of(3))
            w_exp(2)
            w_copy(1)
            w_exp(3)
            w_copy(2)
            copy_xT(4, all_of(0))
            w_copy(3)
            copy_xT(5, all_of(1))
            copy_xT(6, all_of(2))
            copy_xT(7, all_of(3))

            def attention(l, b, more, dst=None):
                n = b + 4 * l
                k = att_before[l]
                nb = b + 1

                copy(l, b, 0)
                exp(l, b, 2)
                copy(l, b, 1)
                copy_xT(n + 1, dst)
                exp(l, b, 3)
                copy(l, b, 2)
                if more:
                    exp(l, nb, 0)
                copy(l, b, 3)
                if more:
                    exp(l, nb, 1)
                act.wait_ge(s_oP, b + (k + 1))
                a.copy(oT[:, :], y_ps[:, :]).then_inc(s_oT, 1)

            def exp(l, b, w):
                act.wait_ge(s_sub, (b + att_before[l]) * W + (w + 1))
                e = tile_of(e_sb, w % 2, 512)
                a.activation(e, e, ACT.Exp, scale=1.0 if l == 2 else DH ** -0.5).then_inc(s_exp, 1)

            def copy(l, b, w):
                act.wait_ge(s_e, (b + att_before[l]) * W + (w + 1))
                a.copy(tile_of(eT, w % 2, 512), e_ps[w % 2][:, :]).then_inc(s_eT, 1)

            def attention_layer(l, dst=None):
                exp(l, 0, 0)
                exp(l, 0, 1)
                with act.Fori(0, B - 1) as b:
                    attention(l, b, True)
                attention(l, B - 1, False, dst)

            def prepare(l, stage):
                i_l = AL.index(l)
                if stage == 0:
                    if l == 2:
                        act.wait_ge(s_ca, loads["s_ca"])
                    act.wait_ge(s_k, i_l + 1)
                    if l == 4:
                        a.activation(kT[:, :], bank[0][:, 0:P], ACT.Identity, bias=bk[:, 0:1]).then_inc(s_kT, 1)
                    else:
                        a.copy(kT[:, :], bank[0][:, 0:P]).then_inc(s_kT, 1)
                elif stage <= B:
                    b = stage - 1
                    act.wait_ge(s_a, 4 * i_l + b + 1)
                    a.copy(aB[l][:, b * 512:(b + 1) * 512], bank[b % 2][:, :]).then_inc(s_aB, 1)
                else:
                    b = stage - 1 - B
                    act.wait_ge(s_c, b + 1)
                    a.copy(cf[:, b * 512:(b + 1) * 512], bank[b % 2][0:1, :]).then_inc(s_cf, 1)

            def moe(l):
                E, C = MOE[l]
                tb, R = tile_before[l], RING[l]

                def rows(s, u, early):
                    act.wait_ge(s_xt, s + (tb + 1))
                    if not early or tb:
                        act.wait_ge(s_hh, s + (tb - 1))
                    a.copy(tile_of(xsT, u % 2), bank[4 + u % 2][:, 0:P]).then_inc(s_xc, 1)

                def relu(s, u, early):
                    act.wait_ge(s_hh, s + (tb + 1))
                    if not early or tb:
                        act.wait_ge(s_my, s + (tb - 1))
                    for c in range(C):
                        i = a.activation(hT[:, (u % 2) * 512 + c * P:(u % 2) * 512 + (c + 1) * P], bank[2 + u % 2][:, c * P:(c + 1) * P],
                                         ACT.Relu, bias=b1s[:, (u % R) * C + c:(u % R) * C + c + 1])
                    i.then_inc(s_hr, 1)

                def body(i, peeled):
                    for u in range(BODY):
                        s = i * BODY + u
                        rows(s, u, peeled and u < 2)
                        if not peeled or u >= 1:
                            relu(s - 1, (u - 1) % BODY, peeled and u < 3)

                body(0, True)
                with act.Fori(1, SLOT_TILES[l] // BODY) as i:
                    body(i, False)
                relu(SLOT_TILES[l] - 1, BODY - 1, False)
                copy_xT(4 * l + 4)

            act.wait_ge(s_cm, loads["s_cm"])
            for stage in range(5):
                prepare(2, stage)
            moe(1)
            attention_layer(2, all_of(0))
            for b in range(1, B):
                copy_xT(12 + b, all_of(b))
            act.wait_ge(s_gsub, 1)
            a.activation(gv[:, :], gv[:, :], ACT.Exp).then_inc(s_gexp, 1)
            for stage in range(9):
                prepare(4, stage)
            for stage in range(5):
                prepare(6, stage)
            moe(3)
            attention_layer(4)
            with act.Fori(0, B) as b:
                for c in range(4):
                    act.wait_ge(s_h5, b * 4 + (c + 1))
                    if c >= 2:
                        act.wait_ge(s_q5, b * 4 + (c - 1))
                    a.activation(tile_of(r5, c % 2, S), bank[2 + c][:, :], ACT.Relu).then_inc(s_r5, 1)
                copy_xT(b + 21)
            attention_layer(6)
            act.wait_ge(s_c7, loads["s_c7"])
            for b in range(B):
                act.wait_ge(s_sg, b + 1)
                e = tile_of(sc7, b, W * (CL + NT))
                a.activation(e, e, ACT.Exp).then_inc(s_ex, 1)
                if b < B - 1:
                    copy_xT(29 + b)
            for b in range(B):
                act.wait_ge(s_hc7, b + 1)
                if b >= 2:
                    act.wait_ge(s_cp7, b - 1)
                a.activation(tile_of(h7, b % 2, S), bank[4 + b][0:COMP, :], ACT.Gelu, bias=cb1[:, 0:1]).then_inc(s_hg7, 1)
            act.wait_ge(s_cb7, 1)
            a.activation(comp7[:, :], comp7[:, :], ACT.Tanh).then_inc(s_th7, 1)
            for b in range(B):
                act.wait_ge(s_ohP, b + 1)
                a.copy(tile_of(oneT7, b % 2, S), one_bank(b)[0:NT, :]).then_inc(s_ohT, 1)
                for w in range(2 * b, 2 * b + 2):
                    act.wait_ge(s_tb, w + 1)
                    a.copy(par7[:, 2 * w * (TAB - D):(2 * w + 2) * (TAB - D)].rearrange("p (w n) -> p w n", w=2),
                           table_bank(2 * w)[:, 0:2 * TAB].rearrange("p (w n) -> p w n", w=2)[:, :, 0:TAB - D]).then_inc(s_par, 1)

        @block.tensor
        def _(pe):
            mm = nc.tensor.matmul

            pe.wait_ge(s_c0, loads["s_c0"])
            pe.wait_ge(s_hc, 1)
            for c in range(4):
                i = mm(tile_of(bank[0], c), tile_of(wk0, c), hcT[:, :], start=True, stop=True)
            i.then_inc(s_pp, 1)
            for c in range(4):
                i = mm(tile_of(bank[1], c), tile_of(wv0, c), hcT[:, :], start=True, stop=True)
            i.then_inc(s_pp, 1)
            pe.wait_ge(s_pv, 1)
            for g in range(2):
                r = 64 * g
                for c in range(4):
                    i = mm(tile_of(bank[2 + g], c), wq0T[r:r + 64, c * P:(c + 1) * P], kT0[r:r + 64, c * P:(c + 1) * P],
                           start=True, stop=True)
                i.then_inc(s_pp, 1)
            pe.wait_ge(s_pv, 2)
            vz = vZ[:, :].rearrange("p (c t m) -> p c t m", c=4, t=B * W)
            for t in range(B * W):
                for c in range(4):
                    i = mm(tile_of(bank[4 + t // 4], t % 4)[0:64], vz[:, c, t, :], tile_of(wo0, c), start=(c == 0), stop=(c == 3))
                if t % 4 == 3:
                    i.then_inc(s_pp, 1)
            def transposes(n, src=None):
                pe.wait_ge(s_xn, n + 1)
                if not (isinstance(n, int) and n == 0):
                    pe.wait_ge(s_xnT, n)
                for w in range(W):
                    i = nc.tensor.transpose(tile_of(xT_ps, w), tile_of(xn if src is None else src, w), ident[:, :])
                i.then_inc(s_xT, 1)

            def bias_then(layer):
                if layer in bo_row:
                    mm(y_ps[:, :], onerow[0:1, :], bo_row[layer][0:1, :], start=True, stop=False, skip_group_check=True)

            def y_matmul(layer, w, lhsT, rhs, first=True, last=True):
                biased = layer in bo_row
                return mm(tile_of(y_ps, w), lhsT, rhs, start=(first and not biased), stop=last, skip_group_check=biased)

            def w_scores(b):
                pe.wait_ge(s_xnT, b + 1)
                for w in range(W):
                    i = mm(s_ps[b % 2][:, w * 64:(w + 1) * 64], tile_of(xnT_all, b * W + w), A0[:, (b * W + w) * 64:(b * W + w + 1) * 64], start=True, stop=True)
                i.then_inc(s_s0, 1)

            def w_turn(b):
                pe.wait_ge(s_p0, b + 1)
                for w in range(W):
                    i = nc.tensor.transpose(e_ps[b % 2][0:64, w * P:(w + 1) * P], p0[:, (b % 2) * 256 + w * 64:(b % 2) * 256 + (w + 1) * 64], ident[:, :])
                i.then_inc(s_pP0, 1)

            def w_out(b):
                pe.wait_ge(s_res, b + 1)
                bias_then(0)
                pe.wait_ge(s_pT0, b + 1)
                for w in range(W):
                    i = y_matmul(0, w, pT0[:, (b % 2) * 512 + w * P:(b % 2) * 512 + (w + 1) * P], VW0[0:64, (b * W + w) * P:(b * W + w + 1) * P])
                i.then_inc(s_y, 1)

            def logits(l, b):
                E = MOE[l][0]
                pe.wait_ge(s_xnT, 4 * l + b + 1)
                for t in range(b * W, (b + 1) * W):
                    i = mm(bank[1][:, t * E:(t + 1) * E], tile_of(xnT_all, t), gw[l][:, :], start=True, stop=True)
                i.then_inc(s_g, 1)

            pe.wait_ge(s_pv, 8)
            transposes(0)
            transposes(1)
            w_scores(0)
            transposes(2)
            w_scores(1)
            w_turn(0)
            transposes(3)
            w_scores(2)
            w_turn(1)
            w_out(0)
            w_scores(3)
            w_turn(2)
            w_out(1)
            transposes(4, tile_of(xn_all, 0, S))
            w_turn(3)
            w_out(2)
            transposes(5, tile_of(xn_all, 1, S))
            pe.wait_ge(s_cm, loads["s_cm"])
            logits(1, 0)
            w_out(3)
            transposes(6, tile_of(xn_all, 2, S))
            logits(1, 1)
            transposes(7, tile_of(xn_all, 3, S))
            logits(1, 2)
            logits(1, 3)

            def scores(l, b, w):
                split = l == 4
                i = mm(s_ps[w % 2][:, :], tile_of(xnT, w), aB[l][:, bass.ds(b * 512, 512)], start=True, stop=not split)
                if split:
                    mm(s_ps[w % 2][:, :], oner[0:1, :], chi[0:1, bass.ds(b * 512, 512)], start=False, stop=False)
                    i = mm(s_ps[w % 2][:, :], oner[0:1, :], clo[0:1, bass.ds(b * 512, 512)], start=False, stop=True)
                i.then_inc(s_s, 1)

            def attention(l, b, more, src=None):
                n = b + 4 * l
                k = att_before[l]

                def e(w):
                    t = (b + k) * W + w
                    pe.wait_ge(s_exp, t + 1)
                    for c in range(4):
                        i = nc.tensor.transpose(tile_of(e_ps[w % 2], c), e_sb[:, (w % 2) * 512 + c * P:(w % 2) * 512 + (c + 1) * P], ident[:, :])
                    i.then_inc(s_e, 1)

                def o(w):
                    t = (b + k) * W + w
                    pe.wait_ge(s_eT, t + 1)
                    if w >= 2:
                        pe.wait_ge(s_on, t - 1)
                    for c in range(4):
                        i = mm(o_ps[w % 2][:, c * VC:(c + 1) * VC],
                               eT[:, (w % 2) * 512 + c * P:(w % 2) * 512 + (c + 1) * P],
                               vB[l][:, bass.ds((b * 4 + c) * VC, VC)], start=True, stop=True)
                    i.then_inc(s_o, 1)

                e(0)
                scores(l, b, 2)
                e(1)
                o(0)
                scores(l, b, 3)
                o(1)
                transposes(n + 1, src)
                e(2)
                o(2)
                e(3)
                if more:
                    pe.wait_ge(s_xnT, n + 2)
                    scores(l, b + 1, 0)
                o(3)
                if more:
                    scores(l, b + 1, 1)
                pe.wait_ge(s_on, (b + k + 1) * W)
                pe.wait_ge(s_res, b + (res_before[l] + 1))
                for w in range(W):
                    i = nc.tensor.transpose(tile_of(y_ps, w), tile_of(on, w), ident[:, :])
                i.then_inc(s_oP, 1)
                pe.wait_ge(s_oT, b + (k + 1))
                bias_then(l)
                for w in range(W):
                    i = y_matmul(l, w, tile_of(oT, w), wo[l][:, :])
                i.then_inc(s_y, 1)

            def attention_layer(l, src=None):
                i_l = AL.index(l)
                pe.wait_ge(s_aB, 4 * i_l + 4)
                if l == 4:
                    pe.wait_ge(s_cr, 1)
                pe.wait_ge(s_xnT, 4 * l + 1)
                scores(l, 0, 0)
                scores(l, 0, 1)
                with pe.Fori(0, B - 1) as b:
                    attention(l, b, True)
                attention(l, B - 1, False, src)

            def prepare(l, stage):
                i_l = AL.index(l)
                if stage == 0:
                    if l == 2:
                        pe.wait_ge(s_ca, loads["s_ca"])
                    mm(bank[0][:, 0:P], wk[l][:, :], ctxT[:, :], start=True, stop=True).then_inc(s_k, 1)
                    for b in range(B):
                        i = mm(tile_of(bank[1], b), tile_of(ctxR, b), wv[l][:, :], start=True, stop=(l != 4), skip_group_check=(l == 4))
                        if l == 4:
                            i = mm(tile_of(bank[1], b), onerow[0:1, :], bv_row[0:1, :], start=False, stop=True, skip_group_check=True)
                    i.then_inc(s_v, 1)
                elif stage <= B:
                    b = stage - 1
                    pe.wait_ge(s_kB, 4 * i_l + b + 1)
                    if b == 1:
                        pe.wait_ge(s_vB, i_l + 1)
                    elif b > 1:
                        pe.wait_ge(s_aB, 4 * i_l + b - 1)
                    mm(bank[b % 2][:, :], wq[l][:, :], kB[:, b * 512:(b + 1) * 512], start=True, stop=True).then_inc(s_a, 1)
                else:
                    b = stage - 1 - B
                    if b < 2:
                        pe.wait_ge(s_aB, 4 * i_l + 3 + b)
                    else:
                        pe.wait_ge(s_cf, b - 1)
                    mm(bank[b % 2][0:1, :], bq[:, 0:1], kB[:, b * 512:(b + 1) * 512], start=True, stop=True).then_inc(s_c, 1)

            def prepare5(stage):
                if stage < 2:
                    if stage == 0:
                        pe.wait_ge(s_c5, loads["s_c5"])
                        pe.wait_ge(s_aB, 4)
                    pe.wait_ge(s_pv, 9 + stage)
                    for c in range(4):
                        i = nc.tensor.transpose(tile_of(bank[stage], c), tile_of(ab, c), ident[:, :])
                    i.then_inc(s_pp, 1)
                    if stage == 1:
                        mm(bank[0][0:16, 0:P], fbT[:, :], v5[:, :], start=True, stop=True).then_inc(s_pp, 1)
                else:
                    pe.wait_ge(s_pv, 12)
                    mm(bank[1][:, :], t1[:, :], u5T[:, :], start=True, stop=True).then_inc(s_pp, 1)

            def ranks(l):
                E = MOE[l][0]
                pe.wait_ge(s_sel, 1 if l == 1 else 2)
                mm(bank[2][:, 0:(T + 1) * E], tri[:, :], gsel[:, 0:(T + 1) * E], start=True, stop=False, skip_group_check=True)
                for t in range(T):
                    i = mm(bank[2][:, (t + 1) * E:(T + 1) * E].rearrange("p (n e) -> p n e", e=E), ones[:, :],
                           gsel[:, t * E:(t + 1) * E].unsqueeze(1).to_broadcast([P, T - t, E]), start=False, stop=(t == T - 1), skip_group_check=True)
                i.then_inc(s_rank, 1)

            def moe(l):
                E, C = MOE[l]
                tb, R = tile_before[l], RING[l]
                n = C * P

                def turn(i, s, u, early):
                    if u % GT == 0:
                        pe.wait_ge(s_xs[u // GT], i * 16 + (16 * (tb // BODY) + 16))
                    if not early or tb:
                        pe.wait_ge(s_xc, s + (tb - 1))
                    nc.tensor.transpose(bank[4 + u % 2][:, 0:P], tile_of(xs, u), ident[:, :]).then_inc(s_xt, 1)

                def hidden(s, u, early):
                    pe.wait_ge(s_wc, s + (tb + 1))
                    pe.wait_ge(s_xc, s + (tb + 1))
                    if not early or tb:
                        pe.wait_ge(s_hr, s + (tb - 1))
                    for c in range(C):
                        h = mm(tile_of(bank[2 + u % 2], c), w1s[:, (u % R) * n + c * P:(u % R) * n + (c + 1) * P], tile_of(xsT, u % 2), start=True, stop=True)
                    h.then_inc(s_hh, 1)

                def second(s, u, early):
                    pe.wait_ge(s_wd, s + (tb + 1))
                    pe.wait_ge(s_hr, s + (tb + 1))
                    if not early or tb:
                        pe.wait_ge(s_yb, s + (tb - 1))
                    for c in range(C):
                        y = mm(bank[6 + u % 2][:, 0:P], hT[:, (u % 2) * 512 + c * P:(u % 2) * 512 + (c + 1) * P],
                               w2s[:, (u % R) * n + c * P:(u % R) * n + (c + 1) * P], start=(c == 0), stop=(c == C - 1))
                    y.then_inc(s_my, 1)

                def body(i, peeled):
                    for u in range(BODY):
                        s = i * BODY + u
                        turn(i, s, u, peeled and u < 2)
                        if not peeled or u >= 1:
                            hidden(s - 1, (u - 1) % BODY, peeled and u < 3)
                        if not peeled or u >= 2:
                            second(s - 2, (u - 2) % BODY, peeled and u < 4)

                last = SLOT_TILES[l] - 1
                body(0, True)
                with pe.Fori(1, SLOT_TILES[l] // BODY) as i:
                    body(i, False)
                hidden(last, BODY - 1, False)
                second(last - 1, BODY - 2, False)
                second(last, BODY - 1, False)
                transposes(4 * l + 4)

            ranks(1)
            for stage in range(5):
                prepare(2, stage)
            for stage in range(3):
                prepare5(stage)
            moe(1)
            attention_layer(2, tile_of(xn_all, 0, S))
            for b in range(1, B):
                logits(3, b - 1)
                transposes(12 + b, tile_of(xn_all, b, S))
            logits(3, 3)
            ranks(3)
            for stage in range(9):
                prepare(4, stage)
            pe.wait_ge(s_cf, 4)
            for stage in range(5):
                prepare(6, stage)
            moe(3)
            attention_layer(4)

            with pe.Fori(0, B) as b:
                pe.wait_ge(s_xnT, b + 21)
                for c in range(4):
                    mm(bank[2 + c][:, :], tile_of(wfcT, c), xnT[:, :], start=True, stop=True).then_inc(s_h5, 1)
                transposes(b + 21)
                pe.wait_ge(s_res, b + (res_before[5] + 1))
                pe.wait_ge(s_q5, b * 4 + 4)
                for w in range(W):
                    for c in range(4):
                        i = mm(tile_of(y_ps, w), h_sb[:, c * S + w * P:c * S + (w + 1) * P], tile_of(wpjT, c), start=(c == 0), stop=(c == 3))
                i.then_inc(s_y, 1)

            attention_layer(6, tile_of(xn7, 0, S))

            pe.wait_ge(s_c7, loads["s_c7"])
            n = CL + NT
            for b in range(B):
                pe.wait_ge(s_xnT, b + 29)
                if b >= 2:
                    pe.wait_ge(s_sg, b - 1)
                for w in range(W):
                    i = mm(s_ps[b % 2][:, w * n:(w + 1) * n], tile_of(xnT, w), rhs7[:, :], start=True, stop=True)
                i.then_inc(s_sc, 1)
                if b == B - 1:
                    pe.wait_ge(s_res, 21)
                mm(bank[4 + b][0:COMP, :], cw1[:, :], xnT[:, :], start=True, stop=True).then_inc(s_hc7, 1)
                if b < B - 1:
                    transposes(29 + b, tile_of(xn7, b + 1, S))
            for b in range(B):
                pe.wait_ge(s_hg7, b + 1)
                for w in range(W):
                    t = b * W + w
                    i = mm(bank[1][:, 2 * t:2 * t + 2], h7[:, (b % 2) * S + w * P:(b % 2) * S + (w + 1) * P], cw2[:, :], start=True, stop=True)
                i.then_inc(s_cp7, 1)
            for b in range(B):
                pe.wait_ge(s_oh, b + 1)
                if b == 1:
                    pe.wait_ge(s_cb7, 1)
                for w in range(W):
                    t = b * W + w
                    i = nc.tensor.transpose(one_bank(b)[0:NT, w * P:(w + 1) * P], one7[:, t * NT:(t + 1) * NT], ident[:, :])
                i.then_inc(s_ohP, 1)
            for b in range(B):
                pe.wait_ge(s_ohT, b + 1)
                for w in range(W):
                    t = b * W + w
                    i = mm(table_bank(t)[:, (t % 2) * TAB:(t % 2 + 1) * TAB], oneT7[:, (b % 2) * S + w * P:(b % 2) * S + (w + 1) * P], table[:, :], start=True, stop=True)
                    if w % 2:
                        i.then_inc(s_tb, 1)


def constants(np):
    f = np.float32
    rows = np.arange(P)
    pos = np.arange(SK, dtype=f)[:, None]
    denom = np.power(f(10000.0), f(2.0) * np.arange(D // 2, dtype=f) / f(D))
    ang = pos / denom
    pe = np.zeros((SK, D), f)
    pe[:, 0::2] = np.sin(ang)
    pe[:, 1::2] = np.cos(ang)
    q, k = np.arange(P)[:, None], np.arange(SK)[None, :]
    e = np.arange(16)
    return {
        "tri": (rows[:, None] <= rows[None, :]).astype(f),
        "before": np.tile((e[None, :] < e[:, None]).astype(f).reshape(1, 256), (P, 1)),
        "full": np.tile(np.arange(16, dtype=f) * P, (P, 1)),
        "number": np.arange(64, dtype=f)[None],
        "ident": np.eye(P, dtype=f),
        "peT": np.ascontiguousarray(pe.T),
        "mask16": (rows[:, None] // DH == np.arange(H)[None, :]).astype(f),
        "mask4": (rows[:, None] // SK == np.arange(HC)[None, :]).astype(f),
        "desc": np.tile(np.arange(16, 0, -1).astype(f), (P, 1)),
        "cap4": np.where(k > q, f(-BIG), f(BIG)).astype(f),
    }


def kernel(**inputs):
    import numpy as np
    import concourse.bacc as bacc
    from concourse.bass_utils import run_bass_kernel_spmd

    I = {k: np.asarray(v) for k, v in inputs.items()}

    def lay(a):
        return np.ascontiguousarray(a)

    def by_chunk(w):
        return lay(w.reshape(-1, P, w.shape[1]).transpose(1, 0, 2).reshape(P, -1))

    A = constants(np)
    for name in ("x", "L0_xattn_Wk", "L0_xattn_Wv", "L0_ffn_gate_b", "L0_ffn_expert_bias", "L0_ffn_b2", "L1_ffn_b2",
                 "L1_ffn_gate", "L2_ffn_w_fc", "L2_ffn_w_proj", "L2_ffn_v", "L3_ffn_compress_w1", "L3_ffn_compress_w2",
                 "L3_ffn_compress_b2", "L3_ffn_knot_values", "L3_ffn_temperature", "L3_ffn_output_scale",
                 "L3_ffn_norm_gamma", "L3_ffn_norm_beta"):
        A[name] = lay(I[name])
    A["ctxT"] = lay(I["ctx_1024"].reshape(B * SK, D).T)
    A["wq0T"] = by_chunk(I["L0_xattn_Wq"].T)
    A["wo0"] = by_chunk(I["L0_xattn_Wo"])
    A["bo0"] = lay(np.tile(I["L0_xattn_bo"], W)[None])
    for l, name, flip in ((2, "L1", False), (4, "L2", True), (6, "L3", True)):
        for w in "qkvo":
            a = I[f"{name}_xattn_W{w}"]
            A[f"w{w}{l}"] = lay(a.T if flip != (w == "q") else a)
    A["bq"] = lay(I["L2_xattn_bq"][:, None])
    A["bk"] = lay(I["L2_xattn_bk"][:, None])
    A["bv"] = lay(I["L2_xattn_bv"][None])
    A["bo4"] = lay(np.tile(I["L2_xattn_bo"], W)[None])
    A["mask"] = lay(I["mask_Bx1xSxS2_bk1"]).reshape(B * S, SK)
    A["gw1"] = lay(I["L0_ffn_gate_w"].T)
    for l, name in ((1, "L0_ffn_"), (3, "L1_ffn_")):
        E, C = MOE[l]
        u = "w" if l == 1 else "W"
        A[f"b1_{l}"] = lay(I[name + "b1"].reshape(E, C, P).transpose(2, 0, 1).reshape(P, E * C))
        A[f"w1_{l}"] = lay(I[name + u + "1"])
        A[f"w2_{l}"] = lay(I[name + u + "2"].reshape(E, C, P, D).transpose(0, 2, 1, 3).reshape(E, P, C * D))
    A["fbT"] = lay(I["L2_ffn_fast_b"].T)
    A["uT"] = lay(I["L2_ffn_u"].T)
    A["gate5"] = lay(I["L2_ffn_gate"].reshape(1))
    A["rawT"] = lay(I["L3_ffn_signatures_raw"].T)
    A["cb1"] = lay(I["L3_ffn_compress_b1"][:, None])
    A["table"] = lay(np.concatenate([I["L3_ffn_spline_w1"].reshape(NT, 2 * GRID), I["L3_ffn_spline_b1"],
                                     I["L3_ffn_spline_w2"].reshape(NT, GRID), I["L3_ffn_spline_b2"],
                                     I["L3_ffn_directions"]], axis=1))

    nc = bacc.Bacc("TRN2", target_bir_lowering=False, num_devices=1)
    handles = {k: nc.dram_tensor(f"in_{k}", a.shape, mybir.dt.from_np(a.dtype), kind="ExternalInput").ap() for k, a in A.items()}
    out = nc.dram_tensor("out_0", (B, S, D), F32, kind="ExternalOutput").ap()
    build(nc, handles, out)
    r = run_bass_kernel_spmd(nc, [{f"in_{k}": a for k, a in A.items()}], core_ids=[0])
    return r.results[0]["out_0"]
```
